# Optimizing a Trainium2 kernel written in Bass

```python
import numpy as np
import jax
import jax.numpy as jnp

def _softmax(x, axis=-1):
    return jax.nn.softmax(x, axis=axis)

def _gelu(x):
    return jax.nn.gelu(x, approximate=True)

def _silu(x):
    return jax.nn.silu(x)

def _sigmoid(x):
    return jax.nn.sigmoid(x)

def _layernorm(x, axis=-1, eps=1e-05):
    m = jnp.mean(x, axis=axis, keepdims=True)
    v = jnp.var(x, axis=axis, keepdims=True)
    return (x - m) / jnp.sqrt(v + eps)

def _scatter_add(tgt, idx, src, axis=0):
    return tgt.at[idx].add(src)

def _segment_sum(src, seg, n):
    return jax.ops.segment_sum(src, seg, n)
kernel_name = 'mk_prb_d2_jaxref_r8_5a176e'

def setup_inputs(seed: int=0):
    np.random.seed(seed)
    _w = jnp.asarray

    def _L0_attn_setup():
        import jax, jax.numpy as jnp
        import numpy as np
        D_MODEL = 128
        D_STATE = 16
        D_CONV = 4
        EXPAND = 2
        D_INNER = EXPAND * D_MODEL
        DT_RANK = (D_MODEL + 15) // 16
        BATCH = 2
        SEQ = 256
        EPS = 1e-05

        def _mamba_params(key, scale=0.02):
            ks = jax.random.split(key, 8)
            n = lambda k, s: jax.random.normal(k, s, jnp.float32) * scale
            return {'Win': n(ks[0], (2 * D_INNER, D_MODEL)), 'convw': n(ks[1], (D_INNER, 1, D_CONV)), 'convb': n(ks[2], (D_INNER,)), 'Wx': n(ks[3], (DT_RANK + 2 * D_STATE, D_INNER)), 'Wdt': n(ks[4], (D_INNER, DT_RANK)), 'bdt': n(ks[5], (D_INNER,)), 'Alog': jnp.log(jnp.tile(jnp.arange(1, D_STATE + 1, dtype=jnp.float32), (D_INNER, 1))), 'D': jnp.ones((D_INNER,), jnp.float32), 'Wout': n(ks[6], (D_MODEL, D_INNER))}

        def _mamba(x, Win, convw, convb, Wx, Wdt, bdt, Alog, Dp, Wout):
            B, L, _ = x.shape
            xz = jnp.einsum('bld,ed->ble', x, Win)
            u, z = jnp.split(xz, 2, axis=-1)
            uc = jnp.transpose(u, (0, 2, 1))
            uc = jnp.pad(uc, ((0, 0), (0, 0), (D_CONV - 1, 0)))
            uc = jax.lax.conv_general_dilated(uc, convw, (1,), 'VALID', feature_group_count=D_INNER)
            uc = uc + convb[None, :, None]
            u = jax.nn.silu(jnp.transpose(uc, (0, 2, 1)))
            xdbl = jnp.einsum('bld,ed->ble', u, Wx)
            dtr, Bm, Cm = jnp.split(xdbl, [DT_RANK, DT_RANK + D_STATE], axis=-1)
            dt = jax.nn.softplus(jnp.einsum('blr,dr->bld', dtr, Wdt) + bdt)
            A = -jnp.exp(Alog)

            def step(h, ins):
                dt_t, u_t, B_t, C_t = ins
                h = jnp.exp(dt_t[..., None] * A) * h + (dt_t * u_t)[..., None] * B_t[:, None, :]
                y_t = jnp.einsum('bdn,bn->bd', h, C_t)
                return (h, y_t)
            h0 = jnp.zeros((B, D_INNER, D_STATE), jnp.float32)
            xs = (jnp.moveaxis(dt, 1, 0), jnp.moveaxis(u, 1, 0), jnp.moveaxis(Bm, 1, 0), jnp.moveaxis(Cm, 1, 0))
            _, ys = jax.lax.scan(step, h0, xs)
            y = jnp.moveaxis(ys, 0, 1) + u * Dp
            y = y * jax.nn.silu(z)
            return jnp.einsum('bld,ed->ble', y, Wout)
        key = jax.random.key(seed)
        kx, kf, kb = jax.random.split(key, 3)
        inp = {'x': jax.random.normal(kx, (BATCH, SEQ, D_MODEL), jnp.float32), 'norm_g': jnp.ones((D_MODEL,), jnp.float32), 'norm_b': jnp.zeros((D_MODEL,), jnp.float32)}
        for pfx, k in (('f', kf), ('b', kb)):
            for name, v in _mamba_params(k).items():
                inp[f'{pfx}_{name}'] = v
        return inp
    _L0_attn_in = _L0_attn_setup()

    def _L0_ffn_setup():
        import jax, jax.numpy as jnp
        import numpy as np
        B, S, D, F, E, TOP_K = (4, 256, 128, 512, 8, 2)
        LN_EPS = 1e-05
        key = jax.random.key(seed)
        ks = jax.random.split(key, 4)
        sc = lambda fan_in: 1.0 / np.sqrt(fan_in)
        return {'x': jax.random.normal(ks[0], (B, S, D), jnp.float32), 'W1': jax.random.normal(ks[1], (E, D, F), jnp.float32) * sc(D), 'b1': jnp.zeros((E, F), jnp.float32), 'W2': jax.random.normal(ks[2], (E, F, D), jnp.float32) * sc(F), 'b2': jnp.zeros((E, D), jnp.float32), 'Wr': jax.random.normal(ks[3], (D, E), jnp.float32) * sc(D), 'br': jnp.zeros((E,), jnp.float32), 'gamma': jnp.ones((D,), jnp.float32), 'beta': jnp.zeros((D,), jnp.float32)}
    _L0_ffn_in = _L0_ffn_setup()

    def _L1_attn_setup():
        import jax, jax.numpy as jnp
        import numpy as np
        D = 128
        H = 16
        KVH = 4
        HD = D // H
        LAT = 32
        WIN = 32
        B, S = (1, 256)
        BASE_G, BASE_L = (1000000.0, 10000.0)
        EPS = 1e-06

        def rmsnorm(x, w):
            return x * jax.lax.rsqrt(jnp.mean(x * x, axis=-1, keepdims=True) + EPS) * w

        def qk_norm(x):
            return x * jax.lax.rsqrt(jnp.mean(x * x, axis=-1, keepdims=True) + EPS)

        def rope(x, base):
            s, hd = (x.shape[-2], x.shape[-1])
            inv_freq = 1.0 / base ** (jnp.arange(0, hd, 2, dtype=jnp.float32) / hd)
            freqs = jnp.arange(s, dtype=jnp.float32)[:, None] * inv_freq[None, :]
            cos, sin = (jnp.cos(freqs), jnp.sin(freqs))
            xe, xo = (x[..., ::2], x[..., 1::2])
            out = jnp.stack([xe * cos - xo * sin, xe * sin + xo * cos], axis=-1)
            return out.reshape(x.shape)

        def split_heads(x, n_heads):
            b, s, _ = x.shape
            return x.reshape(b, s, n_heads, HD).transpose(0, 2, 1, 3)

        def repeat_kv(x):
            return jnp.repeat(x, H // KVH, axis=1)

        def sdpa(q, k, v, mask):
            scores = jnp.einsum('bhqd,bhkd->bhqk', q, k) / np.sqrt(HD).astype(np.float32)
            scores = jnp.where(mask, scores, jnp.float32(-1e+30))
            probs = jax.nn.softmax(scores, axis=-1)
            return jnp.einsum('bhqk,bhkd->bhqd', probs, v)

        def merge_heads(x):
            b, h, s, hd = x.shape
            return x.transpose(0, 2, 1, 3).reshape(b, s, h * hd)

        def global_latent_attn(x, wq, w_kv_down, w_k_up, w_v_up, wo):
            q = split_heads(x @ wq, H)
            latent = x @ w_kv_down
            k = split_heads(latent @ w_k_up, KVH)
            v = split_heads(latent @ w_v_up, KVH)
            q, k = (rope(q, BASE_G), rope(k, BASE_G))
            q, k = (qk_norm(q), qk_norm(k))
            k, v = (repeat_kv(k), repeat_kv(v))
            i = jnp.arange(x.shape[1])
            causal = i[:, None] >= i[None, :]
            return merge_heads(sdpa(q, k, v, causal)) @ wo

        def local_gqa_attn(x, wq, wk, wv, wo):
            q = split_heads(x @ wq, H)
            k = split_heads(x @ wk, KVH)
            v = split_heads(x @ wv, KVH)
            q, k = (rope(q, BASE_L), rope(k, BASE_L))
            q, k = (qk_norm(q), qk_norm(k))
            k, v = (repeat_kv(k), repeat_kv(v))
            i = jnp.arange(x.shape[1])
            diff = i[:, None] - i[None, :]
            mask = (diff >= 0) & (diff < WIN)
            return merge_heads(sdpa(q, k, v, mask)) @ wo
        key = jax.random.key(seed)
        ks = jax.random.split(key, 12)
        std = 0.02
        return {'hidden': jax.random.normal(ks[0], (B, S, D), dtype=jnp.float32), 'norm1_w': jnp.ones((D,), jnp.float32), 'norm2_w': jnp.ones((D,), jnp.float32), 'g_wq': jax.random.normal(ks[1], (D, H * HD), jnp.float32) * std, 'g_kv_down': jax.random.normal(ks[2], (D, LAT), jnp.float32) * std, 'g_k_up': jax.random.normal(ks[3], (LAT, KVH * HD), jnp.float32) * std, 'g_v_up': jax.random.normal(ks[4], (LAT, KVH * HD), jnp.float32) * std, 'g_wo': jax.random.normal(ks[5], (D, D), jnp.float32) * std, 'l_wq': jax.random.normal(ks[6], (D, H * HD), jnp.float32) * std, 'l_wk': jax.random.normal(ks[7], (D, KVH * HD), jnp.float32) * std, 'l_wv': jax.random.normal(ks[8], (D, KVH * HD), jnp.float32) * std, 'l_wo': jax.random.normal(ks[9], (D, D), jnp.float32) * std}
    _L1_attn_in = _L1_attn_setup()

    def _L1_ffn_setup():
        import jax, jax.numpy as jnp
        import numpy as np
        CAPACITY_FACTOR = 1.0

        def _route(token_inputs, Wg, capacity):
            dt = token_inputs.dtype
            logits = jnp.einsum('bnd,de->bne', token_inputs, Wg)
            gates = jax.nn.softmax(logits, axis=-1)
            expert_idx = jnp.argmax(gates, axis=-1)
            mask = jax.nn.one_hot(expert_idx, Wg.shape[1], dtype=dt)
            gate = jnp.sum(gates * mask, axis=-1)
            pos = jnp.cumsum(mask, axis=1) * mask - mask
            keep = mask * (pos < capacity).astype(dt)
            pos_oh = jax.nn.one_hot(pos.astype(jnp.int32), capacity, dtype=dt)
            dispatch = keep[..., None] * pos_oh
            combine = dispatch * gate[:, :, None, None]
            return (dispatch, combine)
        key = jax.random.key(seed)
        k1, k2, k3, k4 = jax.random.split(key, 4)
        B, N, D, E, H = (8, 256, 128, 8, 512)
        return {'token_inputs': jax.random.normal(k1, (B, N, D), dtype=jnp.float32), 'Wg': jax.random.normal(k2, (D, E), dtype=jnp.float32) * 0.02, 'W1': jax.random.normal(k3, (E, D, H), dtype=jnp.float32) * 0.02, 'W2': jax.random.normal(k4, (E, H, D), dtype=jnp.float32) * 0.02}
    _L1_ffn_in = _L1_ffn_setup()
    _d = {'L0_attn_x': _L0_attn_in['x'], 'L0_attn_norm_g': _L0_attn_in['norm_g'], 'L0_attn_norm_b': _L0_attn_in['norm_b'], 'L0_attn_f_Win': _L0_attn_in['f_Win'], 'L0_attn_f_convw': _L0_attn_in['f_convw'], 'L0_attn_f_convb': _L0_attn_in['f_convb'], 'L0_attn_f_Wx': _L0_attn_in['f_Wx'], 'L0_attn_f_Wdt': _L0_attn_in['f_Wdt'], 'L0_attn_f_bdt': _L0_attn_in['f_bdt'], 'L0_attn_f_Alog': _L0_attn_in['f_Alog'], 'L0_attn_f_D': _L0_attn_in['f_D'], 'L0_attn_f_Wout': _L0_attn_in['f_Wout'], 'L0_attn_b_Win': _L0_attn_in['b_Win'], 'L0_attn_b_convw': _L0_attn_in['b_convw'], 'L0_attn_b_convb': _L0_attn_in['b_convb'], 'L0_attn_b_Wx': _L0_attn_in['b_Wx'], 'L0_attn_b_Wdt': _L0_attn_in['b_Wdt'], 'L0_attn_b_bdt': _L0_attn_in['b_bdt'], 'L0_attn_b_Alog': _L0_attn_in['b_Alog'], 'L0_attn_b_D': _L0_attn_in['b_D'], 'L0_attn_b_Wout': _L0_attn_in['b_Wout'], 'L0_ffn_W1': _L0_ffn_in['W1'], 'L0_ffn_b1': _L0_ffn_in['b1'], 'L0_ffn_W2': _L0_ffn_in['W2'], 'L0_ffn_b2': _L0_ffn_in['b2'], 'L0_ffn_Wr': _L0_ffn_in['Wr'], 'L0_ffn_br': _L0_ffn_in['br'], 'L0_ffn_gamma': _L0_ffn_in['gamma'], 'L0_ffn_beta': _L0_ffn_in['beta'], 'L1_attn_norm1_w': _L1_attn_in['norm1_w'], 'L1_attn_norm2_w': _L1_attn_in['norm2_w'], 'L1_attn_g_wq': _L1_attn_in['g_wq'], 'L1_attn_g_kv_down': _L1_attn_in['g_kv_down'], 'L1_attn_g_k_up': _L1_attn_in['g_k_up'], 'L1_attn_g_v_up': _L1_attn_in['g_v_up'], 'L1_attn_g_wo': _L1_attn_in['g_wo'], 'L1_attn_l_wq': _L1_attn_in['l_wq'], 'L1_attn_l_wk': _L1_attn_in['l_wk'], 'L1_attn_l_wv': _L1_attn_in['l_wv'], 'L1_attn_l_wo': _L1_attn_in['l_wo'], 'L1_ffn_Wg': _L1_ffn_in['Wg'], 'L1_ffn_W1': _L1_ffn_in['W1'], 'L1_ffn_W2': _L1_ffn_in['W2']}
    _x0 = _d['L0_attn_x']
    _d['L0_attn_x'] = jax.random.normal(jax.random.fold_in(jax.random.key(seed), 1), (8, 256, 128), dtype=_x0.dtype)
    del _x0
    return _d

def reference(L0_attn_x, L0_attn_norm_g, L0_attn_norm_b, L0_attn_f_Win, L0_attn_f_convw, L0_attn_f_convb, L0_attn_f_Wx, L0_attn_f_Wdt, L0_attn_f_bdt, L0_attn_f_Alog, L0_attn_f_D, L0_attn_f_Wout, L0_attn_b_Win, L0_attn_b_convw, L0_attn_b_convb, L0_attn_b_Wx, L0_attn_b_Wdt, L0_attn_b_bdt, L0_attn_b_Alog, L0_attn_b_D, L0_attn_b_Wout, L0_ffn_W1, L0_ffn_b1, L0_ffn_W2, L0_ffn_b2, L0_ffn_Wr, L0_ffn_br, L0_ffn_gamma, L0_ffn_beta, L1_attn_norm1_w, L1_attn_norm2_w, L1_attn_g_wq, L1_attn_g_kv_down, L1_attn_g_k_up, L1_attn_g_v_up, L1_attn_g_wo, L1_attn_l_wq, L1_attn_l_wk, L1_attn_l_wv, L1_attn_l_wo, L1_ffn_Wg, L1_ffn_W1, L1_ffn_W2):

    def _L0_attn_ref(x, norm_g, norm_b, f_Win, f_convw, f_convb, f_Wx, f_Wdt, f_bdt, f_Alog, f_D, f_Wout, b_Win, b_convw, b_convb, b_Wx, b_Wdt, b_bdt, b_Alog, b_D, b_Wout):
        import jax, jax.numpy as jnp
        import numpy as np
        D_MODEL = 128
        D_STATE = 16
        D_CONV = 4
        EXPAND = 2
        D_INNER = EXPAND * D_MODEL
        DT_RANK = (D_MODEL + 15) // 16
        BATCH = 2
        SEQ = 256
        EPS = 1e-05

        def _mamba_params(key, scale=0.02):
            ks = jax.random.split(key, 8)
            n = lambda k, s: jax.random.normal(k, s, jnp.float32) * scale
            return {'Win': n(ks[0], (2 * D_INNER, D_MODEL)), 'convw': n(ks[1], (D_INNER, 1, D_CONV)), 'convb': n(ks[2], (D_INNER,)), 'Wx': n(ks[3], (DT_RANK + 2 * D_STATE, D_INNER)), 'Wdt': n(ks[4], (D_INNER, DT_RANK)), 'bdt': n(ks[5], (D_INNER,)), 'Alog': jnp.log(jnp.tile(jnp.arange(1, D_STATE + 1, dtype=jnp.float32), (D_INNER, 1))), 'D': jnp.ones((D_INNER,), jnp.float32), 'Wout': n(ks[6], (D_MODEL, D_INNER))}

        def _mamba(x, Win, convw, convb, Wx, Wdt, bdt, Alog, Dp, Wout):
            B, L, _ = x.shape
            xz = jnp.einsum('bld,ed->ble', x, Win)
            u, z = jnp.split(xz, 2, axis=-1)
            uc = jnp.transpose(u, (0, 2, 1))
            uc = jnp.pad(uc, ((0, 0), (0, 0), (D_CONV - 1, 0)))
            uc = jax.lax.conv_general_dilated(uc, convw, (1,), 'VALID', feature_group_count=D_INNER)
            uc = uc + convb[None, :, None]
            u = jax.nn.silu(jnp.transpose(uc, (0, 2, 1)))
            xdbl = jnp.einsum('bld,ed->ble', u, Wx)
            dtr, Bm, Cm = jnp.split(xdbl, [DT_RANK, DT_RANK + D_STATE], axis=-1)
            dt = jax.nn.softplus(jnp.einsum('blr,dr->bld', dtr, Wdt) + bdt)
            A = -jnp.exp(Alog)

            def step(h, ins):
                dt_t, u_t, B_t, C_t = ins
                h = jnp.exp(dt_t[..., None] * A) * h + (dt_t * u_t)[..., None] * B_t[:, None, :]
                y_t = jnp.einsum('bdn,bn->bd', h, C_t)
                return (h, y_t)
            h0 = jnp.zeros((B, D_INNER, D_STATE), jnp.float32)
            xs = (jnp.moveaxis(dt, 1, 0), jnp.moveaxis(u, 1, 0), jnp.moveaxis(Bm, 1, 0), jnp.moveaxis(Cm, 1, 0))
            _, ys = jax.lax.scan(step, h0, xs)
            y = jnp.moveaxis(ys, 0, 1) + u * Dp
            y = y * jax.nn.silu(z)
            return jnp.einsum('bld,ed->ble', y, Wout)
        mu = jnp.mean(x, axis=-1, keepdims=True)
        var = jnp.var(x, axis=-1, keepdims=True)
        xn = (x - mu) * jax.lax.rsqrt(var + EPS) * norm_g + norm_b
        y_fwd = _mamba(xn, f_Win, f_convw, f_convb, f_Wx, f_Wdt, f_bdt, f_Alog, f_D, f_Wout)
        y_bwd = _mamba(jnp.flip(xn, axis=1), b_Win, b_convw, b_convb, b_Wx, b_Wdt, b_bdt, b_Alog, b_D, b_Wout)
        y_bwd = jnp.flip(y_bwd, axis=1)
        return x + y_fwd + y_bwd

    def _L0_ffn_ref(x, W1, b1, W2, b2, Wr, br, gamma, beta):
        import jax, jax.numpy as jnp
        import numpy as np
        B, S, D, F, E, TOP_K = (4, 256, 128, 512, 8, 2)
        LN_EPS = 1e-05
        b, s, d = x.shape
        e = Wr.shape[1]
        rw = jax.nn.softmax(x.mean(axis=1) @ Wr + br, axis=-1)
        x_flat = x.reshape(-1, d)
        rw_tok = jnp.repeat(rw, s, axis=0)
        tk_w, tk_i = jax.lax.top_k(rw_tok, TOP_K)
        tk_w = jax.nn.softmax(tk_w, axis=-1)
        h = jax.nn.gelu(jnp.einsum('nd,edf->enf', x_flat, W1) + b1[:, None, :], approximate=False)
        expert_out = jnp.einsum('enf,efd->end', h, W2) + b2[:, None, :]
        onehot = jax.nn.one_hot(tk_i, e, dtype=x.dtype)
        cw = jnp.einsum('nk,nke->ne', tk_w, onehot)
        out = jnp.einsum('ne,end->nd', cw, expert_out).reshape(b, s, d)
        y = out + x
        mu = y.mean(axis=-1, keepdims=True)
        var = y.var(axis=-1, keepdims=True)
        return (y - mu) / jnp.sqrt(var + LN_EPS) * gamma + beta

    def _L1_attn_ref(hidden, norm1_w, norm2_w, g_wq, g_kv_down, g_k_up, g_v_up, g_wo, l_wq, l_wk, l_wv, l_wo):
        import jax, jax.numpy as jnp
        import numpy as np
        D = 128
        H = 16
        KVH = 4
        HD = D // H
        LAT = 32
        WIN = 32
        B, S = (1, 256)
        BASE_G, BASE_L = (1000000.0, 10000.0)
        EPS = 1e-06

        def rmsnorm(x, w):
            return x * jax.lax.rsqrt(jnp.mean(x * x, axis=-1, keepdims=True) + EPS) * w

        def qk_norm(x):
            return x * jax.lax.rsqrt(jnp.mean(x * x, axis=-1, keepdims=True) + EPS)

        def rope(x, base):
            s, hd = (x.shape[-2], x.shape[-1])
            inv_freq = 1.0 / base ** (jnp.arange(0, hd, 2, dtype=jnp.float32) / hd)
            freqs = jnp.arange(s, dtype=jnp.float32)[:, None] * inv_freq[None, :]
            cos, sin = (jnp.cos(freqs), jnp.sin(freqs))
            xe, xo = (x[..., ::2], x[..., 1::2])
            out = jnp.stack([xe * cos - xo * sin, xe * sin + xo * cos], axis=-1)
            return out.reshape(x.shape)

        def split_heads(x, n_heads):
            b, s, _ = x.shape
            return x.reshape(b, s, n_heads, HD).transpose(0, 2, 1, 3)

        def repeat_kv(x):
            return jnp.repeat(x, H // KVH, axis=1)

        def sdpa(q, k, v, mask):
            scores = jnp.einsum('bhqd,bhkd->bhqk', q, k) / np.sqrt(HD).astype(np.float32)
            scores = jnp.where(mask, scores, jnp.float32(-1e+30))
            probs = jax.nn.softmax(scores, axis=-1)
            return jnp.einsum('bhqk,bhkd->bhqd', probs, v)

        def merge_heads(x):
            b, h, s, hd = x.shape
            return x.transpose(0, 2, 1, 3).reshape(b, s, h * hd)

        def global_latent_attn(x, wq, w_kv_down, w_k_up, w_v_up, wo):
            q = split_heads(x @ wq, H)
            latent = x @ w_kv_down
            k = split_heads(latent @ w_k_up, KVH)
            v = split_heads(latent @ w_v_up, KVH)
            q, k = (rope(q, BASE_G), rope(k, BASE_G))
            q, k = (qk_norm(q), qk_norm(k))
            k, v = (repeat_kv(k), repeat_kv(v))
            i = jnp.arange(x.shape[1])
            causal = i[:, None] >= i[None, :]
            return merge_heads(sdpa(q, k, v, causal)) @ wo

        def local_gqa_attn(x, wq, wk, wv, wo):
            q = split_heads(x @ wq, H)
            k = split_heads(x @ wk, KVH)
            v = split_heads(x @ wv, KVH)
            q, k = (rope(q, BASE_L), rope(k, BASE_L))
            q, k = (qk_norm(q), qk_norm(k))
            k, v = (repeat_kv(k), repeat_kv(v))
            i = jnp.arange(x.shape[1])
            diff = i[:, None] - i[None, :]
            mask = (diff >= 0) & (diff < WIN)
            return merge_heads(sdpa(q, k, v, mask)) @ wo
        x = hidden
        x = x + global_latent_attn(rmsnorm(x, norm1_w), g_wq, g_kv_down, g_k_up, g_v_up, g_wo)
        x = x + local_gqa_attn(rmsnorm(x, norm2_w), l_wq, l_wk, l_wv, l_wo)
        return x

    def _L1_ffn_ref(token_inputs, Wg, W1, W2):
        import jax, jax.numpy as jnp
        import numpy as np
        CAPACITY_FACTOR = 1.0

        def _route(token_inputs, Wg, capacity):
            dt = token_inputs.dtype
            logits = jnp.einsum('bnd,de->bne', token_inputs, Wg)
            gates = jax.nn.softmax(logits, axis=-1)
            expert_idx = jnp.argmax(gates, axis=-1)
            mask = jax.nn.one_hot(expert_idx, Wg.shape[1], dtype=dt)
            gate = jnp.sum(gates * mask, axis=-1)
            pos = jnp.cumsum(mask, axis=1) * mask - mask
            keep = mask * (pos < capacity).astype(dt)
            pos_oh = jax.nn.one_hot(pos.astype(jnp.int32), capacity, dtype=dt)
            dispatch = keep[..., None] * pos_oh
            combine = dispatch * gate[:, :, None, None]
            return (dispatch, combine)
        B, N, D = token_inputs.shape
        E = Wg.shape[1]
        capacity = int(N * CAPACITY_FACTOR // E)
        dispatch, combine = _route(token_inputs, Wg, capacity)
        expert_inputs = jnp.einsum('bnd,bnec->becd', token_inputs, dispatch)
        h = jax.nn.gelu(jnp.einsum('becd,edh->bech', expert_inputs, W1))
        expert_outputs = jnp.einsum('bech,ehd->becd', h, W2)
        output = jnp.einsum('becd,bnec->bnd', expert_outputs, combine)
        return output
    x = L0_attn_x
    xn = _layernorm(x, axis=-1)
    x = x + _L0_attn_ref(xn, L0_attn_norm_g, L0_attn_norm_b, L0_attn_f_Win, L0_attn_f_convw, L0_attn_f_convb, L0_attn_f_Wx, L0_attn_f_Wdt, L0_attn_f_bdt, L0_attn_f_Alog, L0_attn_f_D, L0_attn_f_Wout, L0_attn_b_Win, L0_attn_b_convw, L0_attn_b_convb, L0_attn_b_Wx, L0_attn_b_Wdt, L0_attn_b_bdt, L0_attn_b_Alog, L0_attn_b_D, L0_attn_b_Wout) + _L0_ffn_ref(xn, L0_ffn_W1, L0_ffn_b1, L0_ffn_W2, L0_ffn_b2, L0_ffn_Wr, L0_ffn_br, L0_ffn_gamma, L0_ffn_beta)
    xn = _layernorm(x, axis=-1)
    x = x + _L1_attn_ref(xn, L1_attn_norm1_w, L1_attn_norm2_w, L1_attn_g_wq, L1_attn_g_kv_down, L1_attn_g_k_up, L1_attn_g_v_up, L1_attn_g_wo, L1_attn_l_wq, L1_attn_l_wk, L1_attn_l_wv, L1_attn_l_wo) + _L1_ffn_ref(xn, L1_ffn_Wg, L1_ffn_W1, L1_ffn_W2)
    return x

_drawn_inputs = setup_inputs


def setup_inputs(seed=0):
    import zlib

    import numpy as np

    out = dict(_drawn_inputs(seed))
    spreads = {'L0_attn_norm_g': (1.0, 0.6),
     'L0_attn_norm_b': (0.0, 0.8),
     'L0_attn_f_D': (1.0, 0.6),
     'L0_attn_b_D': (1.0, 0.6),
     'L0_ffn_b1': (0.0, 2.0),
     'L0_ffn_b2': (0.0, 2.0),
     'L0_ffn_br': (0.0, 0.339),
     'L0_ffn_gamma': (1.0, 0.6),
     'L0_ffn_beta': (0.0, 2.0),
     'L1_attn_norm1_w': (1.0, 0.6),
     'L1_attn_norm2_w': (1.0, 0.6)}
    factors = {'L0_attn_f_Win': 8.0,
     'L0_attn_f_convw': 8.0,
     'L0_attn_f_convb': 8.0,
     'L0_attn_f_Wx': 8.0,
     'L0_attn_f_Wdt': 8.0,
     'L0_attn_f_bdt': 8.0,
     'L0_attn_f_Alog': 8.0,
     'L0_attn_f_Wout': 8.0,
     'L0_attn_b_Win': 8.0,
     'L0_attn_b_convw': 8.0,
     'L0_attn_b_convb': 8.0,
     'L0_attn_b_Wx': 8.0,
     'L0_attn_b_Wdt': 8.0,
     'L0_attn_b_bdt': 8.0,
     'L0_attn_b_Alog': 8.0,
     'L0_attn_b_Wout': 8.0,
     'L1_attn_g_wq': 8.0,
     'L1_attn_g_kv_down': 8.0,
     'L1_attn_g_k_up': 8.0,
     'L1_attn_g_v_up': 8.0,
     'L1_attn_g_wo': 8.0,
     'L1_attn_l_wq': 8.0,
     'L1_attn_l_wk': 8.0,
     'L1_attn_l_wv': 8.0,
     'L1_attn_l_wo': 8.0,
     'L1_ffn_Wg': 8.0,
     'L1_ffn_W1': 8.0,
     'L1_ffn_W2': 8.0,
     'L0_ffn_W1': 4.859,
     'L0_ffn_W2': 3.927,
     'L0_ffn_Wr': 7.677}
    for name, (base, spread) in spreads.items():
        noise = np.random.default_rng([zlib.crc32(name.encode()), seed]).standard_normal(out[name].shape)
        drawn = base * np.exp(spread * noise) if base else spread * noise
        out[name] = jnp.asarray(drawn.astype(out[name].dtype))
    for name, factor in factors.items():
        out[name] = (out[name] * factor).astype(out[name].dtype)
    return out
```

```python
from contextlib import ExitStack

import concourse.bass as bass
from concourse import mybir
from concourse.bass import ds

F32 = mybir.dt.float32
BF16 = mybir.dt.bfloat16
F16 = mybir.dt.float16
U32 = mybir.dt.uint32
ALU = mybir.AluOpType
ACT = mybir.ActivationFunctionType
AX = mybir.AxisListType

P = 128
D = 128
SEQS, SEQ = 8, 256
TOK = SEQS * SEQ
TILES = TOK // P
INNER = 256
HALVES = INNER // P
STATES = 16
RANK = 8
TAPS = 4
LN_EPS = 1e-5
RMS_EPS = 1e-6
EXPERTS = 8
HIDDEN = 512
CHUNKS = HIDDEN // P
HEADS, KV, HD = 16, 4, 8
GROUP = HEADS // KV
LAT = 32
WINDOW = 32
VW = 32
CAP = SEQ // EXPERTS

COLS = 512
PAIRS = TOK // COLS
STEPS = 2 * PAIRS
BODIES = STATES // 2
UNITS = 2 * HALVES
NPAR = TAPS + 3 + STATES
XROWS = 3 * 2 * STATES + RANK
DT_ROW = 3 * 2 * STATES
PACK = HIDDEN + CHUNKS + HIDDEN
PACK1 = 2 * HIDDEN
R_BASE = 4
MASKED = -30000.0

SIGNALS = [
    "x_loaded", "consts_loaded", "mamba_weights_loaded", "gate_weights_loaded", "l1_weights_loaded",
    "expert_loaded0", "expert_loaded1", "out_stored",
    "sum_done", "centred", "squared", "var_done", "pow_done", "normed", "halfconst",
    "spread_ready", "a_ready", "a_exp", "diag_ready", "zero_cols",
    "turned", "turned_copied",
    "side_ready", "side_free",
    "u_copied", "conv_base", "conv_tap", "u_ready", "z_ready", "hi_ready", "mid_ready",
    "bc_part", "bc_ready", "dtr_ready", "dt_abs", "dt_exp", "dt_ln", "dt_ready", "dtu_ready",
    "b_spread", "b_copied", "c_spread", "decay_ready", "drive_ready", "scan_done", "hc_ready", "y_added",
    "gated", "acc_added",
    "pool_mean", "gate_step", "gate_act", "gate_pe", "index_ready", "cw_ready", "gelu_done",
    "moe_bias",
    "x1_ready", "r_pe", "r_dve", "r_act", "slots_spread", "slots_copied", "e_up", "e_gelu", "e_down",
    "e_out", "e_turn", "e_turned", "e_comb", "e_added", "d_turn", "d_turned",
    "at_copied", "lat_ready", "lat_copied", "qkv_ready", "rope_a", "rope_b", "roped", "v_ready",
    "qk_sq", "qk_sum", "qk_var", "qk_sqrt", "qk_inv", "qk_normed", "qk_hi", "qk_split",
    "turn_q", "turn_copied", "scores_ready", "probs_ready", "av_done", "den_done", "head_out",
    "o_turn", "o_copied", "o_proj", "resid", "ones_ready", "v_placed", "av_copied", "av_turned", "rms_done",
]


def timeline():
    pair = iter(range(2 * SEQS))
    order = [("proj", 0, s) for s in range(4)]
    for g in range(STEPS):
        more = g + 1 < STEPS
        order.append(("body", g, 0))
        if g:
            order.append(("finish", g - 1))
        else:
            order.append(("gate",))
        if more:
            order.append(("proj", g + 1, 0))
        order.append(("loop", g, 1, 3))
        if more:
            order.append(("proj", g + 1, 1))
        if g in (1, 2):
            order.append(("expert", next(pair)))
        order.append(("loop", g, 3, 5))
        if more:
            order.append(("proj", g + 1, 2))
        if g:
            order.append(("expert", next(pair)))
        order.append(("loop", g, 5, 7))
        if more:
            order.append(("proj", g + 1, 3))
        if g:
            order.append(("expert", next(pair)))
        order.append(("body", g, 7))
        order.append(("tail", g))
    order.append(("finish", STEPS - 1))
    return order


ORDER = timeline()


def side_uses():
    parts = {"finish": 1, "gate": 3, "expert": 3}
    uses = {}
    for ev in ORDER:
        n = (2, 2, 1, 2)[ev[2]] if ev[0] == "proj" else parts.get(ev[0], 0)
        for k in range(n):
            uses[ev, k] = len(uses)
    return uses


SIDE = side_uses()


def build(nc, a, out):
    with ExitStack() as ctx:
        def sb(name, shape, dt=F32):
            return ctx.enter_context(nc.sbuf_tensor(name, shape, dt))

        sem = {name: ctx.enter_context(nc.semaphore(name)) for name in SIGNALS}

        ps = ctx.enter_context(nc.psum_tensor("ps", [P, 8, 512], F32))

        x_sb = sb("x_sb", [P, TILES, D])
        xn = sb("xn", [P, TILES, D])
        xm = sb("xm", [P, TILES, D])
        sq = sb("sq", [P, TILES, D])
        xnT = sb("xnT", [P, TOK])
        xmT = sb("xmT", [P, TOK])
        acc = sb("acc", [P, TILES, D])
        moe = sb("moe", [P, TILES, D])
        stat = sb("stat", [P, 4, TILES])
        halfc = sb("halfc", [P, TILES])
        ident = sb("ident", [P, P])
        cols = sb("cols", [P, 4])
        par = sb("par", [P, 2, HALVES, NPAR])
        diagD = sb("diagD", [P, 2, HALVES, P])
        spread = sb("spread", [96, 2 * STATES], BF16)
        spreadf = sb("spreadf", [96, 2 * STATES])
        negA = sb("negA", [P, 2, HALVES, STATES])

        l0 = ExitStack()

        def sb(name, shape, dt=F32):
            return l0.enter_context(nc.sbuf_tensor(name, shape, dt))

        w_in = sb("w_in", [P, 2, 2 * INNER])
        w_x = sb("w_x", [P, 2, HALVES, XROWS])
        w_dt = sb("w_dt", [P, 2, INNER])
        u_raw = sb("u_raw", [P, HALVES, COLS])
        conv = sb("conv", [P, HALVES, COLS])
        w_out = sb("w_out", [P, 2, HALVES, D])

        u_s = sb("u_s", [P, 2, HALVES, COLS])
        z_s = sb("z_s", [P, 2, HALVES, COLS])
        dt = sb("dt", [P, 2, HALVES, COLS])
        dtu = sb("dtu", [P, 2, HALVES, COLS])
        dt_a = sb("dt_a", [P, COLS])
        dt_b = sb("dt_b", [P, COLS])
        dtr = sb("dtr", [P, COLS])
        bc = sb("bc", [96, 2, COLS], BF16)
        bc_rest = sb("bc_rest", [96, COLS])
        bc_mid = sb("bc_mid", [96, COLS], BF16)
        b_sb = sb("b_sb", [P, 2, COLS])
        drive = sb("drive", [P, UNITS, COLS])
        h = sb("h", [P, UNITS, COLS])
        hc = sb("hc", [P, UNITS, COLS])
        yg = sb("yg", [P, HALVES, COLS])

        w_r = sb("w_r", [P, EXPERTS])
        br = sb("br", [SEQS, EXPERTS])
        b2 = sb("b2", [EXPERTS, D])
        gb = sb("gb", [P, 2, D])
        small = sb("small", [SEQS, 16, EXPERTS])
        iota8 = sb("iota8", [SEQS, EXPERTS])
        pooled = sb("pooled", [P, SEQS])
        index = sb("index", [SEQS, EXPERTS], U32)
        ones8 = sb("ones8", [SEQS, P])
        cwT = sb("cwT", [EXPERTS, SEQS])
        wdiag = sb("wdiag", [SEQS, SEQS, 2])
        cw = sb("cw", [P, SEQS, 2])
        wbuf = sb("wbuf", [P, 2, PACK])
        hT = sb("hT", [P, 2, CHUNKS, SEQ])

        l0.close()

        def sb(name, shape, dt=F32):
            return ctx.enter_context(nc.sbuf_tensor(name, shape, dt))

        rope = sb("rope", [P, 2, 2, 2 * D])
        masks = sb("masks", [P, 3, P], F16)
        ident16 = sb("ident16", [P, P], F16)
        w_q = sb("w_q", [P, 2, D])
        w_kvd = sb("w_kvd", [P, LAT])
        w_kvu = sb("w_kvu", [LAT, 2 * KV * HD])
        w_kv = sb("w_kv", [P, 2 * KV * HD])
        w_o = sb("w_o", [P, 2, D])
        w_g = sb("w_g", [P, EXPERTS])
        tri = sb("tri", [P, 2, P], F16)
        iota32 = sb("iota32", [P, CAP])
        iotar = sb("iotar", [P, EXPERTS])
        qk = sb("qk", [P, TILES * (HEADS + KV), HD])
        rot = sb("rot", [P, 2, TILES * (HEADS + KV) * HD])
        norm = sb("norm", [P, 3, TILES * (HEADS + KV)])
        qs = sb("qs", [P, TILES * HEADS, 4, HD], F16)
        ks = sb("ks", [P, TILES * KV, 4, HD], F16)
        qT = sb("qT", [P, 2, GROUP, SEQ], F16)
        kT = sb("kT", [P, 2, SEQ], F16)
        probs = sb("probs", [P, 6, COLS])
        v_sb = sb("v_sb", [P, TILES, KV, HD])
        v_ring = sb("v_ring", [P, 2, 2, KV, VW])
        avT = sb("avT", [P, 2, COLS])
        den = sb("den", [P, 2, HEADS])
        latT = sb("latT", [LAT, TOK])
        route = sb("route", [P, 6, TILES, EXPERTS])
        rstat = sb("rstat", [P, 4, TILES])
        mask16 = sb("mask16", [P, TILES, EXPERTS], F16)
        slot = sb("slot", [P, TILES, EXPERTS, CAP])
        slotT = sb("slotT", [P, 2, TILES, P])
        xe = sb("xe", [P, SEQS, EXPERTS, CAP])
        eo = slot[:].rearrange("p t e c -> p (t e c)")[:, 0:SEQS * 2 * D].rearrange("p (b s d) -> p b s d", b=SEQS, s=2)
        wbuf1 = rot[:, 0, 0:2 * PACK1].rearrange("p (r n) -> p r n", r=2)
        hT1 = rot[:, 1, 0:2 * CHUNKS * SEQ].rearrange("p (r c n) -> p r c n", r=2, c=CHUNKS)
        heads = moe

        B_BANK, C_BANK, DECAY, Y_BANK, SIDE_BANK = 0, 1, 3, 5, 7
        side = ps[:, SIDE_BANK, :]

        block = ctx.enter_context(nc.Block())

        def after(eng, name, count):
            if not (isinstance(count, int) and count <= 0):
                eng.wait_ge(sem[name], count)

        def seqs(t):
            return t.rearrange("p (b t) -> p b t", t=SEQ)

        @block.sync
        def _(sp):
            sp.dma_start(x_sb[:], a["x"].rearrange("(t p) d -> p t d", p=P)).then_inc(sem["x_loaded"], 16)
            sp.dma_start(ident[:], a["ident"]).then_inc(sem["consts_loaded"], 16)
            sp.dma_start(cols[:], a["cols"]).then_inc(sem["consts_loaded"], 16)
            sp.dma_start(par[:], a["par"]).then_inc(sem["consts_loaded"], 16)
            sp.dma_start(w_in[:], a["w_in"]).then_inc(sem["mamba_weights_loaded"], 16)
            sp.dma_start(w_x[:], a["w_x"]).then_inc(sem["mamba_weights_loaded"], 16)
            sp.dma_start(w_dt[DT_ROW:DT_ROW + RANK], a["w_dt"]).then_inc(sem["mamba_weights_loaded"], 16)
            sp.dma_start(w_out[:], a["w_out"]).then_inc(sem["mamba_weights_loaded"], 16)
            sp.dma_start(w_r[:], a["w_r"]).then_inc(sem["gate_weights_loaded"], 16)
            sp.dma_start(br[:], a["br"].partition_broadcast(SEQS)).then_inc(sem["gate_weights_loaded"], 16)
            sp.dma_start(b2[:], a["b2"]).then_inc(sem["gate_weights_loaded"], 16)
            sp.dma_start(iota8[:], a["iota8"].partition_broadcast(SEQS)).then_inc(sem["gate_weights_loaded"], 16)
            sp.dma_start(gb[:, 0], a["gamma"].partition_broadcast(P)).then_inc(sem["gate_weights_loaded"], 16)
            sp.dma_start(gb[:, 1], a["beta"].partition_broadcast(P)).then_inc(sem["gate_weights_loaded"], 16)
            for p in range(2 * SEQS):
                after(sp, "index_ready", 1)
                if p >= 2:
                    sp.wait_ge(sem["side_free"], SIDE[("expert", p - 2), 2] + 1)
                e = sp.value_load(index[p // 2:p // 2 + 1, p % 2:p % 2 + 1], min_val=0, max_val=EXPERTS - 1)
                sp.dma_start(wbuf[:, p % 2], a["pack0"][ds(e, 1)].rearrange("e p n -> p (e n)")) \
                    .then_inc(sem[f"expert_loaded{p % 2}"], 16)
            sp.wait_ge(sem["side_free"], SIDE[("proj", STEPS - 1, 3), 1] + 1)
            for dst, name in ((rope, "rope"), (masks, "masks"), (ident16, "ident16"), (w_q, "w_q"), (w_kvd, "w_kvd"),
                              (w_kvu, "w_kvu"), (w_kv, "w_kv"), (w_o, "w_o"), (w_g, "w_g"), (tri, "tri")):
                sp.dma_start(dst[:], a[name]).then_inc(sem["l1_weights_loaded"], 16)
            sp.dma_start(iota32[:], a["iota32"].partition_broadcast(P)).then_inc(sem["l1_weights_loaded"], 16)
            sp.dma_start(iotar[:], a["iotar"].partition_broadcast(P)).then_inc(sem["l1_weights_loaded"], 16)
            sp.wait_ge(sem["x1_ready"], 1)
            for e in range(EXPERTS):
                after(sp, "e_down", e - 1)
                sp.dma_start(wbuf1[:, e % 2], a["pack1"][e]).then_inc(sem["expert_loaded%d" % (e % 2)], 16)
            sp.wait_ge(sem["x1_ready"], 5)
            sp.dma_start(out.rearrange("(t p) d -> p t d", p=P), x_sb[:]).then_inc(sem["out_stored"], 16)
            sp.wait_ge(sem["out_stored"], 16)

        @block.gpsimd
        def _(pool):
            pool.memset(halfc[:], -0.5).then_inc(sem["halfconst"], 1)
            pool.memset(ones8[:], 1.0).then_inc(sem["halfconst"], 1)
            pool.wait_ge(sem["halfconst"], 2)

            def rstd(use):
                after(pool, "var_done", use + 1)
                pool.tensor_tensor(stat[:, 3], stat[:, 2], halfc[:], ALU.pow).then_inc(sem["pow_done"], 1)

            rstd(0)
            rstd(1)

            def body(g, i):
                for s in range(2):
                    N = g * STATES + i * 2 + s
                    for half in range(HALVES):
                        q = N * 2 + half
                        after(pool, "b_copied", N + 1)
                        after(pool, "scan_done", q - UNITS + 1)
                        pool.tensor_tensor(drive[:, 2 * s + half], dtu[:, g % 2, half], b_sb[:, s], ALU.mult) \
                            .then_inc(sem["drive_ready"], 1)

            for ev in ORDER:
                if ev[0] == "body":
                    if ev[2] == 0:
                        after(pool, "dtu_ready", HALVES * (ev[1] + 1))
                    body(ev[1], ev[2])
                elif ev[0] == "loop":
                    with pool.Fori(ev[2], ev[3]) as i:
                        body(ev[1], i)
            for use in range(2, 6):
                rstd(use)
                if use == 2:
                    pool.wait_ge(sem["x1_ready"], 1)
                    pool.memset(v_ring[:], 0.0).then_inc(sem["ones_ready"], 1)
                    pool.wait_ge(sem["ones_ready"], 1)
                    pool.memset(v_ring[:, :, :, :, HD:HD + 1], 1.0).then_inc(sem["ones_ready"], 1)
                if use >= 4:
                    l = use - 4

                    def copy_v(b, r):
                        after(pool, "av_done", KV * (SEQS * l + b - 1))
                        pool.tensor_copy(v_ring[:, r, :, :, 0:HD], v_sb[:, ds(2 * b, 2)]).then_inc(sem["v_placed"], 1)

                    pool.wait_ge(sem["v_ready"], l + 1)
                    copy_v(0, 0)
                    copy_v(1, 1)
                    with pool.Fori(1, 4) as i:
                        copy_v(2 * i, 0)
                        copy_v(2 * i + 1, 1)

        @block.scalar
        def _(act):
            act.preload_act_table_set("natural_log_exp_and_others")
            act.wait_ge(sem["consts_loaded"], 48)
            act.activation(negA[:], par[:, :, :, TAPS + 3:], ACT.Exp).then_inc(sem["a_exp"], 1)
            for use in range(2):
                act.wait_ge(sem["centred"], use + 1)
                act.activation(sq[:], xm[:], ACT.Square).then_inc(sem["squared"], 1)

            for k in range(4):
                act.wait_ge(sem["turned"], k + 1)
                act.activation(xnT[:, k * 512:(k + 1) * 512], ps[:, k], ACT.Copy).then_inc(sem["turned_copied"], 1)
            for k in range(4):
                act.wait_ge(sem["turned"], k + 5)
                act.activation(xmT[:, k * 512:(k + 1) * 512], ps[:, k + 4], ACT.Identity,
                               scale=cols[:, 0:1], bias=cols[:, 1:2]).then_inc(sem["turned_copied"], 1)

            def proj(ev):
                _, g, s = ev
                dr = g // PAIRS
                if s == 0:
                    for half in range(HALVES):
                        act.wait_ge(sem["side_ready"], SIDE[ev, half] + 1)
                        after(act, "conv_tap", 3 * (HALVES * (g - 1) + half + 1))
                        after(act, "u_ready", HALVES * (g - 1) + half + 1)
                        act.activation(u_raw[:, half], side, ACT.Copy).then_inc(sem["u_copied"], 1)
                        act.activation(conv[:, half], side, ACT.Identity, scale=par[:, dr, half, TAPS - 1:TAPS],
                                       bias=par[:, dr, half, TAPS:TAPS + 1]).then_inc(sem["side_free"], 1)
                elif s == 1:
                    for half in range(HALVES):
                        act.wait_ge(sem["conv_tap"], 3 * (HALVES * g + half + 1))
                        after(act, "gated", HALVES * (g - 1))
                        act.activation(u_s[:, g % 2, half], conv[:, half], ACT.Silu).then_inc(sem["u_ready"], 1)
                    for half in range(HALVES):
                        act.wait_ge(sem["side_ready"], SIDE[ev, half] + 1)
                        act.activation(z_s[:, g % 2, half], side, ACT.Silu).then_inc(sem["side_free"], 1)
                    act.preload_act_table_set("natural_log_exp_and_others")
                elif s == 2:
                    act.wait_ge(sem["side_ready"], SIDE[ev, 0] + 1)
                    act.activation(dtr[DT_ROW:DT_ROW + RANK], ps[DT_ROW:DT_ROW + RANK, SIDE_BANK], ACT.Copy) \
                        .then_inc(sem["dtr_ready"], 1)
                    after(act, "c_spread", STATES * (g - 1))
                    act.activation(bc[:, g % 2], ps[0:96, SIDE_BANK], ACT.Copy).then_inc(sem["hi_ready"], 1)
                    act.wait_ge(sem["side_free"], SIDE[ev, 0] + 1)
                    after(act, "bc_ready", g)
                    act.activation(bc_mid[:], bc_rest[:], ACT.Copy).then_inc(sem["mid_ready"], 1)
                else:
                    for half in range(HALVES):
                        n = HALVES * g + half
                        bias = par[:, dr, half, TAPS + 1:TAPS + 2]
                        act.wait_ge(sem["side_ready"], SIDE[ev, half] + 1)
                        after(act, "dt_ready", n)
                        act.activation(dt_a[:], side, ACT.Abs, bias=bias).then_inc(sem["dt_abs"], 1)
                        act.activation(dt_b[:], side, ACT.Relu, bias=bias).then_inc(sem["side_free"], 1)
                        act.wait_ge(sem["dt_abs"], n + 1)
                        act.activation(dt_a[:], dt_a[:], ACT.Exp, scale=-1.0).then_inc(sem["dt_exp"], 1)
                        act.wait_ge(sem["dt_exp"], n + 1)
                        act.activation(dt_a[:], dt_a[:], ACT.Ln, bias=1.0).then_inc(sem["dt_ln"], 1)

            def body(g, i):
                back = g >= PAIRS
                lo = 0 if back else 1
                for s in range(2):
                    N = g * STATES + i * 2 + s
                    after(act, "b_spread", N + 1)
                    after(act, "drive_ready", 2 * N - 2)
                    act.activation(b_sb[:, s], ps[:, B_BANK], ACT.Copy).then_inc(sem["b_copied"], 1)
                    for half in range(HALVES):
                        q = N * 2 + half
                        after(act, "scan_done", q - 1)
                        scale = negA[:, g // PAIRS, half, ds(i * 2 + s, 1)]
                        act.activation(seqs(ps[:, DECAY + half])[:, :, lo:lo + SEQ - 1],
                                       seqs(dt[:, g % 2, half])[:, :, lo:lo + SEQ - 1],
                                       ACT.Exp, scale=scale).then_inc(sem["decay_ready"], 1)

            def gate(ev):
                act.wait_ge(sem["gate_step"], 2)
                act.activation(small[:, 2], small[:, 1], ACT.Exp).then_inc(sem["gate_act"], 1)
                act.wait_ge(sem["gate_step"], 6)
                act.activation(small[:, 9, 0:1], small[:, 8, 0:1], ACT.Exp).then_inc(sem["gate_act"], 1)

            def expert(ev):
                p = ev[1]
                act.wait_ge(sem[f"expert_loaded{p % 2}"], 16 * (p // 2 + 1))
                if p >= 2:
                    act.wait_ge(sem["side_ready"], SIDE[("expert", p - 2), 2] + 1)
                for c in range(CHUNKS):
                    act.wait_ge(sem["side_ready"], SIDE[ev, c // 2] + 1)
                    done = act.activation(hT[:, p % 2, c], side[:, (c % 2) * SEQ:(c % 2 + 1) * SEQ], ACT.Gelu,
                                          bias=wbuf[:, p % 2, HIDDEN + c:HIDDEN + c + 1])
                    done.then_inc(sem["side_free" if c % 2 else "gelu_done"], 1)
                act.preload_act_table_set("natural_log_exp_and_others")

            for ev in ORDER:
                if ev[0] == "proj":
                    proj(ev)
                elif ev[0] == "body":
                    if ev[2] == 0:
                        act.wait_ge(sem["dt_ready"], HALVES * (ev[1] + 1))
                        act.wait_ge(sem["a_ready"], 1)
                        act.wait_ge(sem["zero_cols"], HALVES * (ev[1] // PAIRS + 1))
                    body(ev[1], ev[2])
                elif ev[0] == "loop":
                    with act.Fori(ev[2], ev[3]) as i:
                        body(ev[1], i)
                elif ev[0] == "gate":
                    gate(ev)
                elif ev[0] == "expert":
                    expert(ev)
            for use in (2, 3):
                act.wait_ge(sem["centred"], use + 1)
                act.activation(sq[:], xm[:], ACT.Square).then_inc(sem["squared"], 1)

            for k in range(4):
                act.wait_ge(sem["turned"], k + 9)
                act.activation(xnT[:, k * 512:(k + 1) * 512], ps[:, k], ACT.Copy).then_inc(sem["turned_copied"], 1)
            act.wait_ge(sem["r_dve"], R_BASE + 2)
            act.activation(route[:, 1], route[:, 0], ACT.Exp).then_inc(sem["r_act"], 1)
            for k in range(4):
                act.wait_ge(sem["slots_spread"], k + 1)
                act.activation(xe[:, 2 * k:2 * k + 2].rearrange("p b e c -> p (b e c)"), ps[:, k], ACT.Copy) \
                    .then_inc(sem["slots_copied"], 1)
            for e in range(EXPERTS):
                for c in range(CHUNKS):
                    act.wait_ge(sem["e_up"], 2 * e + c // 2 + 1)
                    if c == 0:
                        after(act, "e_down", e - 1)
                    act.activation(hT1[:, e % 2, c], ps[:, 2 * (e % 2) + c // 2, (c % 2) * SEQ:(c % 2 + 1) * SEQ],
                                   ACT.Gelu_apprx_tanh).then_inc(sem["e_gelu"], 1)
            act.preload_act_table_set("exp_and_others")
            for k in range(4):
                act.wait_ge(sem["e_turn"], k + 1)
                act.wait_ge(sem["d_turned"], 8)
                act.activation(eo[:, 2 * k:2 * k + 2].rearrange("p b s d -> p (b s d)"), ps[:, k], ACT.Copy) \
                    .then_inc(sem["e_turned"], 1)

            for l in range(2):
                act.wait_ge(sem["resid"] if l else sem["normed"], 4)
                act.activation(sq[:], (acc if l else xn)[:], ACT.Square).then_inc(sem["squared"], 1)
                for k in range(4):
                    act.wait_ge(sem["turned"], 12 + 4 * l + k + 1)
                    act.activation(xmT[:, k * 512:(k + 1) * 512], ps[:, k], ACT.Copy, scale=cols[:, 2 + l:3 + l]) \
                        .then_inc(sem["turned_copied"], 1)
                if l == 0:
                    for k in range(4):
                        act.wait_ge(sem["lat_ready"], k + 1)
                        act.activation(latT[:, k * 512:(k + 1) * 512], ps[0:LAT, 4 + k], ACT.Copy) \
                            .then_inc(sem["lat_copied"], 1)
                act.wait_ge(sem["qkv_ready"], l + 1)
                act.activation(v_sb[:],
                               ps[:, 4:6].rearrange("p k (t c) -> p (k t) c", c=2 * KV * HD)[:, :, KV * HD:]
                               .rearrange("p t (g d) -> p t g d", d=HD), ACT.Copy).then_inc(sem["v_ready"], 1)
                act.wait_ge(sem["roped"], 2 * l + 2)
                act.activation(rot[:, 0], qk[:].rearrange("p h d -> p (h d)"), ACT.Square).then_inc(sem["qk_sq"], 1)
                act.wait_ge(sem["qk_var"], l + 1)
                act.activation(norm[:, 1], norm[:, 0], ACT.Sqrt).then_inc(sem["qk_sqrt"], 1)
                act.preload_act_table_set("exp_and_others")
                act.wait_ge(sem["qk_normed"], l + 1)
                q_all, k_all = qk[:, 0:TILES * HEADS], qk[:, TILES * HEADS:]
                act.activation(qs[:, :, 0:2], q_all.unsqueeze(2).broadcast_to([P, TILES * HEADS, 2, HD]), ACT.Copy) \
                    .then_inc(sem["qk_hi"], 1)
                act.activation(ks[:, :, 0::2], k_all.unsqueeze(2).broadcast_to([P, TILES * KV, 2, HD]), ACT.Copy) \
                    .then_inc(sem["qk_hi"], 1)

                def step_probs(b, kv):
                    step = KV * (SEQS * l + b) + kv
                    for n in range(3):
                        unit = 3 * step + n
                        slot_p = 3 * (kv % 2) + n
                        bank = (3 * kv + n) % 4
                        after(act, "scores_ready", unit + 1)
                        after(act, "av_done", step - 1)
                        if l and n == 1:
                            keys, width = slice(P - WINDOW, P), GROUP * WINDOW
                        else:
                            keys, width = slice(0, P), COLS
                        act.activation(probs[keys, slot_p, 0:width], ps[keys, bank, 0:width], ACT.Exp, scale=HD ** -0.5) \
                            .then_inc(sem["probs_ready"], 1)

                def copy_av(b):
                    for qt in range(2):
                        after(act, "av_done", KV * (SEQS * l + b) + KV)
                        after(act, "av_turned", 2 * (SEQS * l + b) + qt - 1)
                        act.activation(avT[:, qt], ps[:, 5 + qt], ACT.Copy).then_inc(sem["av_copied"], 1)

                def sequence_probs(b, first=False):
                    for kv in range(KV):
                        step_probs(b, kv)
                        if kv == 0 and not first:
                            copy_av(b - 1)

                sequence_probs(0, first=True)
                sequence_probs(1)
                with act.Fori(2, SEQS) as b:
                    sequence_probs(b)
                copy_av(SEQS - 1)
                for k in range(4):
                    act.wait_ge(sem["o_turn"], 4 * l + k + 1)
                    act.activation(xmT[:, k * 512:(k + 1) * 512], ps[:, k], ACT.Copy).then_inc(sem["o_copied"], 1)

        @block.vector
        def _(dve):
            dve.wait_ge(sem["consts_loaded"], 48)
            dve.tensor_tensor(spreadf[:], ident[0:96, 0:32], ident[0:96, 32:64], ALU.add).then_inc(sem["spread_ready"], 1)
            dve.wait_ge(sem["spread_ready"], 1)
            dve.tensor_tensor(spread[:], spreadf[:], ident[0:96, 64:96], ALU.add).then_inc(sem["spread_ready"], 1)
            for dr in range(2):
                for half in range(HALVES):
                    dve.tensor_scalar(diagD[:, dr, half], ident[:], par[:, dr, half, TAPS + 2:TAPS + 3], None,
                                      ALU.mult).then_inc(sem["diag_ready"], 1)
            dve.wait_ge(sem["a_exp"], 1)
            dve.tensor_scalar(negA[:], negA[:], -1.0, None, ALU.mult).then_inc(sem["a_ready"], 1)

            def bcast(t):
                return t.unsqueeze(2).broadcast_to([P, TILES, D])

            def layernorm(use, src, dst):
                dve.tensor_reduce(stat[:, 0], src, AX.X, ALU.add).then_inc(sem["sum_done"], 1)
                dve.wait_ge(sem["sum_done"], 2 * use + 1)
                dve.tensor_scalar(stat[:, 1], stat[:, 0], 1.0 / D, None, ALU.mult).then_inc(sem["sum_done"], 1)
                dve.wait_ge(sem["sum_done"], 2 * use + 2)
                dve.tensor_tensor(xm[:], src, bcast(stat[:, 1]), ALU.subtract).then_inc(sem["centred"], 1)
                dve.wait_ge(sem["squared"], use + 1)
                dve.tensor_reduce(stat[:, 0], sq[:], AX.X, ALU.add).then_inc(sem["r_dve"], 1)
                dve.wait_ge(sem["r_dve"], use + 1)
                dve.tensor_scalar(stat[:, 2], stat[:, 0], 1.0 / D, LN_EPS, ALU.mult, ALU.add) \
                    .then_inc(sem["var_done"], 1)
                dve.wait_ge(sem["pow_done"], use + 1)
                dve.wait_ge(sem["centred"], use + 1)
                dve.tensor_tensor(dst, xm[:], bcast(stat[:, 3]), ALU.mult).then_inc(sem["normed"], 1)
                dve.wait_ge(sem["normed"], use + 1)

            dve.wait_ge(sem["x_loaded"], 16)
            layernorm(0, x_sb[:], xn[:])
            layernorm(1, xn[:], xm[:])
            dve.tensor_tensor(acc[:], x_sb[:], xn[:], ALU.add).then_inc(sem["acc_added"], 1)
            dve.wait_ge(sem["turned_copied"], 4)
            dve.tensor_reduce(pooled[:], seqs(xnT[:]), AX.X, ALU.add).then_inc(sem["pool_mean"], 1)

            def proj(ev):
                _, g, s = ev
                dr = g // PAIRS
                if s == 0:
                    for half in range(HALVES):
                        n = HALVES * g + half
                        dve.wait_ge(sem["u_copied"], n + 1)
                        dve.wait_ge(sem["side_free"], SIDE[ev, half] + 1)
                        for k in range(1, TAPS):
                            if dr == 0:
                                to, of = slice(k, SEQ), slice(0, SEQ - k)
                            else:
                                to, of = slice(0, SEQ - k), slice(k, SEQ)
                            c = seqs(conv[:, half])[:, :, to]
                            after(dve, "conv_tap", 3 * n + k - 1)
                            dve.scalar_tensor_tensor(out=c, in0=seqs(u_raw[:, half])[:, :, of],
                                                     scalar=par[:, dr, half, TAPS - 1 - k:TAPS - k], in1=c,
                                                     op0=ALU.mult, op1=ALU.add).then_inc(sem["conv_tap"], 1)
                elif s == 2:
                    dve.wait_ge(sem["hi_ready"], g + 1)
                    dve.tensor_tensor(bc_rest[:], ps[0:96, SIDE_BANK], bc[:, g % 2], ALU.subtract) \
                        .then_inc(sem["side_free"], 1)
                    dve.wait_ge(sem["mid_ready"], g + 1)
                    dve.tensor_copy(bc[32:64, g % 2], bc_mid[32:64]).then_inc(sem["bc_part"], 1)
                    dve.tensor_tensor(bc[64:96, g % 2], bc_rest[64:96], bc_mid[64:96], ALU.subtract) \
                        .then_inc(sem["bc_ready"], 1)
                elif s == 3:
                    for half in range(HALVES):
                        n = HALVES * g + half
                        dve.wait_ge(sem["dt_ln"], n + 1)
                        after(dve, "decay_ready", STATES * HALVES * (g - 1))
                        dve.tensor_tensor(dt[:, g % 2, half], dt_a[:], dt_b[:], ALU.add).then_inc(sem["dt_ready"], 1)
                        dve.wait_ge(sem["dt_ready"], n + 1)
                        dve.wait_ge(sem["u_ready"], n + 1)
                        after(dve, "drive_ready", STATES * HALVES * (g - 1))
                        dve.tensor_tensor(dtu[:, g % 2, half], dt[:, g % 2, half], u_s[:, g % 2, half], ALU.mult) \
                            .then_inc(sem["dtu_ready"], 1)

            def scan(g, i, k):
                N = g * STATES + i * 2 + k // 2
                q = N * 2 + k % 2
                after(dve, "decay_ready", q + 1)
                after(dve, "drive_ready", q + 1)
                after(dve, "hc_ready", q - UNITS + 1)
                turn = slice(None, None, -1) if g >= PAIRS else slice(None)
                dve.tensor_tensor_scan(h[:, k, turn], ps[:, DECAY + k % 2, turn], drive[:, k, turn], 0.0,
                                       ALU.mult, ALU.add).then_inc(sem["scan_done"], 1)

            def times_c(g, i, k):
                N = g * STATES + i * 2 + k // 2
                q = N * 2 + k % 2
                after(dve, "scan_done", q + 1)
                after(dve, "c_spread", N + 1)
                after(dve, "y_added", q - UNITS + 1)
                dve.tensor_tensor(hc[:, k], h[:, k], ps[:, C_BANK + k // 2], ALU.mult).then_inc(sem["hc_ready"], 1)

            def body(g, i):
                scan(g, i, 0)
                for k in range(1, UNITS):
                    scan(g, i, k)
                    times_c(g, i, k - 1)
                times_c(g, i, UNITS - 1)

            def zero_boundary(g):
                after(dve, "scan_done", STATES * HALVES * g)
                col = SEQ - 1 if g >= PAIRS else 0
                for half in range(HALVES):
                    dve.memset(seqs(ps[:, DECAY + half])[:, :, col:col + 1], 0.0).then_inc(sem["zero_cols"], 1)
                dve.wait_ge(sem["zero_cols"], 2 if g == 0 else 4)

            def finish(ev):
                g = ev[1]
                for half in range(HALVES):
                    n = HALVES * g + half
                    dve.wait_ge(sem["y_added"], STATES * HALVES * (g + 1) - 1 + half)
                    if g:
                        dve.wait_ge(sem["side_ready"], SIDE[("finish", g - 1), 0] + 1)
                    dve.tensor_tensor(yg[:, half], ps[:, Y_BANK + half], z_s[:, g % 2, half], ALU.mult) \
                        .then_inc(sem["gated"], 1)
                rows = acc[:, 4 * (g % PAIRS):4 * (g % PAIRS) + 4]
                dve.wait_ge(sem["side_ready"], SIDE[ev, 0] + 1)
                after(dve, "acc_added", 1)
                dve.tensor_tensor(rows, rows, side.rearrange("p (t d) -> p t d", d=D), ALU.add) \
                    .then_inc(sem["side_free"], 1)

            def gate(ev):
                step = [0]

                def link(ins):
                    step[0] += 1
                    ins.then_inc(sem["gate_step"], 1)
                    dve.wait_ge(sem["gate_step"], step[0])

                s = small
                dve.wait_ge(sem["gate_weights_loaded"], 96)
                dve.wait_ge(sem["side_ready"], SIDE[ev, 0] + 1)
                dve.scalar_tensor_tensor(out=s[:, 0], in0=side[0:SEQS, 0:EXPERTS], scalar=1.0 / SEQ, in1=br[:],
                                         op0=ALU.mult, op1=ALU.add).then_inc(sem["side_free"], 1)
                dve.wait_ge(sem["side_free"], SIDE[ev, 0] + 1)
                link(dve.tensor_reduce(s[:, 3, 0:1], s[:, 0], AX.X, ALU.max))
                link(dve.tensor_scalar(s[:, 1], s[:, 0], s[:, 3, 0:1], None, ALU.subtract))
                dve.wait_ge(sem["gate_act"], 1)
                link(dve.tensor_reduce(s[:, 3, 1:2], s[:, 2], AX.X, ALU.add))
                link(dve.reciprocal(s[:, 3, 2:3], s[:, 3, 1:2]))
                link(dve.tensor_scalar(s[:, 4], s[:, 2], s[:, 3, 2:3], None, ALU.mult))
                dve.max(s[:, 5], s[:, 4]).then_inc(sem["cw_ready"], 1)
                dve.wait_ge(sem["cw_ready"], 1)
                link(dve.tensor_tensor(s[:, 8, 0:1], s[:, 5, 1:2], s[:, 5, 0:1], ALU.subtract))
                dve.max_index(index[:], s[:, 5], s[:, 4]).then_inc(sem["index_ready"], 1)
                dve.wait_ge(sem["index_ready"], 1)
                link(dve.tensor_copy(s[:, 6], index[:]))
                dve.wait_ge(sem["gate_act"], 2)
                link(dve.tensor_scalar(s[:, 10, 0:1], s[:, 9, 0:1], 1.0, None, ALU.add))
                link(dve.reciprocal(s[:, 11, 0:1], s[:, 10, 0:1]))
                link(dve.tensor_tensor(s[:, 11, 1:2], s[:, 11, 0:1], s[:, 9, 0:1], ALU.mult))
                for k in range(2):
                    link(dve.tensor_scalar(s[:, 12 + k], iota8[:], s[:, 6, k:k + 1], s[:, 11, k:k + 1],
                                           ALU.is_equal, ALU.mult))
                link(dve.tensor_tensor(s[:, 14], s[:, 12], s[:, 13], ALU.add))
                link(dve.tensor_tensor(wdiag[:], ident[0:SEQS, 0:SEQS].unsqueeze(2).broadcast_to([SEQS, SEQS, 2]),
                                       s[:, 11, 0:2].unsqueeze(1).broadcast_to([SEQS, SEQS, 2]), ALU.mult))
                assert step[0] == 14
                dve.wait_ge(sem["side_ready"], SIDE[ev, 1] + 1)
                dve.tensor_copy(cwT[:], side[0:EXPERTS, 0:SEQS]).then_inc(sem["side_free"], 1)
                dve.wait_ge(sem["side_ready"], SIDE[ev, 2] + 1)
                dve.tensor_copy(cw[:], side[:, 0:2 * SEQS].rearrange("p (b k) -> p b k", k=2)) \
                    .then_inc(sem["side_free"], 1)

            def expert(ev):
                p = ev[1]
                b, k = p // 2, p % 2
                dve.wait_ge(sem["side_ready"], SIDE[ev, 2] + 1)
                rows = moe[:, 2 * b:2 * b + 2]
                if k == 0:
                    dve.tensor_tensor(rows, xn[:, 2 * b:2 * b + 2],
                                      side[:, 2 * D:3 * D].unsqueeze(1).broadcast_to([P, 2, D]), ALU.add) \
                        .then_inc(sem["moe_bias"], 1)
                    dve.wait_ge(sem["moe_bias"], b + 1)
                dve.scalar_tensor_tensor(out=rows, in0=side[:, 0:2 * D].rearrange("p (t d) -> p t d", d=D),
                                         scalar=cw[:, b, k:k + 1], in1=rows, op0=ALU.mult, op1=ALU.add) \
                    .then_inc(sem["side_free"], 1)

            for ev in ORDER:
                if ev[0] == "proj":
                    proj(ev)
                elif ev[0] == "body":
                    if ev[2] == 0 and ev[1] % PAIRS == 0:
                        zero_boundary(ev[1])
                    body(ev[1], ev[2])
                elif ev[0] == "loop":
                    with dve.Fori(ev[2], ev[3]) as i:
                        body(ev[1], i)
                elif ev[0] == "finish":
                    finish(ev)
                elif ev[0] == "gate":
                    gate(ev)
                elif ev[0] == "expert":
                    expert(ev)

            layernorm(2, moe[:], xm[:])
            for k, (dst, b) in enumerate(((xm, gb[:, 0]), (xm, gb[:, 1]), (x_sb, None))):
                other = acc[:] if b is None else b.unsqueeze(1).broadcast_to([P, TILES, D])
                dve.tensor_tensor(dst[:], xm[:], other, ALU.mult if k == 0 else ALU.add).then_inc(sem["x1_ready"], 1)
                dve.wait_ge(sem["x1_ready"], k + 1)

            layernorm(3, x_sb[:], xn[:])

            step = [R_BASE]

            def link(ins):
                step[0] += 1
                ins.then_inc(sem["r_dve"], 1)
                dve.wait_ge(sem["r_dve"], step[0])

            def per_expert(t):
                return t.unsqueeze(2).broadcast_to([P, TILES, EXPERTS])

            dve.wait_ge(sem["r_pe"], 1)
            logits = ps[:, 4, 0:TILES * EXPERTS].rearrange("p (t e) -> p t e", e=EXPERTS)
            link(dve.tensor_reduce(rstat[:, 0], logits, AX.X, ALU.max))
            link(dve.tensor_tensor(route[:, 0], logits, per_expert(rstat[:, 0]), ALU.subtract))
            dve.wait_ge(sem["l1_weights_loaded"], 12 * 16)
            link(dve.tensor_scalar(route[:, 2], route[:, 0], 0.0, None, ALU.is_equal))
            link(dve.tensor_tensor(route[:, 3], route[:, 2], iotar[:].unsqueeze(1).broadcast_to([P, TILES, EXPERTS]),
                                   ALU.mult))
            link(dve.tensor_reduce(rstat[:, 1], route[:, 3], AX.X, ALU.max))
            link(dve.tensor_tensor(route[:, 4], route[:, 3], per_expert(rstat[:, 1]), ALU.is_equal))
            link(dve.tensor_copy(mask16[:], route[:, 4]))
            dve.wait_ge(sem["r_act"], 1)
            link(dve.tensor_reduce(rstat[:, 2], route[:, 1], AX.X, ALU.add))
            link(dve.reciprocal(rstat[:, 3], rstat[:, 2]))
            dve.wait_ge(sem["r_pe"], 2)
            pos = route[:, 5].rearrange("p t e -> p (t e)").rearrange("p (two b e) -> p two b e", two=2, e=EXPERTS)
            for two in range(2):
                link(dve.tensor_tensor(pos[:, two], ps[:, 5, 64 * two:64 * two + 64].rearrange("p (b e) -> p b e", e=EXPERTS),
                                       route[:, 4, two::2], ALU.mult))
            for two in range(2):
                link(dve.tensor_tensor(slot[:, two::2], pos[:, two].unsqueeze(3).broadcast_to([P, SEQS, EXPERTS, CAP]),
                                       iota32[:].unsqueeze(1).unsqueeze(1).broadcast_to([P, SEQS, EXPERTS, CAP]), ALU.is_equal))
            for k in range(8):
                dve.wait_ge(sem["d_turn"], k + 1)
                dve.tensor_copy(slotT[:, k // 4, 4 * (k % 4):4 * (k % 4) + 4].rearrange("p t n -> p (t n)"),
                                ps[:, 4 + k % 4]).then_inc(sem["d_turned"], 1)
            for e in range(EXPERTS):
                dve.wait_ge(sem["e_down"], e + 1)
                dve.tensor_copy(xe[:, :, e], ps[:, 4 + e % 2, 0:SEQ].rearrange("p (b c) -> p b c", c=CAP)).then_inc(sem["e_out"], 1)
            for k in range(4):
                dve.wait_ge(sem["e_comb"], k + 1)
                rows = slice(4 * k, 4 * k + 4)
                dve.tensor_tensor(xm[:, rows], ps[:, 4 + k].rearrange("p (t d) -> p t d", d=D),
                                  rstat[:, 3, rows].unsqueeze(2).broadcast_to([P, 4, D]), ALU.mult) \
                    .then_inc(sem["e_added"], 1)
            dve.wait_ge(sem["e_added"], 4)
            dve.tensor_tensor(x_sb[:], x_sb[:], xm[:], ALU.add).then_inc(sem["x1_ready"], 1)

            for l in range(2):
                src = acc if l else xn
                dve.wait_ge(sem["squared"], 5 + l)
                dve.tensor_reduce(stat[:, 0], sq[:], AX.X, ALU.add).then_inc(sem["sum_done"], 1)
                dve.wait_ge(sem["sum_done"], 9 + l)
                dve.tensor_scalar(stat[:, 2], stat[:, 0], 1.0 / D, RMS_EPS, ALU.mult, ALU.add).then_inc(sem["var_done"], 1)
                dve.wait_ge(sem["pow_done"], 5 + l)
                dve.tensor_tensor(xm[:], src[:], bcast(stat[:, 3]), ALU.mult).then_inc(sem["rms_done"], 1)
                dve.wait_ge(sem["qkv_ready"], l + 1)
                nq = TILES * HEADS * HD
                qps = ps[:, 0:4].rearrange("p k c -> p (k c)")
                cos, sin = rope[:, l, 0], rope[:, l, 1]
                dve.tensor_tensor(rot[:, 0, 0:nq].rearrange("p (b c) -> p b c", b=SEQS), qps.rearrange("p (b c) -> p b c", b=SEQS),
                                  cos.unsqueeze(1).broadcast_to([P, SEQS, 2 * D]), ALU.mult).then_inc(sem["rope_a"], 1)
                dve.tensor_tensor(rot[:, 1, 0:nq].rearrange("p (b c two) -> p b c two", b=SEQS, two=2),
                                  qps.rearrange("p (b c two) -> p b c two", b=SEQS, two=2)[:, :, :, ::-1],
                                  sin.rearrange("p (c two) -> p c two", two=2).unsqueeze(1).broadcast_to([P, SEQS, D, 2]),
                                  ALU.mult).then_inc(sem["rope_a"], 1)
                dve.wait_ge(sem["v_ready"], l + 1)
                kps = ps[:, 4:6].rearrange("p k (t c) -> p (k t) c", c=2 * KV * HD)[:, :, 0:KV * HD]
                kr = rot[:, :, nq:].rearrange("p r (t c) -> p r t c", c=KV * HD)
                for two in range(2):
                    dve.tensor_tensor(kr[:, 0, two::2], kps[:, two::2],
                                      cos[:, two * D:two * D + KV * HD].unsqueeze(1).broadcast_to([P, SEQS, KV * HD]),
                                      ALU.mult).then_inc(sem["rope_a"], 1)
                    dve.tensor_tensor(kr[:, 1, two::2].rearrange("p t (c two) -> p t c two", two=2),
                                      kps[:, two::2].rearrange("p t (c two) -> p t c two", two=2)[:, :, :, ::-1],
                                      sin[:, two * D:two * D + KV * HD].rearrange("p (c two) -> p c two", two=2)
                                      .unsqueeze(1).broadcast_to([P, SEQS, KV * HD // 2, 2]),
                                      ALU.mult).then_inc(sem["rope_a"], 1)
                qk_flat = qk[:].rearrange("p h d -> p (h d)")
                for part, (lo, hi) in enumerate(((0, nq), (nq, nq + TILES * KV * HD))):
                    dve.wait_ge(sem["rope_a"], 6 * l + 2 + 4 * part)
                    dve.tensor_tensor(qk_flat[:, lo:hi], rot[:, 0, lo:hi], rot[:, 1, lo:hi], ALU.add).then_inc(sem["roped"], 1)
                dve.wait_ge(sem["qk_sq"], l + 1)
                dve.tensor_reduce(norm[:, 2], rot[:, 0].rearrange("p (h d) -> p h d", d=HD), AX.X, ALU.add) \
                    .then_inc(sem["qk_sum"], 1)
                dve.wait_ge(sem["qk_sum"], l + 1)
                dve.tensor_scalar(norm[:, 0], norm[:, 2], 1.0 / HD, RMS_EPS, ALU.mult, ALU.add).then_inc(sem["qk_var"], 1)
                dve.wait_ge(sem["qk_sqrt"], l + 1)
                dve.reciprocal(norm[:, 2], norm[:, 1]).then_inc(sem["qk_inv"], 1)
                dve.wait_ge(sem["qk_inv"], l + 1)
                dve.tensor_tensor(qk[:], qk[:], norm[:, 2].unsqueeze(2).broadcast_to([P, TILES * (HEADS + KV), HD]), ALU.mult) \
                    .then_inc(sem["qk_normed"], 1)
                q_all, k_all = qk[:, 0:TILES * HEADS], qk[:, TILES * HEADS:]
                dve.wait_ge(sem["qk_hi"], 2 * l + 1)
                dve.tensor_tensor(qs[:, :, 2:4], q_all.unsqueeze(2).broadcast_to([P, TILES * HEADS, 2, HD]), qs[:, :, 0:2],
                                  ALU.subtract).then_inc(sem["qk_split"], 1)
                dve.wait_ge(sem["qk_hi"], 2 * l + 2)
                dve.tensor_tensor(ks[:, :, 1::2], k_all.unsqueeze(2).broadcast_to([P, TILES * KV, 2, HD]), ks[:, :, 0::2],
                                  ALU.subtract).then_inc(sem["qk_split"], 1)

                def copy_turned(b, r):
                    for k in range(3):
                        after(dve, "turn_q", 3 * SEQS * l + 3 * b + k + 1)
                        if k == 0:
                            after(dve, "scores_ready", 3 * KV * (SEQS * l + b - 1))
                        if k < 2:
                            ins = dve.tensor_copy(qT[:, r, :, k * P:(k + 1) * P],
                                                  ps[:, 4].rearrange("p (j n) -> p j n", n=P))
                        else:
                            ins = dve.tensor_copy(kT[:, r], ps[:, 4, 0:SEQ])
                        ins.then_inc(sem["turn_copied"], 1)

                def seq_out(b):
                    for qt in range(2):
                        n = 2 * (SEQS * l + b) + qt
                        o = ps[:, 7].rearrange("p (j g d) -> p g j d", j=GROUP, g=KV)
                        after(dve, "av_turned", n + 1)
                        after(dve, "head_out", n - 1)
                        dve.reciprocal(den[:, qt].rearrange("p (g j) -> p g j", g=KV), o[:, :, :, HD]) \
                            .then_inc(sem["den_done"], 1)
                        after(dve, "den_done", n + 1)
                        dve.tensor_tensor(heads[:, ds(2 * b + qt, 1)].rearrange("p o (g j d) -> p (o g) j d", g=KV, j=GROUP),
                                          o[:, :, :, 0:HD],
                                          den[:, qt].rearrange("p (g j) -> p g j", g=KV).unsqueeze(3)
                                          .broadcast_to([P, KV, GROUP, HD]), ALU.mult).then_inc(sem["head_out"], 1)

                copy_turned(0, 0)
                copy_turned(1, 1)
                copy_turned(2, 0)
                seq_out(0)
                with dve.Fori(1, 3) as i:
                    copy_turned(2 * i + 1, 1)
                    seq_out(2 * i - 1)
                    copy_turned(2 * i + 2, 0)
                    seq_out(2 * i)
                copy_turned(SEQS - 1, 1)
                seq_out(SEQS - 3)
                seq_out(SEQS - 2)
                seq_out(SEQS - 1)
                for k in range(4):
                    rows = slice(4 * k, 4 * k + 4)
                    dve.wait_ge(sem["o_proj"], 4 * l + k + 1)
                    dve.tensor_tensor(acc[:, rows], src[:, rows], ps[:, 4 + k].rearrange("p (t d) -> p t d", d=D), ALU.add) \
                        .then_inc(sem["resid"], 1)
            dve.wait_ge(sem["resid"], 8)
            dve.tensor_tensor(x_sb[:], x_sb[:], acc[:], ALU.add).then_inc(sem["x1_ready"], 1)

        @block.tensor
        def _(pe):
            def side_free(ev, k):
                after(pe, "side_free", SIDE[ev, k])

            pe.wait_ge(sem["consts_loaded"], 48)
            for use, (src, bank) in enumerate(((xn, 0), (xm, 4))):
                pe.wait_ge(sem["normed"], use + 1)
                for k in range(4):
                    for t in range(4):
                        last = pe.transpose(ps[:, bank + k, t * P:(t + 1) * P], src[:, 4 * k + t], ident[:])
                    last.then_inc(sem["turned"], 1)

            def proj(ev):
                _, g, s = ev
                dr = g // PAIRS
                toks = slice((g % PAIRS) * COLS, (g % PAIRS + 1) * COLS)
                if s < 2:
                    if ev == ("proj", 0, 0):
                        pe.wait_ge(sem["mamba_weights_loaded"], 64)
                        pe.wait_ge(sem["turned_copied"], 8)
                    for half in range(HALVES):
                        side_free(ev, half)
                        c = s * INNER + half * P
                        pe.matmul(side, w_in[:, dr, c:c + P], xmT[:, toks], start=True, stop=True) \
                            .then_inc(sem["side_ready"], 1)
                elif s == 2:
                    side_free(ev, 0)
                    pe.wait_ge(sem["u_ready"], HALVES * (g + 1))
                    for half in range(HALVES):
                        last = pe.matmul(ps[0:XROWS, SIDE_BANK], w_x[:, dr, half], u_s[:, g % 2, half],
                                         start=(half == 0), stop=(half == HALVES - 1))
                    last.then_inc(sem["side_ready"], 1)
                else:
                    for half in range(HALVES):
                        side_free(ev, half)
                        pe.wait_ge(sem["dtr_ready"], g + 1)
                        pe.matmul(side, w_dt[DT_ROW:DT_ROW + RANK, dr, half * P:(half + 1) * P],
                                  dtr[DT_ROW:DT_ROW + RANK], start=True, stop=True).then_inc(sem["side_ready"], 1)

            def add_y(g, i, s):
                N = g * STATES + i * 2 + s
                for half in range(HALVES):
                    after(pe, "hc_ready", N * 2 + half + 1)
                    pe.matmul(ps[:, Y_BANK + half], ident[:], hc[:, 2 * s + half], start=False, stop=True,
                              skip_group_check=True).then_inc(sem["y_added"], 1)

            def body(g, i, first):
                for s in range(2):
                    N = g * STATES + i * 2 + s
                    after(pe, "b_copied", N)
                    pe.matmul(ps[:, B_BANK], spread[:, ds(i * 2 + s, 1)].broadcast_to([96, P]), bc[:, g % 2],
                              start=True, stop=True).then_inc(sem["b_spread"], 1)
                for s in range(2):
                    N = g * STATES + i * 2 + s
                    after(pe, "hc_ready", 2 * N - 2)
                    pe.matmul(ps[:, C_BANK + s], spread[:, ds(i * 2 + s + STATES, 1)].broadcast_to([96, P]),
                              bc[:, g % 2], start=True, stop=True).then_inc(sem["c_spread"], 1)
                    if not first:
                        add_y(g, i - 1, s)

            def start_y(g):
                for half in range(HALVES):
                    after(pe, "gated", HALVES * g)
                    pe.matmul(ps[:, Y_BANK + half], diagD[:, g // PAIRS, half], u_s[:, g % 2, half],
                              start=True, stop=True, skip_group_check=True)

            def finish(ev):
                g = ev[1]
                side_free(ev, 0)
                pe.wait_ge(sem["gated"], HALVES * (g + 1))
                for t in range(4):
                    for half in range(HALVES):
                        last = pe.matmul(side[:, t * D:(t + 1) * D], yg[:, half, t * P:(t + 1) * P],
                                         w_out[:, g // PAIRS, half], start=(half == 0), stop=(half == HALVES - 1))
                last.then_inc(sem["side_ready"], 1)

            def gate(ev):
                side_free(ev, 0)
                pe.wait_ge(sem["pool_mean"], 1)
                pe.wait_ge(sem["gate_weights_loaded"], 96)
                pe.matmul(side[0:SEQS, 0:EXPERTS], pooled[:], w_r[:], start=True, stop=True).then_inc(sem["side_ready"], 1)
                side_free(ev, 1)
                pe.wait_ge(sem["gate_step"], 14)
                pe.transpose(side[0:EXPERTS, 0:SEQS], small[:, 14], ident[0:SEQS, 0:SEQS]).then_inc(sem["side_ready"], 1)
                side_free(ev, 2)
                pe.wait_ge(sem["halfconst"], 2)
                pe.matmul(side[:, 0:2 * SEQS], ones8[:], wdiag[:].rearrange("p b k -> p (b k)"), start=True, stop=True) \
                    .then_inc(sem["side_ready"], 1)

            def expert(ev):
                p = ev[1]
                b, k = p // 2, p % 2
                x = xnT[:, b * SEQ:(b + 1) * SEQ]
                pe.wait_ge(sem[f"expert_loaded{k}"], 16 * (b + 1))
                for c in range(CHUNKS):
                    if c % 2 == 0:
                        side_free(ev, c // 2)
                    last = pe.matmul(side[:, (c % 2) * SEQ:(c % 2 + 1) * SEQ], wbuf[:, k, c * P:(c + 1) * P], x,
                                     start=True, stop=True)
                    if c % 2:
                        last.then_inc(sem["side_ready"], 1)
                side_free(ev, 2)
                for t in range(2):
                    for c in range(CHUNKS):
                        last = pe.matmul(side[:, t * D:(t + 1) * D], hT[:, k, c, t * P:(t + 1) * P],
                                         wbuf[:, k, HIDDEN + CHUNKS + c * D:HIDDEN + CHUNKS + (c + 1) * D],
                                         start=(c == 0), stop=(c == CHUNKS - 1))
                if k == 0:
                    last = pe.matmul(side[:, 2 * D:3 * D], cwT[:, b:b + 1].broadcast_to([EXPERTS, P]), b2[:],
                                     start=True, stop=True)
                last.then_inc(sem["side_ready"], 1)

            for ev in ORDER:
                if ev[0] == "proj":
                    proj(ev)
                elif ev[0] == "body":
                    g, i = ev[1:]
                    if i == 0:
                        if g == 0:
                            pe.wait_ge(sem["spread_ready"], 2)
                            pe.wait_ge(sem["diag_ready"], 4)
                        pe.wait_ge(sem["bc_ready"], g + 1)
                    body(g, i, i == 0)
                elif ev[0] == "loop":
                    if ev[2] == 1:
                        start_y(ev[1])
                    with pe.Fori(ev[2], ev[3]) as i:
                        body(ev[1], i, False)
                elif ev[0] == "tail":
                    for s in range(2):
                        add_y(ev[1], BODIES - 1, s)
                elif ev[0] == "finish":
                    finish(ev)
                elif ev[0] == "gate":
                    gate(ev)
                elif ev[0] == "expert":
                    expert(ev)

            pe.wait_ge(sem["normed"], 4)
            for k in range(4):
                for t in range(4):
                    last = pe.transpose(ps[:, k, t * P:(t + 1) * P], xn[:, 4 * k + t], ident[:])
                last.then_inc(sem["turned"], 1)
            pe.wait_ge(sem["l1_weights_loaded"], 12 * 16)
            for t in range(TILES):
                if t % 4 == 0:
                    pe.wait_ge(sem["turned_copied"], 9 + t // 4)
                last = pe.matmul(ps[:, 4, t * EXPERTS:(t + 1) * EXPERTS], xnT[:, t * P:(t + 1) * P], w_g[:],
                                 start=True, stop=True)
            last.then_inc(sem["r_pe"], 1)
            pe.wait_ge(sem["r_dve"], R_BASE + 7)
            pe.matmul(ps[:, 5, 0:64], tri[:, 0], mask16[:, 0::2], start=True, stop=True)
            pe.matmul(ps[:, 5, 64:128], tri[:, 1], mask16[:, 0::2], start=True, stop=False)
            pe.matmul(ps[:, 5, 64:128], tri[:, 0], mask16[:, 1::2], start=False, stop=True).then_inc(sem["r_pe"], 1)
            pe.wait_ge(sem["r_dve"], R_BASE + 13)
            for k in range(4):
                for b in (2 * k, 2 * k + 1):
                    for two in range(2):
                        last = pe.matmul(ps[:, k, (b % 2) * SEQ:(b % 2 + 1) * SEQ], xn[:, 2 * b + two],
                                         slot[:, 2 * b + two].rearrange("p e c -> p (e c)"), start=(two == 0), stop=(two == 1))
                last.then_inc(sem["slots_spread"], 1)
            for k in range(8):
                after(pe, "d_turned", k - 3)
                for t in range(4):
                    last = pe.transpose(ps[:, 4 + k % 4, t * P:(t + 1) * P],
                                        slot[:, 4 * (k % 4) + t, 4 * (k // 4):4 * (k // 4) + 4].rearrange("p e c -> p (e c)"),
                                        ident[:])
                last.then_inc(sem["d_turn"], 1)

            def up(e):
                pe.wait_ge(sem["expert_loaded%d" % (e % 2)], 16 * (SEQS + e // 2 + 1))
                after(pe, "e_gelu", CHUNKS * (e - 1))
                for c in range(CHUNKS):
                    last = pe.matmul(ps[:, 2 * (e % 2) + c // 2, (c % 2) * SEQ:(c % 2 + 1) * SEQ],
                                     wbuf1[:, e % 2, c * P:(c + 1) * P], xe[:, :, e],
                                     start=True, stop=True)
                    if c % 2:
                        last.then_inc(sem["e_up"], 1)

            def down(e):
                pe.wait_ge(sem["e_gelu"], CHUNKS * (e + 1))
                after(pe, "e_out", e - 1)
                for c in range(CHUNKS):
                    last = pe.matmul(ps[:, 4 + e % 2, 0:SEQ], wbuf1[:, e % 2, HIDDEN + c * D:HIDDEN + (c + 1) * D],
                                     hT1[:, e % 2, c], start=(c == 0), stop=(c == CHUNKS - 1))
                last.then_inc(sem["e_down"], 1)

            pe.wait_ge(sem["slots_copied"], 4)
            pe.wait_ge(sem["d_turned"], 8)
            up(0)
            for e in range(1, EXPERTS):
                up(e)
                down(e - 1)
            down(EXPERTS - 1)
            pe.wait_ge(sem["e_out"], EXPERTS)
            for k in range(4):
                for n, (b, s) in enumerate(((2 * k, 0), (2 * k, 1), (2 * k + 1, 0), (2 * k + 1, 1))):
                    last = pe.transpose(ps[:, k, n * P:(n + 1) * P], xe[:, b, 4 * s:4 * s + 4].rearrange("p e c -> p (e c)"), ident[:])
                last.then_inc(sem["e_turn"], 1)
            for k in range(4):
                pe.wait_ge(sem["e_turned"], k + 1)
                for t in range(4):
                    for s in range(2):
                        last = pe.matmul(ps[:, 4 + k, t * D:(t + 1) * D], slotT[:, s, 4 * k + t], eo[:, 2 * k + t // 2, s],
                                         start=(s == 0), stop=(s == 1))
                last.then_inc(sem["e_comb"], 1)

            for l in range(2):
                pe.wait_ge(sem["rms_done"], l + 1)
                for k in range(4):
                    for t in range(4):
                        last = pe.transpose(ps[:, k, t * P:(t + 1) * P], xm[:, 4 * k + t], ident[:])
                    last.then_inc(sem["turned"], 1)
                if l == 0:
                    pe.wait_ge(sem["e_added"], 4)
                    for k in range(4):
                        pe.wait_ge(sem["turned_copied"], 12 + k + 1)
                        pe.matmul(ps[0:LAT, 4 + k], w_kvd[:], xmT[:, k * 512:(k + 1) * 512], start=True, stop=True) \
                            .then_inc(sem["lat_ready"], 1)
                for t in range(TILES):
                    if t % 4 == 0:
                        pe.wait_ge(sem["turned_copied"], 12 + 4 * l + t // 4 + 1)
                    pe.matmul(ps[:, t // 4, (t % 4) * D:(t % 4 + 1) * D], xmT[:, t * P:(t + 1) * P], w_q[:, l],
                              start=True, stop=True)
                for t in range(TILES):
                    if l == 0 and t == 0:
                        pe.wait_ge(sem["lat_copied"], 4)
                    c = 2 * KV * HD
                    rows, w = (latT, w_kvu) if l == 0 else (xmT, w_kv)
                    last = pe.matmul(ps[:, 4 + t // 8, (t % 8) * c:(t % 8 + 1) * c], rows[:, t * P:(t + 1) * P], w[:],
                                     start=True, stop=True)
                last.then_inc(sem["qkv_ready"], 1)
                pe.wait_ge(sem["qk_split"], 2 * l + 2)

                def turn(b):
                    for k in range(3):
                        after(pe, "turn_copied", 3 * SEQS * l + 3 * b + k)
                        if k < 2:
                            for j in range(GROUP):
                                heads_j = qs[:, ds((2 * b + k) * HEADS + j * KV, KV)].rearrange("p g i d -> p (g i d)")
                                last = pe.matmul(ps[:, 4, j * P:(j + 1) * P], heads_j, ident16[:], start=True, stop=True)
                        else:
                            for t in range(2):
                                last = pe.matmul(ps[:, 4, t * P:(t + 1) * P],
                                                 ks[:, ds((2 * b + t) * KV, KV)].rearrange("p g i d -> p (g i d)"),
                                                 ident16[:], start=True, stop=True)
                        last.then_inc(sem["turn_q"], 1)

                def scores(b, r, kv):
                    if kv == 0:
                        after(pe, "turn_copied", 3 * (SEQS * l + b) + 3)
                    g = slice(32 * kv, 32 * kv + 32)
                    for n, (kt, qt) in enumerate(((0, 0), (0, 1), (1, 1))):
                        unit = 3 * (KV * (SEQS * l + b) + kv) + n
                        bank = (3 * kv + n) % 4
                        after(pe, "probs_ready", unit - 3)
                        if l and n == 1:
                            near = slice(P - WINDOW, P)
                            part = ps[near, bank, 0:GROUP * WINDOW]
                            pe.matmul(part, ident16[:, near],
                                      masks[:, 2, 0:WINDOW].unsqueeze(1).broadcast_to([P, GROUP, WINDOW]), start=True, stop=False)
                            last = pe.matmul(part, kT[g, r, near], qT[g, r, :, P:P + WINDOW], start=False, stop=True)
                        else:
                            if n != 1:
                                pe.matmul(ps[:, bank], ident16[:], masks[:, l].unsqueeze(1).broadcast_to([P, GROUP, P]),
                                          start=True, stop=False)
                            last = pe.matmul(ps[:, bank], kT[g, r, kt * P:(kt + 1) * P], qT[g, r, :, qt * P:(qt + 1) * P],
                                             start=(n == 1), stop=True)
                        last.then_inc(sem["scores_ready"], 1)

                def average(b, r, kv):
                    step = KV * (SEQS * l + b) + kv
                    if kv == 0:
                        after(pe, "v_placed", SEQS * l + b + 1)
                        after(pe, "av_copied", 2 * (SEQS * l + b))
                    g = slice(32 * kv, 32 * kv + 32)

                    for n, qt, kt in ((0, 0, 0), (2, 1, 1), (1, 1, 0)):
                        if n != 1:
                            after(pe, "probs_ready", 3 * step + n + 1)
                        p = probs[:, 3 * (kv % 2) + n]
                        if l and n == 1:
                            near = slice(P - WINDOW, P)
                            last = pe.matmul(ps[g, 6].rearrange("p (j q) -> p j q", j=GROUP)[:, :, 0:WINDOW],
                                             v_ring[near, r, kt, kv], p[near, 0:GROUP * WINDOW], start=False, stop=True)
                        else:
                            last = pe.matmul(ps[g, 5 + qt], v_ring[:, r, kt, kv], p, start=(n != 1), stop=(n != 2))
                    last.then_inc(sem["av_done"], 1)

                def turn_av(b):
                    for qt in range(2):
                        n = 2 * (SEQS * l + b) + qt
                        after(pe, "av_copied", n + 1)
                        after(pe, "head_out", n)
                        for j in range(GROUP):
                            last = pe.transpose(ps[:, 7, j * P:(j + 1) * P], avT[:, qt, j * P:(j + 1) * P], ident[:])
                        last.then_inc(sem["av_turned"], 1)

                def sequence(b, r, first=False, turn_next=True):
                    for kv in range(KV):
                        scores(b, r, kv)
                        if kv == 1 and turn_next:
                            turn(b + 1)
                        if kv:
                            average(b, r, kv - 1)
                        elif not first:
                            average(b - 1, 1 - r, KV - 1)
                        if kv == 2 and not first:
                            turn_av(b - 1)

                turn(0)
                sequence(0, 0, first=True)
                sequence(1, 1)
                with pe.Fori(1, 3) as i:
                    sequence(2 * i, 0)
                    sequence(2 * i + 1, 1)
                sequence(6, 0)
                sequence(7, 1, turn_next=False)
                average(SEQS - 1, 1, KV - 1)
                turn_av(SEQS - 1)

                for k in range(4):
                    pe.wait_ge(sem["head_out"], 2 * SEQS * (l + 1))
                    for t in range(4):
                        last = pe.transpose(ps[:, k, t * P:(t + 1) * P], heads[:, 4 * k + t], ident[:])
                    last.then_inc(sem["o_turn"], 1)
                for k in range(4):
                    pe.wait_ge(sem["o_copied"], 4 * l + k + 1)
                    for t in range(4):
                        last = pe.matmul(ps[:, 4 + k, t * D:(t + 1) * D], xmT[:, (4 * k + t) * P:(4 * k + t + 1) * P],
                                         w_o[:, l], start=True, stop=True)
                    last.then_inc(sem["o_proj"], 1)


def layouts(v):
    import numpy as np

    def mamba(p):
        w = {k: np.asarray(v[f"L0_attn_{p}_{k}"]) for k in ("Win", "convw", "convb", "Wx", "Wdt", "bdt", "Alog", "D", "Wout")}
        per = np.concatenate([w["convw"][:, 0], w["convb"][:, None], w["bdt"][:, None], w["D"][:, None], w["Alog"]], 1)
        bc = w["Wx"][RANK:].T
        return {
            "par": per.reshape(HALVES, P, NPAR).transpose(1, 0, 2),
            "w_in": w["Win"].T,
            "w_x": np.concatenate([bc, bc, bc, w["Wx"][:RANK].T], 1).reshape(HALVES, P, XROWS).transpose(1, 0, 2),
            "w_dt": w["Wdt"].T,
            "w_out": w["Wout"].T.reshape(HALVES, P, D).transpose(1, 0, 2),
        }

    f, b = mamba("f"), mamba("b")
    a = {k: np.stack([f[k], b[k]], 1) for k in f}
    v = {k: np.asarray(x) for k, x in v.items()}
    a["x"] = v["L0_attn_x"].reshape(TOK, D)
    a["ident"] = np.eye(P, dtype=np.float32)
    a["cols"] = np.stack([v["L0_attn_norm_g"], v["L0_attn_norm_b"], v["L1_attn_norm1_w"], v["L1_attn_norm2_w"]], 1)
    a["w_r"] = v["L0_ffn_Wr"]
    a["br"] = v["L0_ffn_br"]
    a["b2"] = v["L0_ffn_b2"]
    a["iota8"] = np.arange(EXPERTS, dtype=np.float32)
    a["gamma"], a["beta"] = v["L0_ffn_gamma"], v["L0_ffn_beta"]
    down = lambda w: w.reshape(EXPERTS, CHUNKS, P, D).transpose(0, 2, 1, 3).reshape(EXPERTS, P, HIDDEN)
    b1 = v["L0_ffn_b1"].reshape(EXPERTS, CHUNKS, P).transpose(0, 2, 1)
    a["pack0"] = np.concatenate([v["L0_ffn_W1"], b1, down(v["L0_ffn_W2"])], 2)
    a["pack1"] = np.concatenate([v["L1_ffn_W1"], down(v["L1_ffn_W2"])], 2)
    a["w_g"] = v["L1_ffn_Wg"]
    a["w_q"] = np.stack([v["L1_attn_g_wq"], v["L1_attn_l_wq"]], 1).reshape(P, 2, KV, GROUP, HD).swapaxes(2, 3).reshape(P, 2, D)
    a["w_o"] = np.stack([v["L1_attn_g_wo"], v["L1_attn_l_wo"]], 1)
    a["w_kvd"] = v["L1_attn_g_kv_down"]
    a["w_kvu"] = np.concatenate([v["L1_attn_g_k_up"], v["L1_attn_g_v_up"]], 1)
    a["w_kv"] = np.concatenate([v["L1_attn_l_wk"], v["L1_attn_l_wv"]], 1)
    a.update(constants())
    return a


def constants():
    import numpy as np

    key, query = np.arange(P)[:, None], np.arange(P)[None, :]
    hide = lambda seen: np.where(seen, 0.0, MASKED)
    masks = [hide(query >= key), hide((query >= key) & (query - key < WINDOW)), hide(query + P - key < WINDOW)]
    ropes = []
    for base in (1000000.0, 10000.0):
        inv = (1.0 / np.float32(base) ** (np.arange(0, HD, 2, dtype=np.float32) / np.float32(HD))).astype(np.float32)
        angle = np.arange(SEQ, dtype=np.float32)[:, None] * inv[None, :]
        cos = np.repeat(np.cos(angle), 2, 1)
        sin = np.stack([-np.sin(angle), np.sin(angle)], 2).reshape(SEQ, HD)
        ropes.append([np.tile(t, (1, HEADS)).reshape(2, P, D).transpose(1, 0, 2).reshape(P, 2 * D) for t in (cos, sin)])
    tri = np.stack([key <= query, np.ones((P, P))], 1)
    return {
        "masks": np.stack(masks, 1).astype(np.float16),
        "ident16": np.eye(P, dtype=np.float16),
        "rope": np.array(ropes).transpose(2, 0, 1, 3).astype(np.float32),
        "tri": tri.astype(np.float16),
        "iota32": np.arange(1, CAP + 1, dtype=np.float32),
        "iotar": np.arange(EXPERTS, 0, -1, dtype=np.float32),
    }


def kernel(**inputs):
    import numpy as _np
    import concourse.bacc as _bacc
    from concourse import mybir as _mybir
    from concourse.bass_utils import run_bass_kernel_spmd as _run

    nc = _bacc.Bacc("TRN2", target_bir_lowering=False, num_devices=1)
    arrays, args = {}, {}
    for name, a in layouts(inputs).items():
        a = _np.ascontiguousarray(a)
        arrays[f"in_{name}"] = a
        args[name] = nc.dram_tensor(f"in_{name}", a.shape, _mybir.dt.from_np(a.dtype), kind="ExternalInput").ap()
    out = nc.dram_tensor("out", (TOK, D), F32, kind="ExternalOutput").ap()
    build(nc, args, out)
    r = _run(nc, [arrays], core_ids=[0])
    return r.results[0]["out"].reshape(SEQS, SEQ, D)
```

```python
from contextlib import ExitStack

import concourse.bass as bass
from concourse import mybir
from concourse.bass import ds

F32 = mybir.dt.float32
BF16 = mybir.dt.bfloat16
F16 = mybir.dt.float16
U32 = mybir.dt.uint32
ALU = mybir.AluOpType
ACT = mybir.ActivationFunctionType
AX = mybir.AxisListType

P = 128
D = 128
SEQS, SEQ = 8, 256
TOK = SEQS * SEQ
TILES = TOK // P
INNER = 256
HALVES = INNER // P
STATES = 16
RANK = 8
TAPS = 4
LN_EPS = 1e-5
RMS_EPS = 1e-6
EXPERTS = 8
HIDDEN = 512
CHUNKS = HIDDEN // P
HEADS, KV, HD = 16, 4, 8
GROUP = HEADS // KV
LAT = 32
WINDOW = 32
VW = 32
CAP = SEQ // EXPERTS

COLS = 512
PAIRS = TOK // COLS
STEPS = 2 * PAIRS
ALL = STEPS * STATES
UNITS = 2 * HALVES
PAIRS0 = 2 * SEQS
RING = 4
NPAR = TAPS + 3 + STATES
XROWS = 3 * 2 * STATES + RANK
DT_ROW = 3 * 2 * STATES
PACK = HIDDEN + CHUNKS + HIDDEN
PACK1 = 2 * HIDDEN
R_BASE = 3
MASKED = -30000.0

SIGNALS = [
    "x_loaded", "consts_loaded", "mamba_weights_loaded", "gate_weights_loaded", "l1_weights_loaded",
    "expert_loaded0", "expert_loaded1", "expert_loaded2", "expert_loaded3", "out_stored",
    "sum_done", "centred", "squared", "var_done", "pow_done", "normed", "halfconst",
    "spread_ready", "a_ready", "a_exp", "diag_ready", "zero_cols",
    "turned", "turned_copied",
    "side_ready", "side_free",
    "u_copied", "conv_tap", "u_ready", "z_copied", "z_ready", "hi_ready", "mid_ready",
    "bc_part", "bc_ready", "dtr_ready", "dt_abs", "dt_exp", "dt_ln", "dt_ready", "dtu_ready",
    "b_spread", "b_copied", "c_spread", "decay_ready", "drive_ready", "scan_done", "hc_ready", "y_added",
    "gated", "acc_added",
    "pool_mean", "gate_step", "gate_act", "index_ready", "cw_ready",
    "bias_ready", "moe_bias", "e0_up", "e0_gelu", "e0_down", "e0_added", "ln0_step", "ln0_var", "ln0_pow", "ln0_added",
    "x1_ready", "r_pe", "r_dve", "r_act", "slots_spread", "slots_copied", "e_up", "e_gelu", "e_down",
    "e_out", "e_turn", "e_turned", "e_comb", "e_added", "d_turn", "d_turned",
    "at_copied", "lat_ready", "lat_copied", "qkv_ready", "rope_a", "rope_b", "roped", "v_ready",
    "qk_sq", "qk_sum", "qk_var", "qk_sqrt", "qk_inv", "qk_normed", "qk_hi", "qk_split",
    "turn_q", "turn_copied", "scores_ready", "probs_ready", "av_done", "den_done", "head_out",
    "o_turn", "o_copied", "o_proj", "resid", "ones_ready", "v_placed", "av_copied", "av_turned", "rms_done",
]


def timeline():
    order = [("gate", 0), ("u", 0, 0), ("u", 0, 1), ("z", 0, 0), ("z", 0, 1), ("gate", 1), ("gate", 2),
             ("x", 0), ("mid", 0), ("dt", 0, 0), ("dt", 0, 1), ("experts",)]
    for g in range(STEPS):
        slots = {}
        if g:
            slots[4] = ("finish", g - 1)
        if g + 1 < STEPS:
            slots.update({0: ("u", g + 1, 0), 2: ("u", g + 1, 1), 5: ("z", g + 1, 0), 6: ("z", g + 1, 1), 8: ("x", g + 1),
                          9: ("mid", g + 1), 10: ("dt", g + 1, 0), 12: ("dt", g + 1, 1)})
        for j in range(STATES):
            if j in slots:
                order.append(slots[j])
            order.append(("state", g * STATES + j))
    order.append(("end",))
    order.append(("finish", STEPS - 1))
    return order


ORDER = timeline()


def swapped(order):
    order = list(order)
    k = 0
    while k + 1 < len(order):
        if order[k][0] != "state" and order[k + 1][0] == "state":
            order[k], order[k + 1] = order[k + 1], order[k]
            k += 1
        k += 1
    return order


READERS = swapped(ORDER)
SIDE = {ev: n for n, ev in enumerate(ev for ev in ORDER if ev[0] in ("gate", "u", "z", "x", "dt", "finish"))}


def build(nc, a, out):
    with ExitStack() as ctx:
        def sb(name, shape, dt=F32):
            return ctx.enter_context(nc.sbuf_tensor(name, shape, dt))

        sem = {name: ctx.enter_context(nc.semaphore(name)) for name in SIGNALS}

        ps = ctx.enter_context(nc.psum_tensor("ps", [P, 8, 512], F32))

        x_sb = sb("x_sb", [P, TILES, D])
        xn = sb("xn", [P, TILES, D])
        xm = sb("xm", [P, TILES, D])
        sq = sb("sq", [P, TILES, D])
        xnT = sb("xnT", [P, TOK])
        xmT = sb("xmT", [P, TOK])
        acc = sb("acc", [P, TILES, D])
        moe = sb("moe", [P, TILES, D])
        stat = sb("stat", [P, 4, TILES])
        halfc = sb("halfc", [P, TILES])
        ident = sb("ident", [P, P])
        cols = sb("cols", [P, 4])
        par = sb("par", [P, 2, HALVES, NPAR])
        diagD = sb("diagD", [P, 2, HALVES, P])
        spread = sb("spread", [96, 2 * STATES], BF16)
        spreadf = sb("spreadf", [96, 2 * STATES])
        negA = sb("negA", [P, 2, HALVES, STATES])

        l0 = ExitStack()

        def sb(name, shape, dt=F32):
            return l0.enter_context(nc.sbuf_tensor(name, shape, dt))

        w_in = sb("w_in", [P, 2, 2 * INNER])
        w_x = sb("w_x", [P, 2, HALVES, XROWS])
        w_dt = sb("w_dt", [P, 2, INNER])
        u_raw = sb("u_raw", [P, HALVES, COLS])
        conv = sb("conv", [P, HALVES, COLS])
        w_out = sb("w_out", [P, 2, HALVES, D])

        u_s = sb("u_s", [P, 2, HALVES, COLS])
        z_s = sb("z_s", [P, 2, HALVES, COLS])
        dt = sb("dt", [P, 2, HALVES, COLS])
        dtu = sb("dtu", [P, 2, HALVES, COLS])
        dt_a = sb("dt_a", [P, COLS])
        dt_b = sb("dt_b", [P, COLS])
        dtr = sb("dtr", [P, COLS])
        bc = sb("bc", [96, 2, COLS], BF16)
        bc_rest = sb("bc_rest", [96, COLS])
        bc_mid = sb("bc_mid", [96, COLS], BF16)
        b_sb = sb("b_sb", [P, 2, COLS])

        w_r = sb("w_r", [P, EXPERTS])
        br = sb("br", [SEQS, EXPERTS])
        b2 = sb("b2", [EXPERTS, D])
        gb = sb("gb", [P, 2, D])
        small = sb("small", [SEQS, 16, EXPERTS])
        iota8 = sb("iota8", [SEQS, EXPERTS])
        pooled = sb("pooled", [P, SEQS])
        index = sb("index", [SEQS, EXPERTS], U32)
        ones8 = sb("ones8", [SEQS, P])
        cwT = sb("cwT", [EXPERTS, SEQS])
        wdiag = sb("wdiag", [SEQS, SEQS, 2])
        cw = sb("cw", [P, 2 * SEQS])
        seqstat = sb("seqstat", [P, 2, 4, 2])
        e0 = ExitStack()
        wbuf = e0.enter_context(nc.sbuf_tensor("wbuf", [P, RING, PACK], F32))
        hT = e0.enter_context(nc.sbuf_tensor("hT", [P, 2, CHUNKS, SEQ], F32))
        e0.close()
        drive = sb("drive", [P, UNITS, COLS])
        h = sb("h", [P, UNITS, COLS])
        hc = sb("hc", [P, UNITS, COLS])
        yg = sb("yg", [P, HALVES, COLS])

        l0.close()

        def sb(name, shape, dt=F32):
            return ctx.enter_context(nc.sbuf_tensor(name, shape, dt))

        rope = sb("rope", [P, 2, 2, 2 * D])
        masks = sb("masks", [P, 3, P], F16)
        ident16 = sb("ident16", [P, P], F16)
        w_q = sb("w_q", [P, 2, D])
        w_kvd = sb("w_kvd", [P, LAT])
        w_kvu = sb("w_kvu", [LAT, 2 * KV * HD])
        w_kv = sb("w_kv", [P, 2 * KV * HD])
        w_o = sb("w_o", [P, 2, D])
        w_g = sb("w_g", [P, EXPERTS])
        tri = sb("tri", [P, 2, P], F16)
        iota32 = sb("iota32", [P, CAP])
        iotar = sb("iotar", [P, EXPERTS])
        qk = sb("qk", [P, TILES * (HEADS + KV), HD])
        rot = sb("rot", [P, 2, TILES * (HEADS + KV) * HD])
        norm = sb("norm", [P, 3, TILES * (HEADS + KV)])
        qs = sb("qs", [P, TILES * HEADS, 4, HD], F16)
        ks = sb("ks", [P, TILES * KV, 4, HD], F16)
        qT = sb("qT", [P, 2, GROUP, SEQ], F16)
        kT = sb("kT", [P, 2, SEQ], F16)
        probs = sb("probs", [P, 6, COLS])
        v_sb = sb("v_sb", [P, TILES, KV, HD])
        v_ring = sb("v_ring", [P, 2, 2, KV, VW])
        avT = sb("avT", [P, 2, COLS])
        den = sb("den", [P, 2, HEADS])
        latT = sb("latT", [LAT, TOK])
        route = sb("route", [P, 6, TILES, EXPERTS])
        rstat = sb("rstat", [P, 4, TILES])
        mask16 = sb("mask16", [P, TILES, EXPERTS], F16)
        slot = sb("slot", [P, TILES, EXPERTS, CAP])
        slotT = sb("slotT", [P, 2, TILES, P])
        xe = sb("xe", [P, SEQS, EXPERTS, CAP])
        eo = slot[:].rearrange("p t e c -> p (t e c)")[:, 0:SEQS * 2 * D].rearrange("p (b s d) -> p b s d", b=SEQS, s=2)
        wbuf1 = rot[:, 0, 0:2 * PACK1].rearrange("p (r n) -> p r n", r=2)
        hT1 = rot[:, 1, 0:2 * CHUNKS * SEQ].rearrange("p (r c n) -> p r c n", r=2, c=CHUNKS)
        heads = moe

        B_BANK, C_BANK, DECAY, Y_BANK, SIDE_BANK = 0, 1, 3, 5, 7
        side = ps[:, SIDE_BANK, :]

        block = ctx.enter_context(nc.Block())

        def after(eng, name, count):
            if not (isinstance(count, int) and count <= 0):
                eng.wait_ge(sem[name], count)

        def seqs(t):
            return t.rearrange("p (b t) -> p b t", t=SEQ)

        @block.sync
        def _(sp):
            sp.dma_start(x_sb[:], a["x"].rearrange("(t p) d -> p t d", p=P)).then_inc(sem["x_loaded"], 16)
            sp.dma_start(ident[:], a["ident"]).then_inc(sem["consts_loaded"], 16)
            sp.dma_start(cols[:], a["cols"]).then_inc(sem["consts_loaded"], 16)
            sp.dma_start(par[:], a["par"]).then_inc(sem["consts_loaded"], 16)
            sp.dma_start(w_in[:], a["w_in"]).then_inc(sem["mamba_weights_loaded"], 16)
            sp.dma_start(w_x[:], a["w_x"]).then_inc(sem["mamba_weights_loaded"], 16)
            sp.dma_start(w_dt[DT_ROW:DT_ROW + RANK], a["w_dt"]).then_inc(sem["mamba_weights_loaded"], 16)
            sp.dma_start(w_out[:], a["w_out"]).then_inc(sem["mamba_weights_loaded"], 16)
            sp.dma_start(w_r[:], a["w_r"]).then_inc(sem["gate_weights_loaded"], 16)
            sp.dma_start(br[:], a["br"].partition_broadcast(SEQS)).then_inc(sem["gate_weights_loaded"], 16)
            sp.dma_start(b2[:], a["b2"]).then_inc(sem["gate_weights_loaded"], 16)
            sp.dma_start(iota8[:], a["iota8"].partition_broadcast(SEQS)).then_inc(sem["gate_weights_loaded"], 16)
            sp.dma_start(gb[:, 0], a["gamma"].partition_broadcast(P)).then_inc(sem["gate_weights_loaded"], 16)
            sp.dma_start(gb[:, 1], a["beta"].partition_broadcast(P)).then_inc(sem["gate_weights_loaded"], 16)
            sp.wait_ge(sem["index_ready"], 1)
            for p in range(PAIRS0):
                after(sp, "e0_down", p - RING + 1)
                e = sp.value_load(index[p // 2:p // 2 + 1, p % 2:p % 2 + 1], min_val=0, max_val=EXPERTS - 1)
                sp.dma_start(wbuf[:, p % RING], a["pack0"][ds(e, 1)].rearrange("e p n -> p (e n)")) \
                    .then_inc(sem[f"expert_loaded{p % RING}"], 16)
            sp.wait_ge(sem["side_free"], SIDE["dt", STEPS - 1, 1] + 1)
            for dst, name in ((rope, "rope"), (masks, "masks"), (ident16, "ident16"), (w_q, "w_q"), (w_kvd, "w_kvd"),
                              (w_kvu, "w_kvu"), (w_kv, "w_kv"), (w_o, "w_o"), (w_g, "w_g"), (tri, "tri")):
                sp.dma_start(dst[:], a[name]).then_inc(sem["l1_weights_loaded"], 16)
            sp.dma_start(iota32[:], a["iota32"].partition_broadcast(P)).then_inc(sem["l1_weights_loaded"], 16)
            sp.dma_start(iotar[:], a["iotar"].partition_broadcast(P)).then_inc(sem["l1_weights_loaded"], 16)
            sp.wait_ge(sem["y_added"], ALL * HALVES)
            sp.wait_ge(sem["side_free"], SIDE["finish", STEPS - 1] + 1)
            for e in range(EXPERTS):
                after(sp, "e_down", e - 1)
                sp.dma_start(wbuf1[:, e % 2], a["pack1"][e]).then_inc(sem["expert_loaded%d" % (e % 2)], 16)
            sp.wait_ge(sem["x1_ready"], 2)
            sp.dma_start(out.rearrange("(t p) d -> p t d", p=P), x_sb[:]).then_inc(sem["out_stored"], 16)
            sp.wait_ge(sem["out_stored"], 16)

        @block.gpsimd
        def _(pool):
            pool.memset(halfc[:], -0.5).then_inc(sem["halfconst"], 1)
            pool.memset(ones8[:], 1.0).then_inc(sem["halfconst"], 1)
            pool.wait_ge(sem["halfconst"], 2)

            def rstd(use):
                after(pool, "var_done", use + 1)
                pool.tensor_tensor(stat[:, 3], stat[:, 2], halfc[:], ALU.pow).then_inc(sem["pow_done"], 1)

            rstd(0)
            rstd(1)

            def drive_state(N):
                for half in range(HALVES):
                    after(pool, "b_copied", N + 1)
                    after(pool, "scan_done", 2 * N + half - UNITS + 1)
                    pool.tensor_tensor(drive[:, 2 * (N % 2) + half], dtu[:, N // STATES % 2, half], b_sb[:, N % 2], ALU.mult) \
                        .then_inc(sem["drive_ready"], 1)

            for ev in READERS:
                if ev[0] == "state":
                    N = ev[1]
                    if N == 0:
                        pool.wait_ge(sem["dtu_ready"], HALVES)
                        drive_state(0)
                    if N + 1 < ALL:
                        if (N + 1) % STATES == 0:
                            pool.wait_ge(sem["dtu_ready"], HALVES * ((N + 1) // STATES + 1))
                        drive_state(N + 1)
                elif ev[0] == "dt":
                    _, g, half = ev
                    n = HALVES * g + half
                    pool.wait_ge(sem["dt_ready"], n + 1)
                    pool.wait_ge(sem["u_ready"], g + 1)
                    after(pool, "drive_ready", STATES * HALVES * (g - 1))
                    pool.tensor_tensor(dtu[:, g % 2, half], dt[:, g % 2, half], u_s[:, g % 2, half], ALU.mult) \
                        .then_inc(sem["dtu_ready"], 1)
                elif ev[0] == "experts":
                    def seq_rstd(b, r):
                        pool.wait_ge(sem["ln0_var"], b + 1)
                        pool.tensor_tensor(seqstat[:, r, 3], seqstat[:, r, 2], halfc[:, 0:2], ALU.pow) \
                            .then_inc(sem["ln0_pow"], 1)

                    with pool.Fori(0, SEQS // 2) as i:
                        seq_rstd(2 * i, 0)
                        seq_rstd(2 * i + 1, 1)
            for use in range(2, 5):
                rstd(use)
                if use == 2:
                    pool.wait_ge(sem["normed"], 3)
                    pool.memset(v_ring[:], 0.0).then_inc(sem["ones_ready"], 1)
                    pool.wait_ge(sem["ones_ready"], 1)
                    pool.memset(v_ring[:, :, :, :, HD:HD + 1], 1.0).then_inc(sem["ones_ready"], 1)
                if use >= 3:
                    l = use - 3

                    def copy_v(b, r):
                        after(pool, "av_done", KV * (SEQS * l + b - 1))
                        pool.tensor_copy(v_ring[:, r, :, :, 0:HD], v_sb[:, ds(2 * b, 2)]).then_inc(sem["v_placed"], 1)

                    pool.wait_ge(sem["v_ready"], l + 1)
                    copy_v(0, 0)
                    copy_v(1, 1)
                    with pool.Fori(1, 4) as i:
                        copy_v(2 * i, 0)
                        copy_v(2 * i + 1, 1)

        @block.scalar
        def _(act):
            act.preload_act_table_set("natural_log_exp_and_others")
            act.wait_ge(sem["consts_loaded"], 48)
            act.activation(negA[:], par[:, :, :, TAPS + 3:], ACT.Exp).then_inc(sem["a_exp"], 1)
            for use in range(2):
                act.wait_ge(sem["centred"], use + 1)
                act.activation(sq[:], xm[:], ACT.Square).then_inc(sem["squared"], 1)

            for k in range(4):
                act.wait_ge(sem["turned"], k + 1)
                act.activation(xnT[:, k * 512:(k + 1) * 512], ps[:, k], ACT.Copy).then_inc(sem["turned_copied"], 1)
            for k in range(4):
                act.wait_ge(sem["turned"], k + 5)
                act.activation(xmT[:, k * 512:(k + 1) * 512], ps[:, k + 4], ACT.Identity,
                               scale=cols[:, 0:1], bias=cols[:, 1:2]).then_inc(sem["turned_copied"], 1)

            def side_part(ev):
                kind, g, half = (*ev, 0)[:3]
                dr = g // PAIRS
                act.wait_ge(sem["side_ready"], SIDE[ev] + 1)
                if kind == "u":
                    after(act, "conv_tap", 3 * (HALVES * (g - 1) + half + 1))
                    after(act, "u_ready", g)
                    act.activation(u_raw[:, half], side, ACT.Copy).then_inc(sem["u_copied"], 1)
                    act.activation(conv[:, half], side, ACT.Identity, scale=par[:, dr, half, TAPS - 1:TAPS],
                                   bias=par[:, dr, half, TAPS:TAPS + 1]).then_inc(sem["side_free"], 1)
                elif kind == "z" and half == 0:
                    after(act, "gated", HALVES * (g - 1))
                    act.activation(z_s[:, g % 2, 0], side, ACT.Copy).then_inc(sem["side_free"], 1)
                elif kind == "z":
                    act.activation(z_s[:, g % 2, 1], side, ACT.Silu).then_inc(sem["side_free"], 1)
                    act.wait_ge(sem["side_free"], SIDE["z", g, 0] + 1)
                    act.activation(z_s[:, g % 2, 0], z_s[:, g % 2, 0], ACT.Silu).then_inc(sem["z_ready"], 1)
                    act.wait_ge(sem["conv_tap"], 3 * HALVES * (g + 1))
                    act.activation(u_s[:, g % 2], conv[:], ACT.Silu).then_inc(sem["u_ready"], 1)
                    act.preload_act_table_set("natural_log_exp_and_others")
                elif kind == "x":
                    act.activation(dtr[DT_ROW:DT_ROW + RANK], ps[DT_ROW:DT_ROW + RANK, SIDE_BANK], ACT.Copy) \
                        .then_inc(sem["dtr_ready"], 1)
                    after(act, "c_spread", STATES * (g - 1))
                    act.activation(bc[:, g % 2], ps[0:96, SIDE_BANK], ACT.Copy).then_inc(sem["hi_ready"], 1)
                else:
                    n = HALVES * g + half
                    bias = par[:, dr, half, TAPS + 1:TAPS + 2]
                    after(act, "dt_ready", n)
                    act.activation(dt_a[:], side, ACT.Abs, bias=bias).then_inc(sem["dt_abs"], 1)
                    act.activation(dt_b[:], side, ACT.Relu, bias=bias).then_inc(sem["side_free"], 1)
                    act.wait_ge(sem["dt_abs"], n + 1)
                    act.activation(dt_a[:], dt_a[:], ACT.Exp, scale=-1.0).then_inc(sem["dt_exp"], 1)
                    act.wait_ge(sem["dt_exp"], n + 1)
                    act.activation(dt_a[:], dt_a[:], ACT.Ln, bias=1.0).then_inc(sem["dt_ln"], 1)

            def mid(g):
                act.wait_ge(sem["side_free"], SIDE["x", g] + 1)
                after(act, "bc_ready", g)
                act.activation(bc_mid[:], bc_rest[:], ACT.Copy).then_inc(sem["mid_ready"], 1)

            def copy_b(N):
                after(act, "b_spread", N + 1)
                after(act, "drive_ready", 2 * N - 2)
                act.activation(b_sb[:, N % 2], ps[:, B_BANK], ACT.Copy).then_inc(sem["b_copied"], 1)

            def state(N):
                g, j = N // STATES, N % STATES
                lo = 0 if g >= PAIRS else 1
                if j == 0:
                    act.wait_ge(sem["dt_ready"], HALVES * (g + 1))
                    act.wait_ge(sem["a_ready"], 1)
                    act.wait_ge(sem["zero_cols"], HALVES * (g // PAIRS + 1))
                if N == 0:
                    copy_b(0)
                for half in range(HALVES):
                    after(act, "scan_done", 2 * N + half - 1)
                    act.activation(seqs(ps[:, DECAY + half])[:, :, lo:lo + SEQ - 1],
                                   seqs(dt[:, g % 2, half])[:, :, lo:lo + SEQ - 1],
                                   ACT.Exp, scale=negA[:, g // PAIRS, half, j:j + 1]).then_inc(sem["decay_ready"], 1)
                    if half == 0 and N + 1 < ALL:
                        copy_b(N + 1)

            def gate():
                act.wait_ge(sem["gate_step"], 2)
                act.activation(small[:, 2], small[:, 1], ACT.Exp).then_inc(sem["gate_act"], 1)
                act.wait_ge(sem["gate_step"], 6)
                act.activation(small[:, 9, 0:1], small[:, 8, 0:1], ACT.Exp).then_inc(sem["gate_act"], 1)

            def experts():
                def gelu(b, k):
                    p = 2 * b[0] + k
                    r = (2 * b[1] + k) % RING
                    after(act, "e0_down", p - 1)
                    for c in range(CHUNKS):
                        after(act, "e0_up", 2 * p + c // 2 + 1)
                        act.activation(hT[:, k, c], ps[:, 2 * k + c // 2, (c % 2) * SEQ:(c % 2 + 1) * SEQ], ACT.Gelu,
                                       bias=wbuf[:, r, HIDDEN + c:HIDDEN + c + 1]).then_inc(sem["e0_gelu"], 1)

                for p in range(RING):
                    gelu((p // 2, p // 2), p % 2)
                with act.Fori(1, SEQS // 2) as i:
                    for p in range(RING):
                        gelu((2 * i + p // 2, p // 2), p % 2)
                act.preload_act_table_set("natural_log_exp_and_others")

            for ev in READERS:
                if ev[0] == "state":
                    state(ev[1])
                elif ev[0] in ("u", "z", "x", "dt"):
                    side_part(ev)
                elif ev[0] == "mid":
                    mid(ev[1])
                elif ev == ("gate", 0):
                    gate()
                elif ev[0] == "experts":
                    experts()
            act.wait_ge(sem["centred"], 3)
            act.activation(sq[:], xm[:], ACT.Square).then_inc(sem["squared"], 1)

            for k in range(4):
                act.wait_ge(sem["turned"], k + 9)
                act.activation(xnT[:, k * 512:(k + 1) * 512], ps[:, k], ACT.Copy).then_inc(sem["turned_copied"], 1)
            act.wait_ge(sem["r_dve"], R_BASE + 2)
            act.activation(route[:, 1], route[:, 0], ACT.Exp).then_inc(sem["r_act"], 1)
            for k in range(4):
                act.wait_ge(sem["slots_spread"], k + 1)
                act.activation(xe[:, 2 * k:2 * k + 2].rearrange("p b e c -> p (b e c)"), ps[:, k], ACT.Copy) \
                    .then_inc(sem["slots_copied"], 1)
            for e in range(EXPERTS):
                for c in range(CHUNKS):
                    act.wait_ge(sem["e_up"], 2 * e + c // 2 + 1)
                    if c == 0:
                        after(act, "e_down", e - 1)
                    act.activation(hT1[:, e % 2, c], ps[:, 2 * (e % 2) + c // 2, (c % 2) * SEQ:(c % 2 + 1) * SEQ],
                                   ACT.Gelu_apprx_tanh).then_inc(sem["e_gelu"], 1)
            act.preload_act_table_set("exp_and_others")
            for k in range(4):
                act.wait_ge(sem["e_turn"], k + 1)
                act.wait_ge(sem["d_turned"], 8)
                act.activation(eo[:, 2 * k:2 * k + 2].rearrange("p b s d -> p (b s d)"), ps[:, k], ACT.Copy) \
                    .then_inc(sem["e_turned"], 1)

            for l in range(2):
                act.wait_ge(sem["resid"] if l else sem["normed"], 4 if l else 3)
                act.activation(sq[:], (acc if l else xn)[:], ACT.Square).then_inc(sem["squared"], 1)
                for k in range(4):
                    act.wait_ge(sem["turned"], 12 + 4 * l + k + 1)
                    act.activation(xmT[:, k * 512:(k + 1) * 512], ps[:, k], ACT.Copy, scale=cols[:, 2 + l:3 + l]) \
                        .then_inc(sem["turned_copied"], 1)
                if l == 0:
                    for k in range(4):
                        act.wait_ge(sem["lat_ready"], k + 1)
                        act.activation(latT[:, k * 512:(k + 1) * 512], ps[0:LAT, 4 + k], ACT.Copy) \
                            .then_inc(sem["lat_copied"], 1)
                act.wait_ge(sem["qkv_ready"], l + 1)
                act.activation(v_sb[:],
                               ps[:, 4:6].rearrange("p k (t c) -> p (k t) c", c=2 * KV * HD)[:, :, KV * HD:]
                               .rearrange("p t (g d) -> p t g d", d=HD), ACT.Copy).then_inc(sem["v_ready"], 1)
                act.wait_ge(sem["roped"], 2 * l + 2)
                act.activation(rot[:, 0], qk[:].rearrange("p h d -> p (h d)"), ACT.Square).then_inc(sem["qk_sq"], 1)
                act.wait_ge(sem["qk_var"], l + 1)
                act.activation(norm[:, 1], norm[:, 0], ACT.Sqrt).then_inc(sem["qk_sqrt"], 1)
                act.preload_act_table_set("exp_and_others")
                act.wait_ge(sem["qk_normed"], l + 1)
                q_all, k_all = qk[:, 0:TILES * HEADS], qk[:, TILES * HEADS:]
                act.activation(qs[:, :, 0:2], q_all.unsqueeze(2).broadcast_to([P, TILES * HEADS, 2, HD]), ACT.Copy) \
                    .then_inc(sem["qk_hi"], 1)
                act.activation(ks[:, :, 0::2], k_all.unsqueeze(2).broadcast_to([P, TILES * KV, 2, HD]), ACT.Copy) \
                    .then_inc(sem["qk_hi"], 1)

                def step_probs(b, kv):
                    step = KV * (SEQS * l + b) + kv
                    for n in range(3):
                        unit = 3 * step + n
                        slot_p = 3 * (kv % 2) + n
                        bank = (3 * kv + n) % 4
                        after(act, "scores_ready", unit + 1)
                        after(act, "av_done", step - 1)
                        if l and n == 1:
                            keys, width = slice(P - WINDOW, P), GROUP * WINDOW
                        else:
                            keys, width = slice(0, P), COLS
                        act.activation(probs[keys, slot_p, 0:width], ps[keys, bank, 0:width], ACT.Exp, scale=HD ** -0.5) \
                            .then_inc(sem["probs_ready"], 1)

                def copy_av(b):
                    for qt in range(2):
                        after(act, "av_done", KV * (SEQS * l + b) + KV)
                        after(act, "av_turned", 2 * (SEQS * l + b) + qt - 1)
                        act.activation(avT[:, qt], ps[:, 5 + qt], ACT.Copy).then_inc(sem["av_copied"], 1)

                def sequence_probs(b, first=False):
                    for kv in range(KV):
                        step_probs(b, kv)
                        if kv == 0 and not first:
                            copy_av(b - 1)

                sequence_probs(0, first=True)
                sequence_probs(1)
                with act.Fori(2, SEQS) as b:
                    sequence_probs(b)
                copy_av(SEQS - 1)
                for k in range(4):
                    act.wait_ge(sem["o_turn"], 4 * l + k + 1)
                    act.activation(xmT[:, k * 512:(k + 1) * 512], ps[:, k], ACT.Copy).then_inc(sem["o_copied"], 1)

        @block.vector
        def _(dve):
            dve.wait_ge(sem["consts_loaded"], 48)
            dve.tensor_tensor(spreadf[:], ident[0:96, 0:32], ident[0:96, 32:64], ALU.add).then_inc(sem["spread_ready"], 1)
            dve.wait_ge(sem["spread_ready"], 1)
            dve.tensor_tensor(spread[:], spreadf[:], ident[0:96, 64:96], ALU.add).then_inc(sem["spread_ready"], 1)
            for dr in range(2):
                for half in range(HALVES):
                    dve.tensor_scalar(diagD[:, dr, half], ident[:], par[:, dr, half, TAPS + 2:TAPS + 3], None,
                                      ALU.mult).then_inc(sem["diag_ready"], 1)
            dve.wait_ge(sem["a_exp"], 1)
            dve.tensor_scalar(negA[:], negA[:], -1.0, None, ALU.mult).then_inc(sem["a_ready"], 1)

            def bcast(t):
                return t.unsqueeze(2).broadcast_to([P, TILES, D])

            def layernorm(use, src, dst):
                dve.tensor_reduce(stat[:, 0], src, AX.X, ALU.add).then_inc(sem["sum_done"], 1)
                dve.wait_ge(sem["sum_done"], 2 * use + 1)
                dve.tensor_scalar(stat[:, 1], stat[:, 0], 1.0 / D, None, ALU.mult).then_inc(sem["sum_done"], 1)
                dve.wait_ge(sem["sum_done"], 2 * use + 2)
                dve.tensor_tensor(xm[:], src, bcast(stat[:, 1]), ALU.subtract).then_inc(sem["centred"], 1)
                dve.wait_ge(sem["squared"], use + 1)
                dve.tensor_reduce(stat[:, 0], sq[:], AX.X, ALU.add).then_inc(sem["r_dve"], 1)
                dve.wait_ge(sem["r_dve"], use + 1)
                dve.tensor_scalar(stat[:, 2], stat[:, 0], 1.0 / D, LN_EPS, ALU.mult, ALU.add) \
                    .then_inc(sem["var_done"], 1)
                dve.wait_ge(sem["pow_done"], use + 1)
                dve.wait_ge(sem["centred"], use + 1)
                dve.tensor_tensor(dst, xm[:], bcast(stat[:, 3]), ALU.mult).then_inc(sem["normed"], 1)
                dve.wait_ge(sem["normed"], use + 1)

            dve.wait_ge(sem["x_loaded"], 16)
            layernorm(0, x_sb[:], xn[:])
            layernorm(1, xn[:], xm[:])
            dve.tensor_tensor(acc[:], x_sb[:], xn[:], ALU.add).then_inc(sem["acc_added"], 1)
            dve.wait_ge(sem["turned_copied"], 4)
            dve.tensor_reduce(pooled[:], seqs(xnT[:]), AX.X, ALU.add).then_inc(sem["pool_mean"], 1)

            def side_part(ev):
                kind, g, half = (*ev, 0)[:3]
                dr = g // PAIRS
                if kind == "u":
                    n = HALVES * g + half
                    dve.wait_ge(sem["u_copied"], n + 1)
                    dve.wait_ge(sem["side_free"], SIDE[ev] + 1)
                    for k in range(1, TAPS):
                        if dr == 0:
                            to, of = slice(k, SEQ), slice(0, SEQ - k)
                        else:
                            to, of = slice(0, SEQ - k), slice(k, SEQ)
                        c = seqs(conv[:, half])[:, :, to]
                        after(dve, "conv_tap", 3 * n + k - 1)
                        dve.scalar_tensor_tensor(out=c, in0=seqs(u_raw[:, half])[:, :, of],
                                                 scalar=par[:, dr, half, TAPS - 1 - k:TAPS - k], in1=c,
                                                 op0=ALU.mult, op1=ALU.add).then_inc(sem["conv_tap"], 1)
                elif kind == "x":
                    dve.wait_ge(sem["hi_ready"], g + 1)
                    dve.tensor_tensor(bc_rest[:], ps[0:96, SIDE_BANK], bc[:, g % 2], ALU.subtract) \
                        .then_inc(sem["side_free"], 1)
                elif kind == "mid":
                    dve.wait_ge(sem["mid_ready"], g + 1)
                    dve.tensor_copy(bc[32:64, g % 2], bc_mid[32:64]).then_inc(sem["bc_part"], 1)
                    dve.tensor_tensor(bc[64:96, g % 2], bc_rest[64:96], bc_mid[64:96], ALU.subtract) \
                        .then_inc(sem["bc_ready"], 1)
                elif kind == "dt":
                    dve.wait_ge(sem["dt_ln"], HALVES * g + half + 1)
                    after(dve, "decay_ready", STATES * HALVES * (g - 1))
                    dve.tensor_tensor(dt[:, g % 2, half], dt_a[:], dt_b[:], ALU.add).then_inc(sem["dt_ready"], 1)

            def scan(N, half):
                q = 2 * N + half
                k = 2 * (N % 2) + half
                dve.wait_ge(sem["decay_ready"], q + 1)
                dve.wait_ge(sem["drive_ready"], q + 1)
                after(dve, "hc_ready", q - UNITS + 1)
                turn = slice(None, None, -1) if N // STATES >= PAIRS else slice(None)
                dve.tensor_tensor_scan(h[:, k, turn], ps[:, DECAY + half, turn], drive[:, k, turn], 0.0,
                                       ALU.mult, ALU.add).then_inc(sem["scan_done"], 1)

            def times_c(N, half):
                q = 2 * N + half
                k = 2 * (N % 2) + half
                dve.wait_ge(sem["scan_done"], q + 1)
                dve.wait_ge(sem["c_spread"], N + 1)
                after(dve, "y_added", q - UNITS + 1)
                dve.tensor_tensor(hc[:, k], h[:, k], ps[:, C_BANK + N % 2], ALU.mult).then_inc(sem["hc_ready"], 1)

            def zero_boundary(g):
                after(dve, "scan_done", STATES * HALVES * g)
                col = SEQ - 1 if g >= PAIRS else 0
                for half in range(HALVES):
                    dve.memset(seqs(ps[:, DECAY + half])[:, :, col:col + 1], 0.0).then_inc(sem["zero_cols"], 1)
                dve.wait_ge(sem["zero_cols"], 2 if g == 0 else 4)

            def state(N):
                if N % (PAIRS * STATES) == 0:
                    zero_boundary(N // STATES)
                scan(N, 0)
                if N:
                    times_c(N - 1, 1)
                if N > STATES and N % STATES == 1:
                    gate_y(N // STATES - 1)
                scan(N, 1)
                times_c(N, 0)

            def gate_y(g):
                for half in range(HALVES):
                    dve.wait_ge(sem["y_added"], STATES * HALVES * (g + 1) - 1 + half)
                    if g:
                        dve.wait_ge(sem["side_ready"], SIDE["finish", g - 1] + 1)
                    dve.tensor_tensor(yg[:, half], ps[:, Y_BANK + half], z_s[:, g % 2, half], ALU.mult) \
                        .then_inc(sem["gated"], 1)

            def finish(ev):
                g = ev[1]
                rows = slice(4 * (g % PAIRS), 4 * (g % PAIRS) + 4)
                dve.wait_ge(sem["side_ready"], SIDE[ev] + 1)
                if g >= PAIRS:
                    dve.wait_ge(sem["side_free"], SIDE["finish", g - PAIRS] + 1)
                else:
                    dve.wait_ge(sem["ln0_added"], SEQS)
                dve.tensor_tensor((x_sb if g >= PAIRS else acc)[:, rows], acc[:, rows],
                                  side.rearrange("p (t d) -> p t d", d=D), ALU.add).then_inc(sem["side_free"], 1)

            def gate():
                step = [0]

                def link(ins):
                    step[0] += 1
                    ins.then_inc(sem["gate_step"], 1)
                    dve.wait_ge(sem["gate_step"], step[0])

                s = small
                dve.wait_ge(sem["gate_weights_loaded"], 96)
                dve.wait_ge(sem["side_ready"], SIDE["gate", 0] + 1)
                dve.scalar_tensor_tensor(out=s[:, 0], in0=side[0:SEQS, 0:EXPERTS], scalar=1.0 / SEQ, in1=br[:],
                                         op0=ALU.mult, op1=ALU.add).then_inc(sem["side_free"], 1)
                dve.wait_ge(sem["side_free"], SIDE["gate", 0] + 1)
                link(dve.tensor_reduce(s[:, 3, 0:1], s[:, 0], AX.X, ALU.max))
                link(dve.tensor_scalar(s[:, 1], s[:, 0], s[:, 3, 0:1], None, ALU.subtract))
                dve.wait_ge(sem["gate_act"], 1)
                link(dve.tensor_reduce(s[:, 3, 1:2], s[:, 2], AX.X, ALU.add))
                link(dve.reciprocal(s[:, 3, 2:3], s[:, 3, 1:2]))
                link(dve.tensor_scalar(s[:, 4], s[:, 2], s[:, 3, 2:3], None, ALU.mult))
                dve.max(s[:, 5], s[:, 4]).then_inc(sem["cw_ready"], 1)
                dve.wait_ge(sem["cw_ready"], 1)
                link(dve.tensor_tensor(s[:, 8, 0:1], s[:, 5, 1:2], s[:, 5, 0:1], ALU.subtract))
                dve.max_index(index[:], s[:, 5], s[:, 4]).then_inc(sem["index_ready"], 1)
                dve.wait_ge(sem["index_ready"], 1)
                link(dve.tensor_copy(s[:, 6], index[:]))
                dve.wait_ge(sem["gate_act"], 2)
                link(dve.tensor_scalar(s[:, 10, 0:1], s[:, 9, 0:1], 1.0, None, ALU.add))
                link(dve.reciprocal(s[:, 11, 0:1], s[:, 10, 0:1]))
                link(dve.tensor_tensor(s[:, 11, 1:2], s[:, 11, 0:1], s[:, 9, 0:1], ALU.mult))
                for k in range(2):
                    link(dve.tensor_scalar(s[:, 12 + k], iota8[:], s[:, 6, k:k + 1], s[:, 11, k:k + 1],
                                           ALU.is_equal, ALU.mult))
                link(dve.tensor_tensor(s[:, 14], s[:, 12], s[:, 13], ALU.add))
                link(dve.tensor_tensor(wdiag[:], ident[0:SEQS, 0:SEQS].unsqueeze(2).broadcast_to([SEQS, SEQS, 2]),
                                       s[:, 11, 0:2].unsqueeze(1).broadcast_to([SEQS, SEQS, 2]), ALU.mult))
                assert step[0] == 14

            def gate_copy(k):
                dve.wait_ge(sem["side_ready"], SIDE["gate", k] + 1)
                if k == 1:
                    dve.tensor_copy(cwT[:], side[0:EXPERTS, 0:SEQS]).then_inc(sem["side_free"], 1)
                else:
                    dve.tensor_copy(cw[:], side[:, 0:2 * SEQS]).then_inc(sem["side_free"], 1)

            def experts():
                dve.wait_ge(sem["side_free"], SIDE["gate", 2] + 1)
                dve.wait_ge(sem["acc_added"], 1)

                def sequence(b, r):
                    rows = moe[:, ds(2 * b, 2)]
                    m, c, q = xm[:, 4 * r:4 * r + 2], xm[:, 4 * r + 2:4 * r + 4], sq[:, 2 * r:2 * r + 2]
                    for k in range(2):
                        bank = ps[:, 4 + k]
                        dve.wait_ge(sem["e0_down"], 2 * b + k + 1)
                        if k:
                            dve.wait_ge(sem["e0_added"], 2 * b + 1)
                        dve.scalar_tensor_tensor(out=m if k else rows, in0=bank[:, 0:2 * D].rearrange("p (t d) -> p t d", d=D),
                                                 scalar=cw[:, ds(2 * b + k, 1)], in1=rows, op0=ALU.mult, op1=ALU.add) \
                            .then_inc(sem["e0_added"], 1)
                    st = seqstat[:, r]

                    def over(t):
                        return t.unsqueeze(2).broadcast_to([P, 2, D])

                    def link(k, ins):
                        ins.then_inc(sem["ln0_step"], 1)
                        dve.wait_ge(sem["ln0_step"], 8 * b + k)

                    dve.wait_ge(sem["e0_added"], 2 * b + 2)
                    link(1, dve.tensor_reduce(st[:, 0], m, AX.X, ALU.add))
                    link(2, dve.tensor_scalar(st[:, 1], st[:, 0], 1.0 / D, None, ALU.mult))
                    link(3, dve.tensor_tensor(c, m, over(st[:, 1]), ALU.subtract))
                    link(4, dve.tensor_tensor(q, c, c, ALU.mult))
                    link(5, dve.tensor_reduce(st[:, 0], q, AX.X, ALU.add))
                    dve.tensor_scalar(st[:, 2], st[:, 0], 1.0 / D, LN_EPS, ALU.mult, ALU.add).then_inc(sem["ln0_var"], 1)
                    dve.wait_ge(sem["ln0_pow"], b + 1)
                    link(6, dve.tensor_tensor(c, c, over(st[:, 3]), ALU.mult))
                    link(7, dve.tensor_tensor(c, c, gb[:, 0].unsqueeze(1).broadcast_to([P, 2, D]), ALU.mult))
                    link(8, dve.tensor_tensor(c, c, gb[:, 1].unsqueeze(1).broadcast_to([P, 2, D]), ALU.add))
                    dve.tensor_tensor(acc[:, ds(2 * b, 2)], acc[:, ds(2 * b, 2)], c, ALU.add).then_inc(sem["ln0_added"], 1)

                dve.wait_ge(sem["bias_ready"], 1)
                for k in range(2):
                    rows = slice(8 * k, 8 * k + 8)
                    dve.tensor_tensor(moe[:, rows].rearrange("p (b two) d -> p b two d", two=2),
                                      xn[:, rows].rearrange("p (b two) d -> p b two d", two=2),
                                      ps[:, 4 + k].rearrange("p (b d) -> p b d", d=D).unsqueeze(2).broadcast_to([P, 4, 2, D]),
                                      ALU.add).then_inc(sem["moe_bias"], 1)
                dve.wait_ge(sem["moe_bias"], 2)
                with dve.Fori(0, SEQS // 2) as i:
                    sequence(2 * i, 0)
                    sequence(2 * i + 1, 1)

            for ev in READERS:
                if ev[0] == "state":
                    state(ev[1])
                elif ev[0] in ("u", "z", "x", "mid", "dt"):
                    side_part(ev)
                elif ev[0] == "finish":
                    finish(ev)
                elif ev[0] == "end":
                    times_c(ALL - 1, 1)
                    gate_y(STEPS - 1)
                elif ev == ("gate", 0):
                    gate()
                elif ev[0] == "gate":
                    gate_copy(ev[1])
                elif ev[0] == "experts":
                    experts()

            dve.wait_ge(sem["side_free"], SIDE["finish", STEPS - 1] + 1)
            layernorm(2, x_sb[:], xn[:])

            step = [R_BASE]

            def link(ins):
                step[0] += 1
                ins.then_inc(sem["r_dve"], 1)
                dve.wait_ge(sem["r_dve"], step[0])

            def per_expert(t):
                return t.unsqueeze(2).broadcast_to([P, TILES, EXPERTS])

            dve.wait_ge(sem["r_pe"], 1)
            logits = ps[:, 4, 0:TILES * EXPERTS].rearrange("p (t e) -> p t e", e=EXPERTS)
            link(dve.tensor_reduce(rstat[:, 0], logits, AX.X, ALU.max))
            link(dve.tensor_tensor(route[:, 0], logits, per_expert(rstat[:, 0]), ALU.subtract))
            dve.wait_ge(sem["l1_weights_loaded"], 12 * 16)
            link(dve.tensor_scalar(route[:, 2], route[:, 0], 0.0, None, ALU.is_equal))
            link(dve.tensor_tensor(route[:, 3], route[:, 2], iotar[:].unsqueeze(1).broadcast_to([P, TILES, EXPERTS]),
                                   ALU.mult))
            link(dve.tensor_reduce(rstat[:, 1], route[:, 3], AX.X, ALU.max))
            link(dve.tensor_tensor(route[:, 4], route[:, 3], per_expert(rstat[:, 1]), ALU.is_equal))
            link(dve.tensor_copy(mask16[:], route[:, 4]))
            dve.wait_ge(sem["r_act"], 1)
            link(dve.tensor_reduce(rstat[:, 2], route[:, 1], AX.X, ALU.add))
            link(dve.reciprocal(rstat[:, 3], rstat[:, 2]))
            dve.wait_ge(sem["r_pe"], 2)
            pos = route[:, 5].rearrange("p t e -> p (t e)").rearrange("p (two b e) -> p two b e", two=2, e=EXPERTS)
            for two in range(2):
                link(dve.tensor_tensor(pos[:, two], ps[:, 5, 64 * two:64 * two + 64].rearrange("p (b e) -> p b e", e=EXPERTS),
                                       route[:, 4, two::2], ALU.mult))
            for two in range(2):
                link(dve.tensor_tensor(slot[:, two::2], pos[:, two].unsqueeze(3).broadcast_to([P, SEQS, EXPERTS, CAP]),
                                       iota32[:].unsqueeze(1).unsqueeze(1).broadcast_to([P, SEQS, EXPERTS, CAP]), ALU.is_equal))
            for k in range(8):
                dve.wait_ge(sem["d_turn"], k + 1)
                dve.tensor_copy(slotT[:, k // 4, 4 * (k % 4):4 * (k % 4) + 4].rearrange("p t n -> p (t n)"),
                                ps[:, 4 + k % 4]).then_inc(sem["d_turned"], 1)
            for e in range(EXPERTS):
                dve.wait_ge(sem["e_down"], e + 1)
                dve.tensor_copy(xe[:, :, e], ps[:, 4 + e % 2, 0:SEQ].rearrange("p (b c) -> p b c", c=CAP)).then_inc(sem["e_out"], 1)
            for k in range(4):
                dve.wait_ge(sem["e_comb"], k + 1)
                rows = slice(4 * k, 4 * k + 4)
                dve.tensor_tensor(xm[:, rows], ps[:, 4 + k].rearrange("p (t d) -> p t d", d=D),
                                  rstat[:, 3, rows].unsqueeze(2).broadcast_to([P, 4, D]), ALU.mult) \
                    .then_inc(sem["e_added"], 1)
            dve.wait_ge(sem["e_added"], 4)
            dve.tensor_tensor(x_sb[:], x_sb[:], xm[:], ALU.add).then_inc(sem["x1_ready"], 1)

            for l in range(2):
                src = acc if l else xn
                dve.wait_ge(sem["squared"], 4 + l)
                dve.tensor_reduce(stat[:, 0], sq[:], AX.X, ALU.add).then_inc(sem["sum_done"], 1)
                dve.wait_ge(sem["sum_done"], 7 + l)
                dve.tensor_scalar(stat[:, 2], stat[:, 0], 1.0 / D, RMS_EPS, ALU.mult, ALU.add).then_inc(sem["var_done"], 1)
                dve.wait_ge(sem["pow_done"], 4 + l)
                dve.tensor_tensor(xm[:], src[:], bcast(stat[:, 3]), ALU.mult).then_inc(sem["rms_done"], 1)
                dve.wait_ge(sem["qkv_ready"], l + 1)
                nq = TILES * HEADS * HD
                qps = ps[:, 0:4].rearrange("p k c -> p (k c)")
                cos, sin = rope[:, l, 0], rope[:, l, 1]
                dve.tensor_tensor(rot[:, 0, 0:nq].rearrange("p (b c) -> p b c", b=SEQS), qps.rearrange("p (b c) -> p b c", b=SEQS),
                                  cos.unsqueeze(1).broadcast_to([P, SEQS, 2 * D]), ALU.mult).then_inc(sem["rope_a"], 1)
                dve.tensor_tensor(rot[:, 1, 0:nq].rearrange("p (b c two) -> p b c two", b=SEQS, two=2),
                                  qps.rearrange("p (b c two) -> p b c two", b=SEQS, two=2)[:, :, :, ::-1],
                                  sin.rearrange("p (c two) -> p c two", two=2).unsqueeze(1).broadcast_to([P, SEQS, D, 2]),
                                  ALU.mult).then_inc(sem["rope_a"], 1)
                dve.wait_ge(sem["v_ready"], l + 1)
                kps = ps[:, 4:6].rearrange("p k (t c) -> p (k t) c", c=2 * KV * HD)[:, :, 0:KV * HD]
                kr = rot[:, :, nq:].rearrange("p r (t c) -> p r t c", c=KV * HD)
                for two in range(2):
                    dve.tensor_tensor(kr[:, 0, two::2], kps[:, two::2],
                                      cos[:, two * D:two * D + KV * HD].unsqueeze(1).broadcast_to([P, SEQS, KV * HD]),
                                      ALU.mult).then_inc(sem["rope_a"], 1)
                    dve.tensor_tensor(kr[:, 1, two::2].rearrange("p t (c two) -> p t c two", two=2),
                                      kps[:, two::2].rearrange("p t (c two) -> p t c two", two=2)[:, :, :, ::-1],
                                      sin[:, two * D:two * D + KV * HD].rearrange("p (c two) -> p c two", two=2)
                                      .unsqueeze(1).broadcast_to([P, SEQS, KV * HD // 2, 2]),
                                      ALU.mult).then_inc(sem["rope_a"], 1)
                qk_flat = qk[:].rearrange("p h d -> p (h d)")
                for part, (lo, hi) in enumerate(((0, nq), (nq, nq + TILES * KV * HD))):
                    dve.wait_ge(sem["rope_a"], 6 * l + 2 + 4 * part)
                    dve.tensor_tensor(qk_flat[:, lo:hi], rot[:, 0, lo:hi], rot[:, 1, lo:hi], ALU.add).then_inc(sem["roped"], 1)
                dve.wait_ge(sem["qk_sq"], l + 1)
                dve.tensor_reduce(norm[:, 2], rot[:, 0].rearrange("p (h d) -> p h d", d=HD), AX.X, ALU.add) \
                    .then_inc(sem["qk_sum"], 1)
                dve.wait_ge(sem["qk_sum"], l + 1)
                dve.tensor_scalar(norm[:, 0], norm[:, 2], 1.0 / HD, RMS_EPS, ALU.mult, ALU.add).then_inc(sem["qk_var"], 1)
                dve.wait_ge(sem["qk_sqrt"], l + 1)
                dve.reciprocal(norm[:, 2], norm[:, 1]).then_inc(sem["qk_inv"], 1)
                dve.wait_ge(sem["qk_inv"], l + 1)
                dve.tensor_tensor(qk[:], qk[:], norm[:, 2].unsqueeze(2).broadcast_to([P, TILES * (HEADS + KV), HD]), ALU.mult) \
                    .then_inc(sem["qk_normed"], 1)
                q_all, k_all = qk[:, 0:TILES * HEADS], qk[:, TILES * HEADS:]
                dve.wait_ge(sem["qk_hi"], 2 * l + 1)
                dve.tensor_tensor(qs[:, :, 2:4], q_all.unsqueeze(2).broadcast_to([P, TILES * HEADS, 2, HD]), qs[:, :, 0:2],
                                  ALU.subtract).then_inc(sem["qk_split"], 1)
                dve.wait_ge(sem["qk_hi"], 2 * l + 2)
                dve.tensor_tensor(ks[:, :, 1::2], k_all.unsqueeze(2).broadcast_to([P, TILES * KV, 2, HD]), ks[:, :, 0::2],
                                  ALU.subtract).then_inc(sem["qk_split"], 1)

                def copy_turned(b, r):
                    for k in range(3):
                        after(dve, "turn_q", 3 * SEQS * l + 3 * b + k + 1)
                        if k == 0:
                            after(dve, "scores_ready", 3 * KV * (SEQS * l + b - 1))
                        if k < 2:
                            ins = dve.tensor_copy(qT[:, r, :, k * P:(k + 1) * P],
                                                  ps[:, 4].rearrange("p (j n) -> p j n", n=P))
                        else:
                            ins = dve.tensor_copy(kT[:, r], ps[:, 4, 0:SEQ])
                        ins.then_inc(sem["turn_copied"], 1)

                def seq_out(b):
                    for qt in range(2):
                        n = 2 * (SEQS * l + b) + qt
                        o = ps[:, 7].rearrange("p (j g d) -> p g j d", j=GROUP, g=KV)
                        after(dve, "av_turned", n + 1)
                        after(dve, "head_out", n - 1)
                        dve.reciprocal(den[:, qt].rearrange("p (g j) -> p g j", g=KV), o[:, :, :, HD]) \
                            .then_inc(sem["den_done"], 1)
                        after(dve, "den_done", n + 1)
                        dve.tensor_tensor(heads[:, ds(2 * b + qt, 1)].rearrange("p o (g j d) -> p (o g) j d", g=KV, j=GROUP),
                                          o[:, :, :, 0:HD],
                                          den[:, qt].rearrange("p (g j) -> p g j", g=KV).unsqueeze(3)
                                          .broadcast_to([P, KV, GROUP, HD]), ALU.mult).then_inc(sem["head_out"], 1)

                copy_turned(0, 0)
                copy_turned(1, 1)
                copy_turned(2, 0)
                seq_out(0)
                with dve.Fori(1, 3) as i:
                    copy_turned(2 * i + 1, 1)
                    seq_out(2 * i - 1)
                    copy_turned(2 * i + 2, 0)
                    seq_out(2 * i)
                copy_turned(SEQS - 1, 1)
                seq_out(SEQS - 3)
                seq_out(SEQS - 2)
                seq_out(SEQS - 1)
                for k in range(4):
                    rows = slice(4 * k, 4 * k + 4)
                    dve.wait_ge(sem["o_proj"], 4 * l + k + 1)
                    dve.tensor_tensor(acc[:, rows], src[:, rows], ps[:, 4 + k].rearrange("p (t d) -> p t d", d=D), ALU.add) \
                        .then_inc(sem["resid"], 1)
            dve.wait_ge(sem["resid"], 8)
            dve.tensor_tensor(x_sb[:], x_sb[:], acc[:], ALU.add).then_inc(sem["x1_ready"], 1)

        @block.tensor
        def _(pe):
            def side_free(ev):
                after(pe, "side_free", SIDE[ev])

            pe.wait_ge(sem["consts_loaded"], 48)
            for use, (src, bank) in enumerate(((xn, 0), (xm, 4))):
                pe.wait_ge(sem["normed"], use + 1)
                for k in range(4):
                    for t in range(4):
                        last = pe.transpose(ps[:, bank + k, t * P:(t + 1) * P], src[:, 4 * k + t], ident[:])
                    last.then_inc(sem["turned"], 1)

            def project(ev):
                kind, g, half = (*ev, 0)[:3]
                dr = g // PAIRS
                toks = slice((g % PAIRS) * COLS, (g % PAIRS + 1) * COLS)
                side_free(ev)
                if kind in "uz":
                    c = (kind == "z") * INNER + half * P
                    pe.wait_ge(sem["mamba_weights_loaded"], 64)
                    last = pe.matmul(side, w_in[:, dr, c:c + P], xmT[:, toks], start=True, stop=True)
                elif kind == "x":
                    pe.wait_ge(sem["u_ready"], g + 1)
                    for h2 in range(HALVES):
                        last = pe.matmul(ps[0:XROWS, SIDE_BANK], w_x[:, dr, h2], u_s[:, g % 2, h2],
                                         start=(h2 == 0), stop=(h2 == HALVES - 1))
                else:
                    pe.wait_ge(sem["dtr_ready"], g + 1)
                    last = pe.matmul(side, w_dt[DT_ROW:DT_ROW + RANK, dr, half * P:(half + 1) * P],
                                     dtr[DT_ROW:DT_ROW + RANK], start=True, stop=True)
                last.then_inc(sem["side_ready"], 1)

            def add_y(N):
                g = N // STATES
                if N % STATES == 0:
                    after(pe, "gated", HALVES * g)
                    for half in range(HALVES):
                        pe.matmul(ps[:, Y_BANK + half], diagD[:, g // PAIRS, half], u_s[:, g % 2, half],
                                  start=True, stop=True, skip_group_check=True)
                for half in range(HALVES):
                    pe.wait_ge(sem["hc_ready"], 2 * N + half + 1)
                    pe.matmul(ps[:, Y_BANK + half], ident[:], hc[:, 2 * (N % 2) + half], start=False, stop=True,
                              skip_group_check=True).then_inc(sem["y_added"], 1)

            def spread_b(N):
                g, j = N // STATES, N % STATES
                if j == 0:
                    pe.wait_ge(sem["bc_ready"], g + 1)
                after(pe, "b_copied", N)
                pe.matmul(ps[:, B_BANK], spread[:, j:j + 1].broadcast_to([96, P]), bc[:, g % 2],
                          start=True, stop=True).then_inc(sem["b_spread"], 1)

            def state(N):
                g, j = N // STATES, N % STATES
                if N == 0:
                    pe.wait_ge(sem["spread_ready"], 2)
                    pe.wait_ge(sem["diag_ready"], 4)
                    pe.wait_ge(sem["e0_added"], PAIRS0)
                    spread_b(0)
                if N + 1 < ALL:
                    spread_b(N + 1)
                after(pe, "hc_ready", 2 * N - 2)
                pe.matmul(ps[:, C_BANK + N % 2], spread[:, STATES + j:STATES + j + 1].broadcast_to([96, P]),
                          bc[:, g % 2], start=True, stop=True).then_inc(sem["c_spread"], 1)
                if N >= 2:
                    add_y(N - 2)

            def finish(ev):
                g = ev[1]
                side_free(ev)
                pe.wait_ge(sem["gated"], HALVES * (g + 1))
                for t in range(4):
                    for half in range(HALVES):
                        last = pe.matmul(side[:, t * D:(t + 1) * D], yg[:, half, t * P:(t + 1) * P],
                                         w_out[:, g // PAIRS, half], start=(half == 0), stop=(half == HALVES - 1))
                last.then_inc(sem["side_ready"], 1)

            def gate(ev):
                side_free(ev)
                if ev[1] == 0:
                    pe.wait_ge(sem["turned_copied"], 8)
                    pe.wait_ge(sem["pool_mean"], 1)
                    pe.wait_ge(sem["gate_weights_loaded"], 96)
                    last = pe.matmul(side[0:SEQS, 0:EXPERTS], pooled[:], w_r[:], start=True, stop=True)
                elif ev[1] == 1:
                    pe.wait_ge(sem["gate_step"], 14)
                    last = pe.transpose(side[0:EXPERTS, 0:SEQS], small[:, 14], ident[0:SEQS, 0:SEQS])
                else:
                    pe.wait_ge(sem["halfconst"], 2)
                    last = pe.matmul(side[:, 0:2 * SEQS], ones8[:], wdiag[:].rearrange("p b k -> p (b k)"),
                                     start=True, stop=True)
                last.then_inc(sem["side_ready"], 1)

            def experts():
                def up(b, half, k):
                    p = 2 * b + k
                    r = (2 * half + k) % RING
                    pe.wait_ge(sem[f"expert_loaded{r}"], 16 * ((b - half) // 2 + 1) if isinstance(b, int) else 8 * (b - half) + 16)
                    after(pe, "e0_gelu", CHUNKS * (p - 1))
                    for c in range(CHUNKS):
                        last = pe.matmul(ps[:, 2 * k + c // 2, (c % 2) * SEQ:(c % 2 + 1) * SEQ],
                                         wbuf[:, r, c * P:(c + 1) * P], xnT[:, ds(b * SEQ, SEQ)], start=True, stop=True)
                        if c % 2:
                            last.then_inc(sem["e0_up"], 1)

                def down(b, half, k):
                    p = 2 * b + k
                    r = 2 * half + k
                    bank = ps[:, 4 + k]
                    after(pe, "e0_added", p - 1)
                    for t in range(2):
                        for c in range(CHUNKS):
                            if t == 0:
                                after(pe, "e0_gelu", CHUNKS * p + c + 1)
                            last = pe.matmul(bank[:, t * D:(t + 1) * D], hT[:, k, c, t * P:(t + 1) * P],
                                             wbuf[:, r, HIDDEN + CHUNKS + c * D:HIDDEN + CHUNKS + (c + 1) * D],
                                             start=(c == 0), stop=(c == CHUNKS - 1))
                    last.then_inc(sem["e0_down"], 1)

                def two_sequences(b, more=True):
                    up(b, 0, 1)
                    down(b, 0, 0)
                    up(b + 1, 1, 0)
                    down(b, 0, 1)
                    up(b + 1, 1, 1)
                    down(b + 1, 1, 0)
                    if more:
                        up(b + 2, 0, 0)
                    down(b + 1, 1, 1)

                up(0, 0, 0)
                for b in range(SEQS):
                    if b == 0:
                        pe.wait_ge(sem["side_free"], SIDE["gate", 2] + 1)
                    last = pe.matmul(ps[:, 4 + b // 4, (b % 4) * D:(b % 4 + 1) * D], cwT[:, b:b + 1].broadcast_to([EXPERTS, P]),
                                     b2[:], start=True, stop=True)
                last.then_inc(sem["bias_ready"], 1)
                pe.wait_ge(sem["moe_bias"], 2)
                two_sequences(0)
                with pe.Fori(1, SEQS // 2 - 1) as i:
                    two_sequences(2 * i)
                two_sequences(SEQS - 2, more=False)

            for ev in ORDER:
                if ev[0] == "state":
                    state(ev[1])
                elif ev[0] in ("u", "z", "x", "dt"):
                    project(ev)
                elif ev[0] == "finish":
                    finish(ev)
                elif ev[0] == "end":
                    add_y(ALL - 2)
                    add_y(ALL - 1)
                elif ev[0] == "gate":
                    gate(ev)
                elif ev[0] == "experts":
                    experts()

            pe.wait_ge(sem["normed"], 3)
            for k in range(4):
                for t in range(4):
                    last = pe.transpose(ps[:, k, t * P:(t + 1) * P], xn[:, 4 * k + t], ident[:])
                last.then_inc(sem["turned"], 1)
            pe.wait_ge(sem["l1_weights_loaded"], 12 * 16)
            for t in range(TILES):
                if t % 4 == 0:
                    pe.wait_ge(sem["turned_copied"], 9 + t // 4)
                last = pe.matmul(ps[:, 4, t * EXPERTS:(t + 1) * EXPERTS], xnT[:, t * P:(t + 1) * P], w_g[:],
                                 start=True, stop=True)
            last.then_inc(sem["r_pe"], 1)
            pe.wait_ge(sem["r_dve"], R_BASE + 7)
            pe.matmul(ps[:, 5, 0:64], tri[:, 0], mask16[:, 0::2], start=True, stop=True)
            pe.matmul(ps[:, 5, 64:128], tri[:, 1], mask16[:, 0::2], start=True, stop=False)
            pe.matmul(ps[:, 5, 64:128], tri[:, 0], mask16[:, 1::2], start=False, stop=True).then_inc(sem["r_pe"], 1)
            pe.wait_ge(sem["r_dve"], R_BASE + 13)
            for k in range(4):
                for b in (2 * k, 2 * k + 1):
                    for two in range(2):
                        last = pe.matmul(ps[:, k, (b % 2) * SEQ:(b % 2 + 1) * SEQ], xn[:, 2 * b + two],
                                         slot[:, 2 * b + two].rearrange("p e c -> p (e c)"), start=(two == 0), stop=(two == 1))
                last.then_inc(sem["slots_spread"], 1)
            for k in range(8):
                after(pe, "d_turned", k - 3)
                for t in range(4):
                    last = pe.transpose(ps[:, 4 + k % 4, t * P:(t + 1) * P],
                                        slot[:, 4 * (k % 4) + t, 4 * (k // 4):4 * (k // 4) + 4].rearrange("p e c -> p (e c)"),
                                        ident[:])
                last.then_inc(sem["d_turn"], 1)

            def up(e):
                pe.wait_ge(sem["expert_loaded%d" % (e % 2)], 16 * (PAIRS0 // RING + e // 2 + 1))
                after(pe, "e_gelu", CHUNKS * (e - 1))
                for c in range(CHUNKS):
                    last = pe.matmul(ps[:, 2 * (e % 2) + c // 2, (c % 2) * SEQ:(c % 2 + 1) * SEQ],
                                     wbuf1[:, e % 2, c * P:(c + 1) * P], xe[:, :, e],
                                     start=True, stop=True)
                    if c % 2:
                        last.then_inc(sem["e_up"], 1)

            def down(e):
                pe.wait_ge(sem["e_gelu"], CHUNKS * (e + 1))
                after(pe, "e_out", e - 1)
                for c in range(CHUNKS):
                    last = pe.matmul(ps[:, 4 + e % 2, 0:SEQ], wbuf1[:, e % 2, HIDDEN + c * D:HIDDEN + (c + 1) * D],
                                     hT1[:, e % 2, c], start=(c == 0), stop=(c == CHUNKS - 1))
                last.then_inc(sem["e_down"], 1)

            pe.wait_ge(sem["slots_copied"], 4)
            pe.wait_ge(sem["d_turned"], 8)
            up(0)
            for e in range(1, EXPERTS):
                up(e)
                down(e - 1)
            down(EXPERTS - 1)
            pe.wait_ge(sem["e_out"], EXPERTS)
            for k in range(4):
                for n, (b, s) in enumerate(((2 * k, 0), (2 * k, 1), (2 * k + 1, 0), (2 * k + 1, 1))):
                    last = pe.transpose(ps[:, k, n * P:(n + 1) * P], xe[:, b, 4 * s:4 * s + 4].rearrange("p e c -> p (e c)"), ident[:])
                last.then_inc(sem["e_turn"], 1)
            for k in range(4):
                pe.wait_ge(sem["e_turned"], k + 1)
                for t in range(4):
                    for s in range(2):
                        last = pe.matmul(ps[:, 4 + k, t * D:(t + 1) * D], slotT[:, s, 4 * k + t], eo[:, 2 * k + t // 2, s],
                                         start=(s == 0), stop=(s == 1))
                last.then_inc(sem["e_comb"], 1)

            for l in range(2):
                pe.wait_ge(sem["rms_done"], l + 1)
                for k in range(4):
                    for t in range(4):
                        last = pe.transpose(ps[:, k, t * P:(t + 1) * P], xm[:, 4 * k + t], ident[:])
                    last.then_inc(sem["turned"], 1)
                if l == 0:
                    pe.wait_ge(sem["e_added"], 4)
                    for k in range(4):
                        pe.wait_ge(sem["turned_copied"], 12 + k + 1)
                        pe.matmul(ps[0:LAT, 4 + k], w_kvd[:], xmT[:, k * 512:(k + 1) * 512], start=True, stop=True) \
                            .then_inc(sem["lat_ready"], 1)
                for t in range(TILES):
                    if t % 4 == 0:
                        pe.wait_ge(sem["turned_copied"], 12 + 4 * l + t // 4 + 1)
                    pe.matmul(ps[:, t // 4, (t % 4) * D:(t % 4 + 1) * D], xmT[:, t * P:(t + 1) * P], w_q[:, l],
                              start=True, stop=True)
                for t in range(TILES):
                    if l == 0 and t == 0:
                        pe.wait_ge(sem["lat_copied"], 4)
                    c = 2 * KV * HD
                    rows, w = (latT, w_kvu) if l == 0 else (xmT, w_kv)
                    last = pe.matmul(ps[:, 4 + t // 8, (t % 8) * c:(t % 8 + 1) * c], rows[:, t * P:(t + 1) * P], w[:],
                                     start=True, stop=True)
                last.then_inc(sem["qkv_ready"], 1)
                pe.wait_ge(sem["qk_split"], 2 * l + 2)

                def turn(b):
                    for k in range(3):
                        after(pe, "turn_copied", 3 * SEQS * l + 3 * b + k)
                        if k < 2:
                            for j in range(GROUP):
                                heads_j = qs[:, ds((2 * b + k) * HEADS + j * KV, KV)].rearrange("p g i d -> p (g i d)")
                                last = pe.matmul(ps[:, 4, j * P:(j + 1) * P], heads_j, ident16[:], start=True, stop=True)
                        else:
                            for t in range(2):
                                last = pe.matmul(ps[:, 4, t * P:(t + 1) * P],
                                                 ks[:, ds((2 * b + t) * KV, KV)].rearrange("p g i d -> p (g i d)"),
                                                 ident16[:], start=True, stop=True)
                        last.then_inc(sem["turn_q"], 1)

                def scores(b, r, kv):
                    if kv == 0:
                        after(pe, "turn_copied", 3 * (SEQS * l + b) + 3)
                    g = slice(32 * kv, 32 * kv + 32)
                    for n, (kt, qt) in enumerate(((0, 0), (0, 1), (1, 1))):
                        unit = 3 * (KV * (SEQS * l + b) + kv) + n
                        bank = (3 * kv + n) % 4
                        after(pe, "probs_ready", unit - 3)
                        if l and n == 1:
                            near = slice(P - WINDOW, P)
                            part = ps[near, bank, 0:GROUP * WINDOW]
                            pe.matmul(part, ident16[:, near],
                                      masks[:, 2, 0:WINDOW].unsqueeze(1).broadcast_to([P, GROUP, WINDOW]), start=True, stop=False)
                            last = pe.matmul(part, kT[g, r, near], qT[g, r, :, P:P + WINDOW], start=False, stop=True)
                        else:
                            if n != 1:
                                pe.matmul(ps[:, bank], ident16[:], masks[:, l].unsqueeze(1).broadcast_to([P, GROUP, P]),
                                          start=True, stop=False)
                            last = pe.matmul(ps[:, bank], kT[g, r, kt * P:(kt + 1) * P], qT[g, r, :, qt * P:(qt + 1) * P],
                                             start=(n == 1), stop=True)
                        last.then_inc(sem["scores_ready"], 1)

                def average(b, r, kv):
                    step = KV * (SEQS * l + b) + kv
                    if kv == 0:
                        after(pe, "v_placed", SEQS * l + b + 1)
                        after(pe, "av_copied", 2 * (SEQS * l + b))
                    g = slice(32 * kv, 32 * kv + 32)

                    for n, qt, kt in ((0, 0, 0), (2, 1, 1), (1, 1, 0)):
                        if n != 1:
                            after(pe, "probs_ready", 3 * step + n + 1)
                        p = probs[:, 3 * (kv % 2) + n]
                        if l and n == 1:
                            near = slice(P - WINDOW, P)
                            last = pe.matmul(ps[g, 6].rearrange("p (j q) -> p j q", j=GROUP)[:, :, 0:WINDOW],
                                             v_ring[near, r, kt, kv], p[near, 0:GROUP * WINDOW], start=False, stop=True)
                        else:
                            last = pe.matmul(ps[g, 5 + qt], v_ring[:, r, kt, kv], p, start=(n != 1), stop=(n != 2))
                    last.then_inc(sem["av_done"], 1)

                def turn_av(b):
                    for qt in range(2):
                        n = 2 * (SEQS * l + b) + qt
                        after(pe, "av_copied", n + 1)
                        after(pe, "head_out", n)
                        for j in range(GROUP):
                            last = pe.transpose(ps[:, 7, j * P:(j + 1) * P], avT[:, qt, j * P:(j + 1) * P], ident[:])
                        last.then_inc(sem["av_turned"], 1)

                def sequence(b, r, first=False, turn_next=True):
                    for kv in range(KV):
                        scores(b, r, kv)
                        if kv == 1 and turn_next:
                            turn(b + 1)
                        if kv:
                            average(b, r, kv - 1)
                        elif not first:
                            average(b - 1, 1 - r, KV - 1)
                        if kv == 2 and not first:
                            turn_av(b - 1)

                turn(0)
                sequence(0, 0, first=True)
                sequence(1, 1)
                with pe.Fori(1, 3) as i:
                    sequence(2 * i, 0)
                    sequence(2 * i + 1, 1)
                sequence(6, 0)
                sequence(7, 1, turn_next=False)
                average(SEQS - 1, 1, KV - 1)
                turn_av(SEQS - 1)

                for k in range(4):
                    pe.wait_ge(sem["head_out"], 2 * SEQS * (l + 1))
                    for t in range(4):
                        last = pe.transpose(ps[:, k, t * P:(t + 1) * P], heads[:, 4 * k + t], ident[:])
                    last.then_inc(sem["o_turn"], 1)
                for k in range(4):
                    pe.wait_ge(sem["o_copied"], 4 * l + k + 1)
                    for t in range(4):
                        last = pe.matmul(ps[:, 4 + k, t * D:(t + 1) * D], xmT[:, (4 * k + t) * P:(4 * k + t + 1) * P],
                                         w_o[:, l], start=True, stop=True)
                    last.then_inc(sem["o_proj"], 1)


def layouts(v):
    import numpy as np

    def mamba(p):
        w = {k: np.asarray(v[f"L0_attn_{p}_{k}"]) for k in ("Win", "convw", "convb", "Wx", "Wdt", "bdt", "Alog", "D", "Wout")}
        per = np.concatenate([w["convw"][:, 0], w["convb"][:, None], w["bdt"][:, None], w["D"][:, None], w["Alog"]], 1)
        bc = w["Wx"][RANK:].T
        return {
            "par": per.reshape(HALVES, P, NPAR).transpose(1, 0, 2),
            "w_in": w["Win"].T,
            "w_x": np.concatenate([bc, bc, bc, w["Wx"][:RANK].T], 1).reshape(HALVES, P, XROWS).transpose(1, 0, 2),
            "w_dt": w["Wdt"].T,
            "w_out": w["Wout"].T.reshape(HALVES, P, D).transpose(1, 0, 2),
        }

    f, b = mamba("f"), mamba("b")
    a = {k: np.stack([f[k], b[k]], 1) for k in f}
    v = {k: np.asarray(x) for k, x in v.items()}
    a["x"] = v["L0_attn_x"].reshape(TOK, D)
    a["ident"] = np.eye(P, dtype=np.float32)
    a["cols"] = np.stack([v["L0_attn_norm_g"], v["L0_attn_norm_b"], v["L1_attn_norm1_w"], v["L1_attn_norm2_w"]], 1)
    a["w_r"] = v["L0_ffn_Wr"]
    a["br"] = v["L0_ffn_br"]
    a["b2"] = v["L0_ffn_b2"]
    a["iota8"] = np.arange(EXPERTS, dtype=np.float32)
    a["gamma"], a["beta"] = v["L0_ffn_gamma"], v["L0_ffn_beta"]
    down = lambda w: w.reshape(EXPERTS, CHUNKS, P, D).transpose(0, 2, 1, 3).reshape(EXPERTS, P, HIDDEN)
    b1 = v["L0_ffn_b1"].reshape(EXPERTS, CHUNKS, P).transpose(0, 2, 1)
    a["pack0"] = np.concatenate([v["L0_ffn_W1"], b1, down(v["L0_ffn_W2"])], 2)
    a["pack1"] = np.concatenate([v["L1_ffn_W1"], down(v["L1_ffn_W2"])], 2)
    a["w_g"] = v["L1_ffn_Wg"]
    a["w_q"] = np.stack([v["L1_attn_g_wq"], v["L1_attn_l_wq"]], 1).reshape(P, 2, KV, GROUP, HD).swapaxes(2, 3).reshape(P, 2, D)
    a["w_o"] = np.stack([v["L1_attn_g_wo"], v["L1_attn_l_wo"]], 1)
    a["w_kvd"] = v["L1_attn_g_kv_down"]
    a["w_kvu"] = np.concatenate([v["L1_attn_g_k_up"], v["L1_attn_g_v_up"]], 1)
    a["w_kv"] = np.concatenate([v["L1_attn_l_wk"], v["L1_attn_l_wv"]], 1)
    a.update(constants())
    return a


def constants():
    import numpy as np

    key, query = np.arange(P)[:, None], np.arange(P)[None, :]
    hide = lambda seen: np.where(seen, 0.0, MASKED)
    masks = [hide(query >= key), hide((query >= key) & (query - key < WINDOW)), hide(query + P - key < WINDOW)]
    ropes = []
    for base in (1000000.0, 10000.0):
        inv = (1.0 / np.float32(base) ** (np.arange(0, HD, 2, dtype=np.float32) / np.float32(HD))).astype(np.float32)
        angle = np.arange(SEQ, dtype=np.float32)[:, None] * inv[None, :]
        cos = np.repeat(np.cos(angle), 2, 1)
        sin = np.stack([-np.sin(angle), np.sin(angle)], 2).reshape(SEQ, HD)
        ropes.append([np.tile(t, (1, HEADS)).reshape(2, P, D).transpose(1, 0, 2).reshape(P, 2 * D) for t in (cos, sin)])
    tri = np.stack([key <= query, np.ones((P, P))], 1)
    return {
        "masks": np.stack(masks, 1).astype(np.float16),
        "ident16": np.eye(P, dtype=np.float16),
        "rope": np.array(ropes).transpose(2, 0, 1, 3).astype(np.float32),
        "tri": tri.astype(np.float16),
        "iota32": np.arange(1, CAP + 1, dtype=np.float32),
        "iotar": np.arange(EXPERTS, 0, -1, dtype=np.float32),
    }


def kernel(**inputs):
    import numpy as _np
    import concourse.bacc as _bacc
    from concourse import mybir as _mybir
    from concourse.bass_utils import run_bass_kernel_spmd as _run

    nc = _bacc.Bacc("TRN2", target_bir_lowering=False, num_devices=1)
    arrays, args = {}, {}
    for name, a in layouts(inputs).items():
        a = _np.ascontiguousarray(a)
        arrays[f"in_{name}"] = a
        args[name] = nc.dram_tensor(f"in_{name}", a.shape, _mybir.dt.from_np(a.dtype), kind="ExternalInput").ap()
    out = nc.dram_tensor("out", (TOK, D), F32, kind="ExternalOutput").ap()
    build(nc, args, out)
    r = _run(nc, [arrays], core_ids=[0])
    return r.results[0]["out"].reshape(SEQS, SEQ, D)
```

```python
from contextlib import ExitStack

import concourse.bass as bass
from concourse import mybir
from concourse.bass import ds

F32 = mybir.dt.float32
BF16 = mybir.dt.bfloat16
F16 = mybir.dt.float16
U32 = mybir.dt.uint32
ALU = mybir.AluOpType
ACT = mybir.ActivationFunctionType
AX = mybir.AxisListType

P = 128
D = 128
SEQS, SEQ = 8, 256
TOK = SEQS * SEQ
TILES = TOK // P
INNER = 256
HALVES = INNER // P
STATES = 16
RANK = 8
TAPS = 4
LN_EPS = 1e-5
RMS_EPS = 1e-6
EXPERTS = 8
HIDDEN = 512
CHUNKS = HIDDEN // P
HEADS, KV, HD = 16, 4, 8
GROUP = HEADS // KV
LAT = 32
WINDOW = 32
VW = 32
CAP = SEQ // EXPERTS

COLS = 512
PAIRS = TOK // COLS
STEPS = 2 * PAIRS
ALL = STEPS * STATES
UNITS = 2 * HALVES
DEEP = 3
DRIVES = 3
B_RING = 4
AHEAD = 3
C_BANKS = 2
PAIRS0 = 2 * SEQS
GROUPS = 2 * SEQS // 2
GT = TILES // 4
QH, KH = GT * HEADS, GT * KV
RING = 4
NPAR = TAPS + 3 + STATES
XROWS = 3 * 2 * STATES + RANK
DT_ROW = 3 * 2 * STATES
PACK = HIDDEN + CHUNKS + HIDDEN
PACK1 = 2 * HIDDEN
MASKED = -30000.0

SIGNALS = [
    "x_loaded0", "x_loaded1", "x_loaded2", "x_loaded3", "consts_loaded", "mamba_weights_loaded", "gate_weights_loaded", "l1_weights_loaded",
    "expert_loaded0", "expert_loaded1", "expert_loaded2", "expert_loaded3", "out_stored",
    "halfconst",
    "spread_ready", "a_ready", "a_exp", "diag_ready", "zero_cols",
    "ln_sum", "ln_centred", "ln_squared", "ln_sum2", "ln_var", "ln_pow", "ln_done", "ln_turned", "ln_copied",
    "side_ready", "side_free",
    "u_copied", "conv_tap", "u_ready", "z_ready", "hi_ready", "mid_ready",
    "bc_part", "bc_ready", "dtr_ready", "dt_abs", "dt_exp", "dt_ln", "dt_ready", "dtu_ready",
    "b_spread", "b_copied", "c_spread", "decay_ready", "drive_ready", "scan_done", "hc_ready", "y_added",
    "gated", "acc_added",
    "pool_mean", "gate_step", "gate_act", "index_ready", "cw_ready",
    "bias_ready", "moe_bias", "e0_up", "e0_gelu", "e0_down", "e0_added", "ln0_step", "ln0_var", "ln0_pow", "ln0_added",
    "x1_ready", "r_pe", "r_dve", "r_act", "slots_spread", "slots_copied", "e_up", "e_gelu", "e_down",
    "e_out", "e_turn", "e_turned", "e_comb", "e_added", "d_turn", "d_turned",
    "rms_sq", "rms_sum", "rms_var", "rms_pow", "rms_done", "prep_ready", "prep_free",
    "rope_a", "roped", "v_ready", "qk_sq", "qk_sum", "qk_var", "qk_ln", "qk_inv", "qk_normed", "qk_hi", "qk_split",
    "turn_q", "turn_copied", "scores_ready", "probs_ready", "av_done", "den_done",
    "ones_ready", "av_copied", "out_ready",
]


def timeline():
    def events(words):
        names = [word.rstrip("0123456789") for word in words.split()]
        return [(name, *(int(c) for c in word[len(name):])) for name, word in zip(names, words.split())]

    order = events("A00 S00 A01 S01 B00 A02 S02 B01 C00 A03 S03 B02 C01 T00 B03 C02 T01 C03 T02 T03 "
                   "gate0 gate1 gate2 bias up0")
    readers = list(order)
    tensor = {5: "T10", 6: "u00 T11", 7: "u01 T12", 8: "z00 T13", 9: "z01", 11: "x0", 13: "dt00", 15: "dt01"}
    others = {0: "A10 A11", 1: "A12 A13", 2: "S10 S11", 3: "S12 S13 B10 B11", 4: "C10 C11 B12 B13", 5: "T10 C12 C13",
              6: "u00 T11", 7: "u01 T12", 8: "z00 T13", 9: "z01", 10: "setup", 11: "x0", 12: "mid0", 13: "dt00"}
    for p in range(PAIRS0):
        if p + 1 < PAIRS0:
            order.append(("up", p + 1))
        order += events(tensor.get(p, "")) + [("down", p)]
        readers.append(("hidden", p))
        if p == PAIRS0 - 1:
            readers += events("dt01 rates")
        readers += [("down", p)] + events(others.get(p, ""))
    start = len(order)
    for g in range(STEPS):
        slots = {}
        if g:
            slots[7] = ("finish", g - 1)
        if g + 1 < STEPS:
            slots.update({0: ("u", g + 1, 0), 2: ("u", g + 1, 1), 5: ("z", g + 1, 0), 6: ("z", g + 1, 1), 9: ("x", g + 1),
                          10: ("mid", g + 1), 11: ("dt", g + 1, 0), 13: ("dt", g + 1, 1)})
        for j in range(STATES):
            order.append(("spread", g * STATES + j))
            if j in slots:
                order.append(slots[j])
            order.append(("state", g * STATES + j))
    order += [("end",)] + [("finish", STEPS - 1)] + events("T20 T21 T22 T23")
    rest = [ev for ev in order[start:] if ev[0] != "spread"]
    k = 0
    while k + 1 < len(rest):
        if rest[k][0] != "state" and rest[k + 1][0] == "state":
            rest[k], rest[k + 1] = rest[k + 1], rest[k]
            k += 1
        k += 1
    last = rest.index(("end",))
    rest[last:] = events("A20 S20 A21 S21") + [("end",)] + events("A22 B20 C20 S22 B21 C21") + \
        [("finish", STEPS - 1)] + events("T20 A23 S23 T21 B22 C22 T22 B23 C23 T23")
    return order, readers + rest


ORDER, READERS = timeline()
STAGE = {kind: {ev: n for n, ev in enumerate(ev for ev in (ORDER if kind == "T" else READERS) if ev[0] == kind)}
         for kind in "ASBCT"}
SIDE = {ev: n for n, ev in enumerate(ev for ev in ORDER if ev[0] in ("gate", "u", "z", "x", "dt", "finish"))}


def attention_timeline():
    slots = {}

    def put(at, *ev):
        slots.setdefault(at, []).append(ev)

    for b in range(2 * SEQS):
        for part, at in enumerate((-3, -2, 0)):
            put(6 * b + at, "turn", b, part)
        for n, at in ((2 * b, 4), (2 * b + 1, 8)):
            put(6 * b + at + 3, "back", n)
            put(6 * b + at, "copy", n)
    for G in range(GROUPS):
        for name, at in (("rms", -17), ("T", -14), ("L", -12), ("Q", -11), ("K", -9), ("sqr", -8), ("inv", -7), ("split", -6),
                         ("O1", 19), ("O2", 21)):
            if name != "L" or G < GROUPS // 2:
                put(12 * G + at, name, G)
    order, readers = [], []
    for at in range(min(slots), max(slots) + 1):
        here = slots.get(at, [])
        unit = [("unit", at)] if 0 <= at < UNITS1 else []
        if at % 2 and 1 < at <= UNITS1 + 1:
            unit.append(("average", at // 2 - 1))
        first = [ev for ev in here if ev[0] == "turn"]
        order += here + unit
        readers += first + unit + [ev for ev in here if ev[0] != "turn"]
    return order, readers


BLOCKS = ((0, 0), (1, 1), (0, 1))
UNITS1 = 2 * SEQS * len(BLOCKS) * KV // 2
AT_ORDER, AT_READERS = attention_timeline()
FILL = AT_READERS[:AT_READERS.index(("unit", 0))]
assert set(FILL) == set(AT_ORDER[:len(FILL)])
AT_ORDER, AT_READERS = AT_ORDER[len(FILL):], AT_READERS[len(FILL):]
LATER = FILL[4:]
FILL_AT = {e: LATER[2 * (e - 1):2 * e if e < EXPERTS - 1 else None] for e in range(1, EXPERTS)}
TURN = {ev: n for n, ev in enumerate(ev for ev in FILL + AT_ORDER if ev[0] in ("turn", "back"))}
PREP = {ev: n for n, ev in enumerate(ev for ev in FILL + AT_ORDER if ev[0] in ("T", "L", "Q", "K", "O1", "O2"))}


def build(nc, a, out):
    with ExitStack() as ctx:
        def sb(name, shape, dt=F32):
            return ctx.enter_context(nc.sbuf_tensor(name, shape, dt))

        sem = {name: ctx.enter_context(nc.semaphore(name)) for name in SIGNALS}

        ps = ctx.enter_context(nc.psum_tensor("ps", [P, 8, 512], F32))

        x_sb = sb("x_sb", [P, TILES, D])
        xn = sb("xn", [P, TILES, D])
        xm = sb("xm", [P, TILES, D])
        sq = sb("sq", [P, TILES, D])
        xnT = sb("xnT", [P, TOK])
        xmT = sb("xmT", [P, TOK])
        acc = sb("acc", [P, TILES, D])
        moe = sb("moe", [P, TILES, D])
        stat = sb("stat", [P, 4, TILES])
        halfc = sb("halfc", [P, TILES])
        ident = sb("ident", [P, P])
        cols = sb("cols", [P, 4])
        par = sb("par", [P, 2, HALVES, NPAR])
        diagD = sb("diagD", [P, 2, HALVES, P])
        spread_w = sb("spread", [96, 2 * STATES], BF16)
        spreadf = sb("spreadf", [96, 2 * STATES])
        negA = sb("negA", [P, 2, HALVES, STATES])

        l0 = ExitStack()

        def sb(name, shape, dt=F32):
            return l0.enter_context(nc.sbuf_tensor(name, shape, dt))

        w_in = sb("w_in", [P, 2, 2 * INNER])
        w_x = sb("w_x", [P, 2, HALVES, XROWS])
        w_dt = sb("w_dt", [P, 2, INNER])
        u_raw = sb("u_raw", [P, HALVES, COLS])
        conv = sb("conv", [P, HALVES, COLS])
        w_out = sb("w_out", [P, 2, HALVES, D])

        u_s = sb("u_s", [P, 2, HALVES, COLS])
        z_s = sb("z_s", [P, 2, HALVES, COLS])
        dt = sb("dt", [P, 2, HALVES, COLS])
        dtu = sb("dtu", [P, 2, HALVES, COLS])
        dt_a = sb("dt_a", [P, COLS])
        dt_b = sb("dt_b", [P, COLS])
        dtr = sb("dtr", [P, COLS])
        bc = sb("bc", [96, 2, COLS], BF16)
        bc_rest = sb("bc_rest", [96, COLS])
        bc_mid = sb("bc_mid", [96, COLS], BF16)
        b_sb = sb("b_sb", [P, B_RING, COLS])

        w_r = sb("w_r", [P, EXPERTS])
        br = sb("br", [SEQS, EXPERTS])
        b2 = sb("b2", [EXPERTS, D])
        gb = sb("gb", [P, 2, D])
        small = sb("small", [SEQS, 16, EXPERTS])
        iota8 = sb("iota8", [SEQS, EXPERTS])
        pooled = sb("pooled", [P, SEQS])
        index = sb("index", [SEQS, EXPERTS], U32)
        ones8 = sb("ones8", [SEQS, P])
        cwT = sb("cwT", [EXPERTS, SEQS])
        wdiag = sb("wdiag", [SEQS, SEQS, 2])
        cw = sb("cw", [P, 2 * SEQS])
        seqstat = sb("seqstat", [P, 2, 4, 2])
        e0 = ExitStack()
        wbuf = e0.enter_context(nc.sbuf_tensor("wbuf", [P, RING, PACK], F32))
        hT = e0.enter_context(nc.sbuf_tensor("hT", [P, 2, CHUNKS, SEQ], F32))
        e0.close()
        drive = sb("drive", [P, DRIVES * HALVES, COLS])
        decay = sb("decay", [P, DEEP * HALVES, COLS])
        h = sb("h", [P, UNITS, COLS])
        hc = sb("hc", [P, DEEP * HALVES, COLS])
        yg = sb("yg", [P, HALVES, COLS])

        l0.close()

        def sb(name, shape, dt=F32):
            return ctx.enter_context(nc.sbuf_tensor(name, shape, dt))

        rope = sb("rope", [P, 2, 2, 2 * D])
        rope_k = sb("rope_k", [P, 2, 2, GT * KV * HD])
        masks = sb("masks", [P, 3, P], F16)
        ident16 = sb("ident16", [P, P], F16)
        w_q = sb("w_q", [P, 2, D])
        w_kvd = sb("w_kvd", [P, LAT])
        w_kvu = sb("w_kvu", [LAT, 2 * KV * HD])
        w_kv = sb("w_kv", [P, 2 * KV * HD])
        w_o = sb("w_o", [P, 2, D])
        w_g = sb("w_g", [P, EXPERTS])
        tri = sb("tri", [P, 2, P], F16)
        iota32 = sb("iota32", [P, CAP])
        iotar = sb("iotar", [P, EXPERTS])
        qk = sb("qk", [P, 2, QH + KH, HD])
        rot = sb("rot", [P, 2, (QH + KH) * HD])
        qk_sqr = sb("qk_sqr", [P, (QH + KH) * HD])
        norm = sb("norm", [P, 4, QH + KH])
        qs = sb("qs", [P, 2, QH, 4, HD], F16)
        ks = sb("ks", [P, 2, KH, 4, HD], F16)
        qT = sb("qT", [P, 2, GROUP, SEQ], F16)
        kT = sb("kT", [P, 2, SEQ], F16)
        v_ring = sb("v_ring", [P, 2, GT, KV, VW])
        avT = sb("avT", [P, 2, COLS])
        den = sb("den", [P, 2, HEADS])
        latT = sb("latT", [LAT, TOK])
        route = sb("route", [P, 6, TILES, EXPERTS])
        rstat = sb("rstat", [P, 4, TILES])
        mask16 = sb("mask16", [P, TILES, EXPERTS], F16)
        slot = sb("slot", [P, TILES, EXPERTS, CAP])
        slotT = sb("slotT", [P, 2, TILES, P])
        xe = sb("xe", [P, SEQS, EXPERTS, CAP])
        eo = slot[:].rearrange("p t e c -> p (t e c)")[:, 0:SEQS * 2 * D].rearrange("p (b s d) -> p b s d", b=SEQS, s=2)
        probs = sb("probs", [P, 3, KV, COLS])
        wbuf1 = sb("wbuf1", [P, RING, PACK1])
        hT1 = probs[:].rearrange("p n g c -> p (n g c)")[:, 0:2 * CHUNKS * SEQ].rearrange("p (r c n) -> p r c n", r=2, c=CHUNKS)
        heads = moe

        B_BANK, C_BANK, Y_BANK, SIDE_BANK = 0, 1, 3, 7
        PREP_BANK, TURN_BANK, AV_BANK = 6, 7, 4
        BACK_BANK = TURN_BANK
        side = ps[:, SIDE_BANK, :]

        block = ctx.enter_context(nc.Block())

        def after(eng, name, count):
            if not (isinstance(count, int) and count <= 0):
                eng.wait_ge(sem[name], count)

        def seqs(t):
            return t.rearrange("p (b t) -> p b t", t=SEQ)

        @block.sync
        def _(sp):
            for k in range(4):
                rows = slice(4 * k, 4 * k + 4)
                sp.dma_start(x_sb[:, rows], a["x"].rearrange("(t p) d -> p t d", p=P)[:, rows]) \
                    .then_inc(sem[f"x_loaded{k}"], 16)
            sp.dma_start(ident[:], a["ident"]).then_inc(sem["consts_loaded"], 16)
            sp.dma_start(cols[:], a["cols"]).then_inc(sem["consts_loaded"], 16)
            sp.dma_start(par[:], a["par"]).then_inc(sem["consts_loaded"], 16)
            sp.dma_start(w_in[:], a["w_in"]).then_inc(sem["mamba_weights_loaded"], 16)
            sp.dma_start(w_x[:], a["w_x"]).then_inc(sem["mamba_weights_loaded"], 16)
            sp.dma_start(w_dt[DT_ROW:DT_ROW + RANK], a["w_dt"]).then_inc(sem["mamba_weights_loaded"], 16)
            sp.dma_start(w_out[:], a["w_out"]).then_inc(sem["mamba_weights_loaded"], 16)
            sp.dma_start(w_r[:], a["w_r"]).then_inc(sem["gate_weights_loaded"], 16)
            sp.dma_start(br[:], a["br"].partition_broadcast(SEQS)).then_inc(sem["gate_weights_loaded"], 16)
            sp.dma_start(b2[:], a["b2"]).then_inc(sem["gate_weights_loaded"], 16)
            sp.dma_start(iota8[:], a["iota8"].partition_broadcast(SEQS)).then_inc(sem["gate_weights_loaded"], 16)
            sp.dma_start(gb[:, 0], a["gamma"].partition_broadcast(P)).then_inc(sem["gate_weights_loaded"], 16)
            sp.dma_start(gb[:, 1], a["beta"].partition_broadcast(P)).then_inc(sem["gate_weights_loaded"], 16)
            sp.wait_ge(sem["index_ready"], 1)
            for p in range(PAIRS0):
                after(sp, "e0_down", p - RING + 1)
                e = sp.value_load(index[p // 2:p // 2 + 1, p % 2:p % 2 + 1], min_val=0, max_val=EXPERTS - 1)
                sp.dma_start(wbuf[:, p % RING], a["pack0"][ds(e, 1)].rearrange("e p n -> p (e n)")) \
                    .then_inc(sem[f"expert_loaded{p % RING}"], 16)
            sp.wait_ge(sem["side_free"], SIDE["dt", STEPS - 1, 1] + 1)
            for dst, name in ((rope, "rope"), (rope_k, "rope_k"), (masks, "masks"), (ident16, "ident16"), (w_q, "w_q"), (w_kvd, "w_kvd"),
                              (w_kvu, "w_kvu"), (w_kv, "w_kv"), (w_o, "w_o"), (w_g, "w_g"), (tri, "tri")):
                sp.dma_start(dst[:], a[name]).then_inc(sem["l1_weights_loaded"], 16)
            sp.dma_start(iota32[:], a["iota32"].partition_broadcast(P)).then_inc(sem["l1_weights_loaded"], 16)
            sp.dma_start(iotar[:], a["iotar"].partition_broadcast(P)).then_inc(sem["l1_weights_loaded"], 16)
            for e in range(EXPERTS):
                after(sp, "e_down", e - RING + 1)
                sp.dma_start(wbuf1[:, e % RING], a["pack1"][e]).then_inc(sem[f"expert_loaded{e % RING}"], 16)
            for k in range(4):
                rows = slice(4 * k, 4 * k + 4)
                sp.wait_ge(sem["out_ready"], k + 1)
                sp.dma_start(out.rearrange("(t p) d -> p t d", p=P)[:, rows], x_sb[:, rows]).then_inc(sem["out_stored"], 16)
            sp.wait_ge(sem["out_stored"], 4 * 16)

        @block.gpsimd
        def _(pool):
            pool.memset(halfc[:], -0.5).then_inc(sem["halfconst"], 1)
            pool.memset(ones8[:], 1.0).then_inc(sem["halfconst"], 1)
            pool.wait_ge(sem["halfconst"], 2)

            def drive_state(N):
                for half in range(HALVES):
                    after(pool, "b_copied", N + 1)
                    after(pool, "scan_done", 2 * (N - DRIVES) + half + 1)
                    pool.tensor_tensor(drive[:, 2 * (N % DRIVES) + half], dtu[:, N // STATES % 2, half], b_sb[:, N % B_RING], ALU.mult) \
                        .then_inc(sem["drive_ready"], 1)

            for ev in READERS:
                if ev[0] == "B":
                    rows = slice(4 * ev[2], 4 * ev[2] + 4)
                    pool.wait_ge(sem["ln_var"], STAGE["B"][ev] + 1)
                    pool.tensor_tensor(stat[:, 3, rows], stat[:, 2, rows], halfc[:, rows], ALU.pow).then_inc(sem["ln_pow"], 1)
                elif ev[:2] == ("C", 2):
                    rows = slice(4 * ev[2], 4 * ev[2] + 4)
                    pool.wait_ge(sem["ln_pow"], STAGE["B"]["B", 2, ev[2]] + 1)
                    pool.wait_ge(sem["ln_centred"], STAGE["A"]["A", 2, ev[2]] + 1)
                    pool.tensor_tensor(xn[:, rows], xm[:, rows], stat[:, 3, rows].unsqueeze(2).broadcast_to([P, 4, D]), ALU.mult) \
                        .then_inc(sem["ln_done"], 1)
                elif ev[0] == "state":
                    N = ev[1]
                    if N == 0:
                        pool.wait_ge(sem["dtu_ready"], HALVES)
                        pool.wait_ge(sem["e0_down"], PAIRS0)
                        for first in range(DRIVES - 1):
                            drive_state(first)
                    M = N + DRIVES - 1
                    if M < ALL:
                        if M % STATES == 0:
                            pool.wait_ge(sem["dtu_ready"], HALVES * (M // STATES + 1))
                        drive_state(M)
                elif ev[0] == "dt":
                    _, g, half = ev
                    n = HALVES * g + half
                    pool.wait_ge(sem["dt_ready"], n + 1)
                    pool.wait_ge(sem["u_ready"], g + 1)
                    after(pool, "drive_ready", STATES * HALVES * (g - 1))
                    pool.tensor_tensor(dtu[:, g % 2, half], dt[:, g % 2, half], u_s[:, g % 2, half], ALU.mult) \
                        .then_inc(sem["dtu_ready"], 1)
                elif ev[0] == "down" and ev[1] % 2:
                    b = ev[1] // 2
                    pool.wait_ge(sem["ln0_var"], b + 1)
                    pool.tensor_tensor(seqstat[:, b % 2, 3], seqstat[:, b % 2, 2], halfc[:, 0:2], ALU.pow) \
                        .then_inc(sem["ln0_pow"], 1)
            pool.wait_ge(sem["ln_done"], STAGE["C"]["C", 2, 3] + 1)
            pool.memset(v_ring[:], 0.0).then_inc(sem["ones_ready"], 1)
            pool.wait_ge(sem["ones_ready"], 1)
            pool.memset(v_ring[:, :, :, :, HD:HD + 1], 1.0).then_inc(sem["ones_ready"], 1)
            for ev in FILL + AT_READERS:
                if ev[0] == "rms":
                    rows = slice(GT * (ev[1] % 4), GT * (ev[1] % 4 + 1))
                    pool.wait_ge(sem["rms_var"], ev[1] + 1)
                    pool.tensor_tensor(stat[:, 3, rows], stat[:, 2, rows], halfc[:, rows], ALU.pow).then_inc(sem["rms_pow"], 1)

        @block.scalar
        def _(act):
            act.preload_act_table_set("natural_log_exp_and_others")
            def norm_part(ev):
                kind, use, k = ev
                rows, toks = slice(4 * k, 4 * k + 4), slice(k * 512, (k + 1) * 512)
                if kind == "S":
                    act.wait_ge(sem["ln_centred"], STAGE["A"]["A", use, k] + 1)
                    act.activation(sq[:, rows], xm[:, rows], ACT.Square).then_inc(sem["ln_squared"], 1)
                elif kind == "T":
                    act.wait_ge(sem["ln_turned"], STAGE["T"][ev] + 1)
                    if use != 1:
                        act.activation(xnT[:, toks], ps[:, k], ACT.Copy).then_inc(sem["ln_copied"], 1)
                    else:
                        act.activation(xmT[:, toks], ps[:, 6], ACT.Identity,
                                       scale=cols[:, 0:1], bias=cols[:, 1:2]).then_inc(sem["ln_copied"], 1)

            def gelu(p):
                after(act, "e0_down", p - 1)
                for c in range(CHUNKS):
                    act.wait_ge(sem["e0_up"], 2 * p + c // 2 + 1)
                    act.activation(hT[:, p % 2, c], ps[:, 2 * (p % 2) + c // 2, (c % 2) * SEQ:(c % 2 + 1) * SEQ], ACT.Gelu,
                                   bias=wbuf[:, p % RING, HIDDEN + c:HIDDEN + c + 1]).then_inc(sem["e0_gelu"], 1)

            def side_part(ev):
                kind, g, half = (*ev, 0)[:3]
                dr = g // PAIRS
                act.wait_ge(sem["side_ready"], SIDE[ev] + 1)
                if kind == "u":
                    after(act, "conv_tap", 3 * (HALVES * (g - 1) + half + 1))
                    after(act, "u_ready", g)
                    act.activation(u_raw[:, half], side, ACT.Copy).then_inc(sem["u_copied"], 1)
                    act.activation(conv[:, half], side, ACT.Identity, scale=par[:, dr, half, TAPS - 1:TAPS],
                                   bias=par[:, dr, half, TAPS:TAPS + 1]).then_inc(sem["side_free"], 1)
                elif kind == "z" and half == 0:
                    after(act, "gated", HALVES * (g - 1))
                    act.activation(z_s[:, g % 2, 0], side, ACT.Copy).then_inc(sem["side_free"], 1)
                elif kind == "z":
                    act.activation(z_s[:, g % 2, 1], side, ACT.Silu).then_inc(sem["side_free"], 1)
                    act.wait_ge(sem["side_free"], SIDE["z", g, 0] + 1)
                    act.activation(z_s[:, g % 2, 0], z_s[:, g % 2, 0], ACT.Silu).then_inc(sem["z_ready"], 1)
                    act.wait_ge(sem["conv_tap"], 3 * HALVES * (g + 1))
                    act.activation(u_s[:, g % 2], conv[:], ACT.Silu).then_inc(sem["u_ready"], 1)
                    if g:
                        act.preload_act_table_set("natural_log_exp_and_others")
                elif kind == "x":
                    act.activation(dtr[DT_ROW:DT_ROW + RANK], ps[DT_ROW:DT_ROW + RANK, SIDE_BANK], ACT.Copy) \
                        .then_inc(sem["dtr_ready"], 1)
                    after(act, "c_spread", STATES * (g - 1))
                    act.activation(bc[:, g % 2], ps[0:96, SIDE_BANK], ACT.Copy).then_inc(sem["hi_ready"], 1)
                else:
                    n = HALVES * g + half
                    bias = par[:, dr, half, TAPS + 1:TAPS + 2]
                    if g == 0:
                        act.preload_act_table_set("natural_log_exp_and_others")
                    after(act, "dt_ready", n)
                    act.activation(dt_a[:], side, ACT.Abs, bias=bias).then_inc(sem["dt_abs"], 1)
                    act.activation(dt_b[:], side, ACT.Relu, bias=bias).then_inc(sem["side_free"], 1)
                    act.wait_ge(sem["dt_abs"], n + 1)
                    act.activation(dt_a[:], dt_a[:], ACT.Exp, scale=-1.0).then_inc(sem["dt_exp"], 1)
                    act.wait_ge(sem["dt_exp"], n + 1)
                    act.activation(dt_a[:], dt_a[:], ACT.Ln, bias=1.0).then_inc(sem["dt_ln"], 1)

            def mid(g):
                act.wait_ge(sem["side_free"], SIDE["x", g] + 1)
                after(act, "bc_ready", g)
                act.activation(bc_mid[:], bc_rest[:], ACT.Copy).then_inc(sem["mid_ready"], 1)

            def copy_b(N):
                after(act, "b_spread", N + 1)
                after(act, "drive_ready", 2 * (N - B_RING) + 2)
                act.activation(b_sb[:, N % B_RING], ps[:, B_BANK], ACT.Copy).then_inc(sem["b_copied"], 1)

            def state(N):
                g, j = N // STATES, N % STATES
                lo = 0 if g >= PAIRS else 1
                if j == 0:
                    act.wait_ge(sem["dt_ready"], HALVES * (g + 1))
                    act.wait_ge(sem["a_ready"], 1)
                if N == 0:
                    for first in range(AHEAD):
                        copy_b(first)
                for half in range(HALVES):
                    turned = N - PAIRS * STATES
                    if N == 0:
                        act.wait_ge(sem["zero_cols"], 1)
                    elif 0 <= turned < DEEP:
                        act.wait_ge(sem["zero_cols"], 2 + 2 * turned + half)
                    after(act, "scan_done", 2 * (N - DEEP) + half + 1)
                    act.activation(seqs(decay[:, 2 * (N % DEEP) + half])[:, :, lo:lo + SEQ - 1],
                                   seqs(dt[:, g % 2, half])[:, :, lo:lo + SEQ - 1],
                                   ACT.Exp, scale=negA[:, g // PAIRS, half, j:j + 1]).then_inc(sem["decay_ready"], 1)
                    if half == 0 and N + AHEAD < ALL:
                        copy_b(N + AHEAD)

            def gate():
                act.wait_ge(sem["gate_step"], 2)
                act.activation(small[:, 2], small[:, 1], ACT.Exp).then_inc(sem["gate_act"], 1)
                act.wait_ge(sem["gate_step"], 6)
                act.activation(small[:, 9, 0:1], small[:, 8, 0:1], ACT.Exp).then_inc(sem["gate_act"], 1)

            for ev in READERS:
                if ev[0] == "state":
                    state(ev[1])
                elif ev[0] in ("u", "z", "x", "dt"):
                    side_part(ev)
                elif ev[0] in "ASBCT":
                    norm_part(ev)
                elif ev[0] == "mid":
                    mid(ev[1])
                elif ev == ("gate", 0):
                    gate()
                elif ev[0] == "hidden":
                    gelu(ev[1])
                elif ev[0] == "rates":
                    act.wait_ge(sem["consts_loaded"], 48)
                    act.activation(negA[:], par[:, :, :, TAPS + 3:], ACT.Exp).then_inc(sem["a_exp"], 1)
            def prepare(ev):
                kind, G = ev[0], ev[1]
                l, k, r = G // 4, G % 4, G % 2
                cols_k = slice(k * GT * P, (k + 1) * GT * P)
                rows = slice(GT * k, GT * k + GT)
                if kind == "rms":
                    if l:
                        act.wait_ge(sem["prep_free"], PREP["O2", k] + 1)
                    else:
                        act.wait_ge(sem["ln_done"], STAGE["C"]["C", 2, k] + 1)
                    act.activation(sq[:, rows], (acc if l else xn)[:, rows], ACT.Square).then_inc(sem["rms_sq"], 1)
                elif kind == "T":
                    act.wait_ge(sem["prep_ready"], PREP[ev] + 1)
                    act.activation(xmT[:, cols_k], ps[:, PREP_BANK], ACT.Copy, scale=cols[:, 2 + l:3 + l]) \
                        .then_inc(sem["prep_free"], 1)
                elif kind == "L":
                    act.wait_ge(sem["prep_ready"], PREP[ev] + 1)
                    act.activation(latT[:, cols_k], ps[0:LAT, PREP_BANK], ACT.Copy).then_inc(sem["prep_free"], 1)
                elif kind == "K":
                    act.wait_ge(sem["prep_ready"], PREP[ev] + 1)
                    act.wait_ge(sem["ones_ready"], 2)
                    after(act, "av_done", 2 * len(BLOCKS) * (G - 1))
                    act.activation(v_ring[:, r, :, :, 0:HD],
                                   ps[:, PREP_BANK, 0:GT * 2 * KV * HD].rearrange("p (t c) -> p t c", t=GT)[:, :, KV * HD:]
                                   .rearrange("p t (g d) -> p t g d", d=HD), ACT.Copy).then_inc(sem["v_ready"], 1)
                elif kind == "sqr":
                    act.wait_ge(sem["roped"], G + 1)
                    after(act, "qk_sum", G)
                    act.activation(qk_sqr[:], qk[:, r].rearrange("p h d -> p (h d)"), ACT.Square).then_inc(sem["qk_sq"], 1)
                elif kind == "inv":
                    act.wait_ge(sem["qk_var"], G + 1)
                    act.activation(norm[:, 2], norm[:, 1], ACT.Ln).then_inc(sem["qk_ln"], 1)
                    act.wait_ge(sem["qk_ln"], G + 1)
                    after(act, "qk_normed", G)
                    act.activation(norm[:, 3], norm[:, 2], ACT.Exp, scale=-0.5).then_inc(sem["qk_inv"], 1)
                elif kind == "split":
                    act.wait_ge(sem["qk_normed"], G + 1)
                    if G >= 2:
                        act.wait_ge(sem["turn_q"], TURN["turn", 2 * G - 3, 2] + 1)
                    act.activation(qs[:, r, :, 0:2], qk[:, r, 0:QH].unsqueeze(2).broadcast_to([P, QH, 2, HD]), ACT.Copy) \
                        .then_inc(sem["qk_hi"], 1)
                    act.activation(ks[:, r, :, 0::2], qk[:, r, QH:].unsqueeze(2).broadcast_to([P, KH, 2, HD]), ACT.Copy) \
                        .then_inc(sem["qk_hi"], 1)
                elif kind == "O1":
                    act.wait_ge(sem["prep_ready"], PREP[ev] + 1)
                    act.activation(xmT[:, cols_k], ps[:, PREP_BANK], ACT.Copy).then_inc(sem["prep_free"], 1)

            prepare(("rms", 0))
            prepare(("T", 0))
            act.wait_ge(sem["r_dve"], 2)
            act.activation(route[:, 1], route[:, 0], ACT.Exp).then_inc(sem["r_act"], 1)
            prepare(("L", 0))
            for k in range(4):
                act.wait_ge(sem["slots_spread"], k + 1)
                act.activation(xe[:, 2 * k:2 * k + 2].rearrange("p b e c -> p (b e c)"), ps[:, k], ACT.Copy) \
                    .then_inc(sem["slots_copied"], 1)
            for e in range(EXPERTS):
                for c in range(CHUNKS):
                    act.wait_ge(sem["e_up"], 2 * e + c // 2 + 1)
                    if c == 0:
                        after(act, "e_down", e - 1)
                    act.activation(hT1[:, e % 2, c], ps[:, 2 * (e % 2) + c // 2, (c % 2) * SEQ:(c % 2 + 1) * SEQ],
                                   ACT.Gelu_apprx_tanh).then_inc(sem["e_gelu"], 1)
                for ev in FILL_AT.get(e, ()):
                    if ev[0] != "turn":
                        prepare(ev)
            act.preload_act_table_set("natural_log_exp_and_others")
            for k in range(4):
                act.wait_ge(sem["e_turn"], k + 1)
                act.wait_ge(sem["d_turned"], 8)
                act.activation(eo[:, 2 * k:2 * k + 2].rearrange("p b s d -> p (b s d)"), ps[:, k], ACT.Copy) \
                    .then_inc(sem["e_turned"], 1)

            def exps(U):
                t = U // 2
                heads_u = slice(2 * (U % 2), 2 * (U % 2) + 2)
                act.wait_ge(sem["scores_ready"], U + 1)
                after(act, "av_done", t - 2)
                if t >= 3 * SEQS and BLOCKS[t % 3] == (0, 1):
                    keys, width = slice(P - WINDOW, P), GROUP * WINDOW
                else:
                    keys, width = slice(0, P), COLS
                act.activation(probs[keys, t % 3, heads_u, 0:width], ps[keys, heads_u, 0:width], ACT.Exp,
                               scale=HD ** -0.5).then_inc(sem["probs_ready"], 1)

            def copy_av(n):
                act.wait_ge(sem["av_done"], 3 * (n // 2) + (3 if n % 2 else 1))
                if n >= 2:
                    act.wait_ge(sem["turn_q"], TURN["back", n - 2] + 1)
                act.activation(avT[:, n % 2], ps[:, AV_BANK + n % 2], ACT.Copy).then_inc(sem["av_copied"], 1)

            for ev in AT_READERS:
                if ev[0] == "unit":
                    exps(ev[1])
                elif ev[0] == "copy":
                    copy_av(ev[1])
                elif ev[0] not in ("turn", "back", "average"):
                    prepare(ev)

        @block.vector
        def _(dve):
            def setup():
                dve.wait_ge(sem["consts_loaded"], 48)
                dve.tensor_tensor(spreadf[:], ident[0:96, 0:32], ident[0:96, 32:64], ALU.add).then_inc(sem["spread_ready"], 1)
                dve.wait_ge(sem["spread_ready"], 1)
                dve.tensor_tensor(spread_w[:], spreadf[:], ident[0:96, 64:96], ALU.add).then_inc(sem["spread_ready"], 1)
                for dr in range(2):
                    for half in range(HALVES):
                        dve.tensor_scalar(diagD[:, dr, half], ident[:], par[:, dr, half, TAPS + 2:TAPS + 3], None,
                                          ALU.mult).then_inc(sem["diag_ready"], 1)

            def rates():
                dve.wait_ge(sem["a_exp"], 1)
                dve.tensor_scalar(negA[:], negA[:], -1.0, None, ALU.mult).then_inc(sem["a_ready"], 1)
                dve.wait_ge(sem["e0_down"], PAIRS0)
                zero_boundary(slice(0, DEEP * HALVES), 0)

            def norm_part(ev):
                kind, use, k = ev
                n = STAGE[kind][ev]
                rows = slice(4 * k, 4 * k + 4)
                src, dst = ((x_sb, xn), (xn, xm), (x_sb, xn))[use]

                def over(t):
                    return t.unsqueeze(2).broadcast_to([P, 4, D])

                if kind == "A":
                    if use == 0:
                        dve.wait_ge(sem[f"x_loaded{k}"], 16)
                    elif use == 1:
                        dve.wait_ge(sem["ln_done"], STAGE["C"]["C", 0, k] + 1)
                    else:
                        dve.wait_ge(sem["side_free"], SIDE["finish", PAIRS + k] + 1)
                    dve.tensor_reduce(stat[:, 0, rows], src[:, rows], AX.X, ALU.add).then_inc(sem["ln_sum"], 1)
                    dve.wait_ge(sem["ln_sum"], 2 * n + 1)
                    dve.tensor_scalar(stat[:, 1, rows], stat[:, 0, rows], 1.0 / D, None, ALU.mult).then_inc(sem["ln_sum"], 1)
                    dve.wait_ge(sem["ln_sum"], 2 * n + 2)
                    dve.tensor_tensor(xm[:, rows], src[:, rows], over(stat[:, 1, rows]), ALU.subtract) \
                        .then_inc(sem["ln_centred"], 1)
                elif kind == "B":
                    dve.wait_ge(sem["ln_squared"], STAGE["S"]["S", use, k] + 1)
                    dve.tensor_reduce(stat[:, 0, rows], sq[:, rows], AX.X, ALU.add).then_inc(sem["ln_sum2"], 1)
                    dve.wait_ge(sem["ln_sum2"], n + 1)
                    dve.tensor_scalar(stat[:, 2, rows], stat[:, 0, rows], 1.0 / D, LN_EPS, ALU.mult, ALU.add) \
                        .then_inc(sem["ln_var"], 1)
                elif kind == "C" and use < 2:
                    dve.wait_ge(sem["ln_pow"], STAGE["B"]["B", use, k] + 1)
                    dve.wait_ge(sem["ln_centred"], STAGE["A"]["A", use, k] + 1)
                    dve.tensor_tensor(dst[:, rows], xm[:, rows], over(stat[:, 3, rows]), ALU.mult).then_inc(sem["ln_done"], 1)
                elif kind == "T" and use == 0:
                    dve.wait_ge(sem["ln_copied"], STAGE["T"][ev] + 1)
                    dve.tensor_reduce(pooled[:, 2 * k:2 * k + 2], seqs(xnT[:, k * 512:(k + 1) * 512]), AX.X, ALU.add) \
                        .then_inc(sem["pool_mean"], 1)

            def side_part(ev):
                kind, g, half = (*ev, 0)[:3]
                dr = g // PAIRS
                if kind == "u":
                    n = HALVES * g + half
                    dve.wait_ge(sem["u_copied"], n + 1)
                    dve.wait_ge(sem["side_free"], SIDE[ev] + 1)
                    for k in range(1, TAPS):
                        if dr == 0:
                            to, of = slice(k, SEQ), slice(0, SEQ - k)
                        else:
                            to, of = slice(0, SEQ - k), slice(k, SEQ)
                        c = seqs(conv[:, half])[:, :, to]
                        after(dve, "conv_tap", 3 * n + k - 1)
                        dve.scalar_tensor_tensor(out=c, in0=seqs(u_raw[:, half])[:, :, of],
                                                 scalar=par[:, dr, half, TAPS - 1 - k:TAPS - k], in1=c,
                                                 op0=ALU.mult, op1=ALU.add).then_inc(sem["conv_tap"], 1)
                elif kind == "x":
                    dve.wait_ge(sem["hi_ready"], g + 1)
                    dve.tensor_tensor(bc_rest[:], ps[0:96, SIDE_BANK], bc[:, g % 2], ALU.subtract) \
                        .then_inc(sem["side_free"], 1)
                elif kind == "mid":
                    dve.wait_ge(sem["mid_ready"], g + 1)
                    dve.tensor_copy(bc[32:64, g % 2], bc_mid[32:64]).then_inc(sem["bc_part"], 1)
                    dve.tensor_tensor(bc[64:96, g % 2], bc_rest[64:96], bc_mid[64:96], ALU.subtract) \
                        .then_inc(sem["bc_ready"], 1)
                elif kind == "dt":
                    dve.wait_ge(sem["dt_ln"], HALVES * g + half + 1)
                    after(dve, "decay_ready", STATES * HALVES * (g - 1))
                    dve.tensor_tensor(dt[:, g % 2, half], dt_a[:], dt_b[:], ALU.add).then_inc(sem["dt_ready"], 1)

            def scan(N, half):
                q = 2 * N + half
                k = 2 * (N % 2) + half
                dve.wait_ge(sem["decay_ready"], q + 1)
                dve.wait_ge(sem["drive_ready"], q + 1)
                after(dve, "hc_ready", q - UNITS + 1)
                turn = slice(None, None, -1) if N // STATES >= PAIRS else slice(None)
                dve.tensor_tensor_scan(h[:, k, turn], decay[:, 2 * (N % DEEP) + half, turn], drive[:, 2 * (N % DRIVES) + half, turn], 0.0,
                                       ALU.mult, ALU.add).then_inc(sem["scan_done"], 1)

            def times_c(N, half):
                q = 2 * N + half
                k = 2 * (N % 2) + half
                dve.wait_ge(sem["scan_done"], q + 1)
                dve.wait_ge(sem["c_spread"], N + 1)
                after(dve, "y_added", q - DEEP * HALVES + 1)
                dve.tensor_tensor(hc[:, 2 * (N % DEEP) + half], h[:, k], ps[:, C_BANK + N % C_BANKS], ALU.mult).then_inc(sem["hc_ready"], 1)

            def zero_boundary(slots, col):
                dve.memset(decay[:, slots].rearrange("p k (b t) -> p k b t", t=SEQ)[:, :, :, col:col + 1], 0.0) \
                    .then_inc(sem["zero_cols"], 1)

            def state(N):
                if N == 0:
                    dve.wait_ge(sem["zero_cols"], 1)
                last = PAIRS * STATES - DEEP <= N < PAIRS * STATES
                scan(N, 0)
                if N:
                    times_c(N - 1, 1)
                if N > STATES and N % STATES == 4:
                    gate_y(N // STATES - 1)
                scan(N, 1)
                for half in range(HALVES):
                    if last:
                        dve.wait_ge(sem["scan_done"], 2 * N + half + 1)
                        zero_boundary(slice(2 * (N % DEEP) + half, 2 * (N % DEEP) + half + 1), SEQ - 1)
                times_c(N, 0)

            def gate_y(g):
                for half in range(HALVES):
                    dve.wait_ge(sem["y_added"], STATES * HALVES * (g + 1) - 1 + half)
                    if g:
                        dve.wait_ge(sem["side_ready"], SIDE["finish", g - 1] + 1)
                    dve.tensor_tensor(yg[:, half], ps[:, Y_BANK + 2 * (g % 2) + half], z_s[:, g % 2, half], ALU.mult) \
                        .then_inc(sem["gated"], 1)

            def finish(ev):
                g = ev[1]
                rows = slice(4 * (g % PAIRS), 4 * (g % PAIRS) + 4)
                dve.wait_ge(sem["side_ready"], SIDE[ev] + 1)
                if g >= PAIRS:
                    dve.wait_ge(sem["side_free"], SIDE["finish", g - PAIRS] + 1)
                else:
                    dve.wait_ge(sem["ln0_added"], SEQS)
                dve.tensor_tensor((x_sb if g >= PAIRS else acc)[:, rows], acc[:, rows],
                                  side.rearrange("p (t d) -> p t d", d=D), ALU.add).then_inc(sem["side_free"], 1)

            def gate():
                step = [0]

                def link(ins):
                    step[0] += 1
                    ins.then_inc(sem["gate_step"], 1)
                    dve.wait_ge(sem["gate_step"], step[0])

                s = small
                dve.wait_ge(sem["gate_weights_loaded"], 96)
                dve.wait_ge(sem["side_ready"], SIDE["gate", 0] + 1)
                dve.scalar_tensor_tensor(out=s[:, 0], in0=side[0:SEQS, 0:EXPERTS], scalar=1.0 / SEQ, in1=br[:],
                                         op0=ALU.mult, op1=ALU.add).then_inc(sem["side_free"], 1)
                dve.wait_ge(sem["side_free"], SIDE["gate", 0] + 1)
                link(dve.tensor_reduce(s[:, 3, 0:1], s[:, 0], AX.X, ALU.max))
                link(dve.tensor_scalar(s[:, 1], s[:, 0], s[:, 3, 0:1], None, ALU.subtract))
                dve.wait_ge(sem["gate_act"], 1)
                link(dve.tensor_reduce(s[:, 3, 1:2], s[:, 2], AX.X, ALU.add))
                link(dve.reciprocal(s[:, 3, 2:3], s[:, 3, 1:2]))
                link(dve.tensor_scalar(s[:, 4], s[:, 2], s[:, 3, 2:3], None, ALU.mult))
                dve.max(s[:, 5], s[:, 4]).then_inc(sem["cw_ready"], 1)
                dve.wait_ge(sem["cw_ready"], 1)
                link(dve.tensor_tensor(s[:, 8, 0:1], s[:, 5, 1:2], s[:, 5, 0:1], ALU.subtract))
                dve.max_index(index[:], s[:, 5], s[:, 4]).then_inc(sem["index_ready"], 1)
                dve.wait_ge(sem["index_ready"], 1)
                link(dve.tensor_copy(s[:, 6], index[:]))
                dve.wait_ge(sem["gate_act"], 2)
                link(dve.tensor_scalar(s[:, 10, 0:1], s[:, 9, 0:1], 1.0, None, ALU.add))
                link(dve.reciprocal(s[:, 11, 0:1], s[:, 10, 0:1]))
                link(dve.tensor_tensor(s[:, 11, 1:2], s[:, 11, 0:1], s[:, 9, 0:1], ALU.mult))
                for k in range(2):
                    link(dve.tensor_scalar(s[:, 12 + k], iota8[:], s[:, 6, k:k + 1], s[:, 11, k:k + 1],
                                           ALU.is_equal, ALU.mult))
                link(dve.tensor_tensor(s[:, 14], s[:, 12], s[:, 13], ALU.add))
                link(dve.tensor_tensor(wdiag[:], ident[0:SEQS, 0:SEQS].unsqueeze(2).broadcast_to([SEQS, SEQS, 2]),
                                       s[:, 11, 0:2].unsqueeze(1).broadcast_to([SEQS, SEQS, 2]), ALU.mult))
                assert step[0] == 14

            def gate_copy(k):
                dve.wait_ge(sem["side_ready"], SIDE["gate", k] + 1)
                if k == 1:
                    dve.tensor_copy(cwT[:], side[0:EXPERTS, 0:SEQS]).then_inc(sem["side_free"], 1)
                else:
                    dve.tensor_copy(cw[:], side[:, 0:2 * SEQS]).then_inc(sem["side_free"], 1)

            def bias():
                dve.wait_ge(sem["ln_done"], 4)
                dve.tensor_tensor(acc[:], x_sb[:], xn[:], ALU.add).then_inc(sem["acc_added"], 1)
                dve.wait_ge(sem["side_free"], SIDE["gate", 2] + 1)
                dve.wait_ge(sem["acc_added"], 1)
                dve.wait_ge(sem["bias_ready"], 1)
                for k in range(2):
                    rows = slice(8 * k, 8 * k + 8)
                    dve.tensor_tensor(moe[:, rows].rearrange("p (b two) d -> p b two d", two=2),
                                      xn[:, rows].rearrange("p (b two) d -> p b two d", two=2),
                                      ps[:, 4 + k].rearrange("p (b d) -> p b d", d=D).unsqueeze(2).broadcast_to([P, 4, 2, D]),
                                      ALU.add).then_inc(sem["moe_bias"], 1)
                dve.wait_ge(sem["moe_bias"], 2)

            def pair(p):
                b, k = p // 2, p % 2
                r = b % 2
                rows = moe[:, 2 * b:2 * b + 2]
                m, c = (yg[:, r, n * SEQ:(n + 1) * SEQ].rearrange("p (t d) -> p t d", d=D) for n in range(2))
                q = dt[:, 1, r, 0:SEQ].rearrange("p (t d) -> p t d", d=D)
                dve.wait_ge(sem["e0_down"], p + 1)
                after(dve, "e0_added", p)
                dve.scalar_tensor_tensor(out=m if k else rows, in0=ps[:, 4 + k, 0:2 * D].rearrange("p (t d) -> p t d", d=D),
                                         scalar=cw[:, p:p + 1], in1=rows, op0=ALU.mult, op1=ALU.add) \
                    .then_inc(sem["e0_added"], 1)
                if k == 0:
                    return
                st = seqstat[:, r]

                def over(t):
                    return t.unsqueeze(2).broadcast_to([P, 2, D])

                def link(k, ins):
                    ins.then_inc(sem["ln0_step"], 1)
                    dve.wait_ge(sem["ln0_step"], 8 * b + k)

                dve.wait_ge(sem["e0_added"], p + 1)
                link(1, dve.tensor_reduce(st[:, 0], m, AX.X, ALU.add))
                link(2, dve.tensor_scalar(st[:, 1], st[:, 0], 1.0 / D, None, ALU.mult))
                link(3, dve.tensor_tensor(c, m, over(st[:, 1]), ALU.subtract))
                link(4, dve.tensor_tensor(q, c, c, ALU.mult))
                link(5, dve.tensor_reduce(st[:, 0], q, AX.X, ALU.add))
                dve.tensor_scalar(st[:, 2], st[:, 0], 1.0 / D, LN_EPS, ALU.mult, ALU.add).then_inc(sem["ln0_var"], 1)
                dve.wait_ge(sem["ln0_pow"], b + 1)
                link(6, dve.tensor_tensor(c, c, over(st[:, 3]), ALU.mult))
                link(7, dve.tensor_tensor(c, c, gb[:, 0].unsqueeze(1).broadcast_to([P, 2, D]), ALU.mult))
                link(8, dve.tensor_tensor(c, c, gb[:, 1].unsqueeze(1).broadcast_to([P, 2, D]), ALU.add))
                dve.tensor_tensor(acc[:, 2 * b:2 * b + 2], acc[:, 2 * b:2 * b + 2], c, ALU.add).then_inc(sem["ln0_added"], 1)

            for ev in READERS:
                if ev[0] == "state":
                    state(ev[1])
                elif ev[0] in ("u", "z", "x", "mid", "dt"):
                    side_part(ev)
                elif ev[0] in "ASBCT":
                    norm_part(ev)
                elif ev[0] == "finish":
                    finish(ev)
                elif ev[0] == "end":
                    times_c(ALL - 1, 1)
                    gate_y(STEPS - 1)
                elif ev == ("gate", 0):
                    gate()
                elif ev[0] == "gate":
                    gate_copy(ev[1])
                elif ev[0] == "bias":
                    bias()
                elif ev[0] == "down":
                    pair(ev[1])
                elif ev[0] == "setup":
                    setup()
                elif ev[0] == "rates":
                    rates()

            def prepare(ev):
                kind, G = ev[0], ev[1]
                l, k, r = G // 4, G % 4, G % 2
                src = acc if l else xn
                rows = slice(GT * k, GT * k + GT)
                nq, nk = QH * HD, KH * HD
                q_r, k_r = qk[:, r, 0:QH], qk[:, r, QH:]
                cos, sin = rope[:, l, 0], rope[:, l, 1]
                if kind == "rms":
                    dve.wait_ge(sem["rms_sq"], G + 1)
                    dve.tensor_reduce(stat[:, 0, rows], sq[:, rows], AX.X, ALU.add).then_inc(sem["rms_sum"], 1)
                    dve.wait_ge(sem["rms_sum"], G + 1)
                    dve.tensor_scalar(stat[:, 2, rows], stat[:, 0, rows], 1.0 / D, RMS_EPS, ALU.mult, ALU.add) \
                        .then_inc(sem["rms_var"], 1)
                    dve.wait_ge(sem["rms_pow"], G + 1)
                    dve.tensor_tensor(xm[:, rows], src[:, rows], stat[:, 3, rows].unsqueeze(2).broadcast_to([P, GT, D]),
                                      ALU.mult).then_inc(sem["rms_done"], 1)
                elif kind == "Q":
                    dve.wait_ge(sem["prep_ready"], PREP[ev] + 1)
                    after(dve, "roped", G)
                    q_ps = ps[:, PREP_BANK]
                    dve.tensor_tensor(rot[:, 0, 0:nq].rearrange("p (b c) -> p b c", b=2), q_ps.rearrange("p (b c) -> p b c", b=2),
                                      cos.unsqueeze(1).broadcast_to([P, 2, 2 * D]), ALU.mult).then_inc(sem["rope_a"], 1)
                    dve.tensor_tensor(rot[:, 1, 0:nq].rearrange("p (b c two) -> p b c two", b=2, two=2),
                                      q_ps.rearrange("p (b c two) -> p b c two", b=2, two=2)[:, :, :, ::-1],
                                      sin.rearrange("p (c two) -> p c two", two=2).unsqueeze(1).broadcast_to([P, 2, D, 2]),
                                      ALU.mult).then_inc(sem["prep_free"], 1)
                elif kind == "K":
                    dve.wait_ge(sem["v_ready"], G + 1)
                    k_ps = ps[:, PREP_BANK, 0:2 * nk].rearrange("p (t c) -> p t c", t=GT)[:, :, 0:KV * HD]
                    dve.tensor_tensor(rot[:, 0, nq:].rearrange("p (t c) -> p t c", t=GT), k_ps,
                                      rope_k[:, l, 0].rearrange("p (t c) -> p t c", t=GT), ALU.mult).then_inc(sem["rope_a"], 1)
                    dve.tensor_tensor(rot[:, 1, nq:].rearrange("p (t c two) -> p t c two", t=GT, two=2),
                                      k_ps.rearrange("p t (c two) -> p t c two", two=2)[:, :, :, ::-1],
                                      rope_k[:, l, 1].rearrange("p (t c two) -> p t c two", t=GT, two=2),
                                      ALU.mult).then_inc(sem["prep_free"], 1)
                    dve.wait_ge(sem["rope_a"], 2 * G + 2)
                    dve.wait_ge(sem["prep_free"], PREP[ev] + 1)
                    dve.tensor_tensor(qk[:, r].rearrange("p h d -> p (h d)"), rot[:, 0], rot[:, 1], ALU.add) \
                        .then_inc(sem["roped"], 1)
                elif kind == "sqr":
                    dve.wait_ge(sem["qk_sq"], G + 1)
                    after(dve, "qk_var", G)
                    dve.tensor_reduce(norm[:, 0], qk_sqr[:].rearrange("p (h d) -> p h d", d=HD), AX.X, ALU.add) \
                        .then_inc(sem["qk_sum"], 1)
                    dve.wait_ge(sem["qk_sum"], G + 1)
                    after(dve, "qk_ln", G)
                    dve.tensor_scalar(norm[:, 1], norm[:, 0], 1.0 / HD, RMS_EPS, ALU.mult, ALU.add).then_inc(sem["qk_var"], 1)
                elif kind == "inv":
                    dve.wait_ge(sem["qk_inv"], G + 1)
                    dve.tensor_tensor(qk[:, r], qk[:, r], norm[:, 3].unsqueeze(2).broadcast_to([P, QH + KH, HD]), ALU.mult) \
                        .then_inc(sem["qk_normed"], 1)
                elif kind == "split":
                    dve.wait_ge(sem["qk_hi"], 2 * G + 2)
                    dve.tensor_tensor(qs[:, r, :, 2:4], q_r.unsqueeze(2).broadcast_to([P, QH, 2, HD]), qs[:, r, :, 0:2],
                                      ALU.subtract).then_inc(sem["qk_split"], 1)
                    dve.tensor_tensor(ks[:, r, :, 1::2], k_r.unsqueeze(2).broadcast_to([P, KH, 2, HD]), ks[:, r, :, 0::2],
                                      ALU.subtract).then_inc(sem["qk_split"], 1)
                elif kind == "O2":
                    dve.wait_ge(sem["prep_ready"], PREP[ev] + 1)
                    dve.tensor_tensor(acc[:, rows], src[:, rows], ps[:, PREP_BANK].rearrange("p (t d) -> p t d", d=D), ALU.add) \
                        .then_inc(sem["prep_free"], 1)
                    dve.wait_ge(sem["prep_free"], PREP[ev] + 1)
                    if l:
                        dve.tensor_tensor(x_sb[:, rows], x_sb[:, rows], acc[:, rows], ALU.add).then_inc(sem["out_ready"], 1)

            prepare(("rms", 0))

            step = [0]

            def link(ins):
                step[0] += 1
                ins.then_inc(sem["r_dve"], 1)
                dve.wait_ge(sem["r_dve"], step[0])

            def per_expert(t):
                return t.unsqueeze(2).broadcast_to([P, TILES, EXPERTS])

            dve.wait_ge(sem["r_pe"], 1)
            logits = ps[:, 4, 0:TILES * EXPERTS].rearrange("p (t e) -> p t e", e=EXPERTS)
            link(dve.tensor_reduce(rstat[:, 0], logits, AX.X, ALU.max))
            link(dve.tensor_tensor(route[:, 0], logits, per_expert(rstat[:, 0]), ALU.subtract))
            dve.wait_ge(sem["l1_weights_loaded"], 13 * 16)
            link(dve.tensor_scalar(route[:, 2], route[:, 0], 0.0, None, ALU.is_equal))
            link(dve.tensor_tensor(route[:, 3], route[:, 2], iotar[:].unsqueeze(1).broadcast_to([P, TILES, EXPERTS]),
                                   ALU.mult))
            link(dve.tensor_reduce(rstat[:, 1], route[:, 3], AX.X, ALU.max))
            link(dve.tensor_tensor(route[:, 4], route[:, 3], per_expert(rstat[:, 1]), ALU.is_equal))
            link(dve.tensor_copy(mask16[:], route[:, 4]))
            dve.wait_ge(sem["r_act"], 1)
            link(dve.tensor_reduce(rstat[:, 2], route[:, 1], AX.X, ALU.add))
            link(dve.reciprocal(rstat[:, 3], rstat[:, 2]))
            dve.wait_ge(sem["r_pe"], 2)
            pos = route[:, 5].rearrange("p t e -> p (t e)").rearrange("p (two b e) -> p two b e", two=2, e=EXPERTS)
            for two in range(2):
                link(dve.tensor_tensor(pos[:, two], ps[:, 5, 64 * two:64 * two + 64].rearrange("p (b e) -> p b e", e=EXPERTS),
                                       route[:, 4, two::2], ALU.mult))
            for two in range(2):
                link(dve.tensor_tensor(slot[:, two::2], pos[:, two].unsqueeze(3).broadcast_to([P, SEQS, EXPERTS, CAP]),
                                       iota32[:].unsqueeze(1).unsqueeze(1).broadcast_to([P, SEQS, EXPERTS, CAP]), ALU.is_equal))
            prepare(("Q", 0))
            for k in range(8):
                dve.wait_ge(sem["d_turn"], k + 1)
                dve.tensor_copy(slotT[:, k // 4, 4 * (k % 4):4 * (k % 4) + 4].rearrange("p t n -> p (t n)"),
                                ps[:, 4 + k % 4]).then_inc(sem["d_turned"], 1)
            def copy_turned(b, part):
                dve.wait_ge(sem["turn_q"], TURN["turn", b, part] + 1)
                if part == 0:
                    after(dve, "scores_ready", 6 * (b - 1))
                    ins = dve.tensor_copy(kT[:, b % 2], ps[:, TURN_BANK, 0:SEQ])
                else:
                    ins = dve.tensor_copy(qT[:, b % 2, :, (part - 1) * P:part * P],
                                          ps[:, TURN_BANK].rearrange("p (j n) -> p j n", n=P))
                ins.then_inc(sem["turn_copied"], 1)

            def fill(e):
                for ev in FILL_AT.get(e, ()):
                    if ev[0] == "turn":
                        copy_turned(ev[1], ev[2])
                    else:
                        prepare(ev)

            for e in range(EXPERTS):
                dve.wait_ge(sem["e_down"], e + 1)
                dve.tensor_copy(xe[:, :, e], ps[:, 4 + e % 2, 0:SEQ].rearrange("p (b c) -> p b c", c=CAP)).then_inc(sem["e_out"], 1)
                fill(e + 1)
            for k in range(4):
                dve.wait_ge(sem["e_comb"], k + 1)
                rows = slice(4 * k, 4 * k + 4)
                dve.tensor_tensor(sq[:, rows], ps[:, 4 + k % 2].rearrange("p (t d) -> p t d", d=D),
                                  rstat[:, 3, rows].unsqueeze(2).broadcast_to([P, 4, D]), ALU.mult) \
                    .then_inc(sem["e_added"], 1)
            dve.wait_ge(sem["e_added"], 4)
            dve.tensor_tensor(x_sb[:], x_sb[:], sq[:], ALU.add).then_inc(sem["x1_ready"], 1)

            def head_out(n):
                o = ps[:, BACK_BANK].rearrange("p (j g d) -> p g j d", j=GROUP, g=KV)
                dve.wait_ge(sem["turn_q"], TURN["back", n] + 1)
                if n >= 2:
                    dve.wait_ge(sem["turn_copied"], TURN["back", n - 2] + 1)
                dve.reciprocal(den[:, n % 2].rearrange("p (g j) -> p g j", g=KV), o[:, :, :, HD]) \
                    .then_inc(sem["den_done"], 1)
                dve.wait_ge(sem["den_done"], n + 1)
                dve.tensor_tensor(heads[:, n % TILES].rearrange("p (g j d) -> p g j d", g=KV, j=GROUP),
                                  o[:, :, :, 0:HD],
                                  den[:, n % 2].rearrange("p (g j) -> p g j", g=KV).unsqueeze(3)
                                  .broadcast_to([P, KV, GROUP, HD]), ALU.mult).then_inc(sem["turn_copied"], 1)

            for ev in AT_READERS:
                if ev[0] == "turn":
                    copy_turned(ev[1], ev[2])
                elif ev[0] == "back":
                    head_out(ev[1])
                elif ev[0] not in ("unit", "average", "copy"):
                    prepare(ev)

        @block.tensor
        def _(pe):
            def side_free(ev):
                after(pe, "side_free", SIDE[ev])

            pe.wait_ge(sem["consts_loaded"], 48)
            def norm_part(ev):
                _, use, k = ev
                pe.wait_ge(sem["ln_done"], STAGE["C"]["C", use, k] + 1)
                if use == 2:
                    pe.wait_ge(sem["b_copied"], ALL)
                    pe.wait_ge(sem["hc_ready"], HALVES * ALL)
                    pe.wait_ge(sem["gated"], HALVES * (STEPS - 1))
                if use == 1 and k:
                    pe.wait_ge(sem["ln_copied"], STAGE["T"]["T", 1, k - 1] + 1)
                bank = 6 if use == 1 else k
                for t in range(4):
                    last = pe.transpose(ps[:, bank, t * P:(t + 1) * P], (xm if use == 1 else xn)[:, 4 * k + t], ident[:])
                last.then_inc(sem["ln_turned"], 1)
                if use == 2 and k:
                    logits(k - 1)

            def logits(k):
                pe.wait_ge(sem["l1_weights_loaded"], 13 * 16)
                pe.wait_ge(sem["ln_copied"], STAGE["T"]["T", 2, k] + 1)
                for t in range(4 * k, 4 * k + 4):
                    last = pe.matmul(ps[:, 4, t * EXPERTS:(t + 1) * EXPERTS], xnT[:, t * P:(t + 1) * P], w_g[:],
                                     start=True, stop=True)
                return last

            def project(ev):
                kind, g, half = (*ev, 0)[:3]
                dr = g // PAIRS
                toks = slice((g % PAIRS) * COLS, (g % PAIRS + 1) * COLS)
                side_free(ev)
                if kind in "uz":
                    c = (kind == "z") * INNER + half * P
                    pe.wait_ge(sem["mamba_weights_loaded"], 64)
                    pe.wait_ge(sem["ln_copied"], STAGE["T"]["T", 1, g % PAIRS] + 1)
                    last = pe.matmul(side, w_in[:, dr, c:c + P], xmT[:, toks], start=True, stop=True)
                elif kind == "x":
                    pe.wait_ge(sem["u_ready"], g + 1)
                    for h2 in range(HALVES):
                        last = pe.matmul(ps[0:XROWS, SIDE_BANK], w_x[:, dr, h2], u_s[:, g % 2, h2],
                                         start=(h2 == 0), stop=(h2 == HALVES - 1))
                else:
                    pe.wait_ge(sem["dtr_ready"], g + 1)
                    last = pe.matmul(side, w_dt[DT_ROW:DT_ROW + RANK, dr, half * P:(half + 1) * P],
                                     dtr[DT_ROW:DT_ROW + RANK], start=True, stop=True)
                last.then_inc(sem["side_ready"], 1)

            def add_y(N):
                g = N // STATES
                if N % STATES == 0:
                    if N == 0:
                        pe.wait_ge(sem["e0_added"], PAIRS0)
                    after(pe, "gated", HALVES * (g - 1))
                    for half in range(HALVES):
                        pe.matmul(ps[:, Y_BANK + 2 * (g % 2) + half], diagD[:, g // PAIRS, half], u_s[:, g % 2, half],
                                  start=True, stop=True, skip_group_check=True)
                for half in range(HALVES):
                    pe.wait_ge(sem["hc_ready"], 2 * N + half + 1)
                    pe.matmul(ps[:, Y_BANK + 2 * (g % 2) + half], ident[:], hc[:, 2 * (N % DEEP) + half], start=False, stop=True,
                              skip_group_check=True).then_inc(sem["y_added"], 1)

            def spread_b(N):
                g, j = N // STATES, N % STATES
                if j == 0:
                    pe.wait_ge(sem["bc_ready"], g + 1)
                after(pe, "b_copied", N)
                pe.matmul(ps[:, B_BANK], spread_w[:, j:j + 1].broadcast_to([96, P]), bc[:, g % 2],
                          start=True, stop=True).then_inc(sem["b_spread"], 1)

            def spread(N):
                g, j = N // STATES, N % STATES
                if N == 0:
                    pe.wait_ge(sem["spread_ready"], 2)
                    pe.wait_ge(sem["diag_ready"], 4)
                    pe.wait_ge(sem["e0_gelu"], CHUNKS * PAIRS0)
                    for first in range(AHEAD):
                        spread_b(first)
                if N + AHEAD < ALL:
                    spread_b(N + AHEAD)
                after(pe, "hc_ready", 2 * (N - C_BANKS) + 2)
                pe.matmul(ps[:, C_BANK + N % C_BANKS], spread_w[:, STATES + j:STATES + j + 1].broadcast_to([96, P]),
                          bc[:, g % 2], start=True, stop=True).then_inc(sem["c_spread"], 1)

            def finish(ev):
                g = ev[1]
                side_free(ev)
                pe.wait_ge(sem["gated"], HALVES * (g + 1))
                for t in range(4):
                    for half in range(HALVES):
                        last = pe.matmul(side[:, t * D:(t + 1) * D], yg[:, half, t * P:(t + 1) * P],
                                         w_out[:, g // PAIRS, half], start=(half == 0), stop=(half == HALVES - 1))
                last.then_inc(sem["side_ready"], 1)

            def gate(ev):
                side_free(ev)
                if ev[1] == 0:
                    pe.wait_ge(sem["pool_mean"], 4)
                    pe.wait_ge(sem["gate_weights_loaded"], 96)
                    last = pe.matmul(side[0:SEQS, 0:EXPERTS], pooled[:], w_r[:], start=True, stop=True)
                elif ev[1] == 1:
                    pe.wait_ge(sem["gate_step"], 14)
                    last = pe.transpose(side[0:EXPERTS, 0:SEQS], small[:, 14], ident[0:SEQS, 0:SEQS])
                else:
                    pe.wait_ge(sem["halfconst"], 2)
                    last = pe.matmul(side[:, 0:2 * SEQS], ones8[:], wdiag[:].rearrange("p b k -> p (b k)"),
                                     start=True, stop=True)
                last.then_inc(sem["side_ready"], 1)

            def up(p):
                r, k = p % RING, p % 2
                x = xnT[:, p // 2 * SEQ:(p // 2 + 1) * SEQ]
                pe.wait_ge(sem[f"expert_loaded{r}"], 16 * (p // RING + 1))
                after(pe, "e0_gelu", CHUNKS * (p - 1))
                for c in range(CHUNKS):
                    last = pe.matmul(ps[:, 2 * k + c // 2, (c % 2) * SEQ:(c % 2 + 1) * SEQ],
                                     wbuf[:, r, c * P:(c + 1) * P], x, start=True, stop=True)
                    if c % 2:
                        last.then_inc(sem["e0_up"], 1)

            def down(p):
                r, k = p % RING, p % 2
                bank = ps[:, 4 + k]
                after(pe, "e0_added", p - 1)
                if p == 0:
                    pe.wait_ge(sem["moe_bias"], 2)
                for t in range(2):
                    for c in range(CHUNKS):
                        if t == 0:
                            pe.wait_ge(sem["e0_gelu"], CHUNKS * p + c + 1)
                        last = pe.matmul(bank[:, t * D:(t + 1) * D], hT[:, k, c, t * P:(t + 1) * P],
                                         wbuf[:, r, HIDDEN + CHUNKS + c * D:HIDDEN + CHUNKS + (c + 1) * D],
                                         start=(c == 0), stop=(c == CHUNKS - 1))
                last.then_inc(sem["e0_down"], 1)

            def bias():
                pe.wait_ge(sem["side_free"], SIDE["gate", 2] + 1)
                for b in range(SEQS):
                    last = pe.matmul(ps[:, 4 + b // 4, (b % 4) * D:(b % 4 + 1) * D], cwT[:, b:b + 1].broadcast_to([EXPERTS, P]),
                                     b2[:], start=True, stop=True)
                last.then_inc(sem["bias_ready"], 1)

            for ev in ORDER:
                if ev[0] == "spread":
                    spread(ev[1])
                elif ev[0] == "state":
                    if ev[1] >= DEEP:
                        add_y(ev[1] - DEEP)
                elif ev[0] in ("u", "z", "x", "dt"):
                    project(ev)
                elif ev[0] == "finish":
                    finish(ev)
                elif ev[0] == "end":
                    for N in range(ALL - DEEP, ALL):
                        add_y(N)
                elif ev[0] == "T":
                    norm_part(ev)
                elif ev[0] == "gate":
                    gate(ev)
                elif ev[0] == "bias":
                    bias()
                elif ev[0] == "up":
                    up(ev[1])
                elif ev[0] == "down":
                    down(ev[1])

            def prepare(ev):
                kind, G = ev
                l, k = G // 4, G % 4
                bank = ps[:, PREP_BANK]
                after(pe, "prep_free", PREP[ev])
                if kind == "T":
                    pe.wait_ge(sem["rms_done"], G + 1)
                elif kind == "O1":
                    pe.wait_ge(sem["turn_copied"], TURN["back", GT * (G + 1) - 1] + 1)
                if kind == "L":
                    last = pe.matmul(ps[0:LAT, PREP_BANK], w_kvd[:], xmT[:, k * GT * P:(k + 1) * GT * P], start=True, stop=True)
                else:
                    for t in range(GT):
                        tile = slice((GT * k + t) * P, (GT * k + t + 1) * P)
                        if kind in ("T", "O1"):
                            last = pe.transpose(bank[:, t * P:(t + 1) * P], (xm if kind == "T" else heads)[:, GT * k + t], ident[:])
                        elif kind == "K":
                            c = 2 * KV * HD
                            rows, w = (xmT, w_kv) if l else (latT, w_kvu)
                            last = pe.matmul(bank[:, t * c:(t + 1) * c], rows[:, tile], w[:], start=True, stop=True)
                        else:
                            last = pe.matmul(bank[:, t * D:(t + 1) * D], xmT[:, tile], (w_q if kind == "Q" else w_o)[:, l],
                                             start=True, stop=True)
                last.then_inc(sem["prep_ready"], 1)


            logits(TILES // 4 - 1).then_inc(sem["r_pe"], 1)
            prepare(("T", 0))
            prepare(("L", 0))
            pe.wait_ge(sem["r_dve"], 7)
            pe.matmul(ps[:, 5, 0:64], tri[:, 0], mask16[:, 0::2], start=True, stop=True)
            pe.matmul(ps[:, 5, 64:128], tri[:, 1], mask16[:, 0::2], start=True, stop=False)
            pe.matmul(ps[:, 5, 64:128], tri[:, 0], mask16[:, 1::2], start=False, stop=True).then_inc(sem["r_pe"], 1)
            prepare(("Q", 0))
            pe.wait_ge(sem["r_dve"], 13)
            for k in range(4):
                for b in (2 * k, 2 * k + 1):
                    for two in range(2):
                        last = pe.matmul(ps[:, k, (b % 2) * SEQ:(b % 2 + 1) * SEQ], xn[:, 2 * b + two],
                                         slot[:, 2 * b + two].rearrange("p e c -> p (e c)"), start=(two == 0), stop=(two == 1))
                last.then_inc(sem["slots_spread"], 1)
            for k in range(8):
                after(pe, "d_turned", k - 3)
                if 4 + k == PREP_BANK:
                    pe.wait_ge(sem["prep_free"], PREP["Q", 0] + 1)
                for t in range(4):
                    last = pe.transpose(ps[:, 4 + k % 4, t * P:(t + 1) * P],
                                        slot[:, 4 * (k % 4) + t, 4 * (k // 4):4 * (k // 4) + 4].rearrange("p e c -> p (e c)"),
                                        ident[:])
                last.then_inc(sem["d_turn"], 1)

            def turn(b, part):
                G, r = b // 2, b // 2 % 2
                first = 2 * (b % 2)
                pe.wait_ge(sem["qk_split"], 2 * G + 2)
                after(pe, "turn_copied", TURN["turn", b, part])
                if part == 0:
                    for t in range(2):
                        last = pe.matmul(ps[:, TURN_BANK, t * P:(t + 1) * P],
                                         ks[:, r, (first + t) * KV:(first + t + 1) * KV].rearrange("p g i d -> p (g i d)"),
                                         ident16[:], start=True, stop=True)
                else:
                    for j in range(GROUP):
                        h0 = (first + part - 1) * HEADS + j * KV
                        last = pe.matmul(ps[:, TURN_BANK, j * P:(j + 1) * P],
                                         qs[:, r, h0:h0 + KV].rearrange("p g i d -> p (g i d)"),
                                         ident16[:], start=True, stop=True)
                last.then_inc(sem["turn_q"], 1)

            def up(e):
                pe.wait_ge(sem[f"expert_loaded{e % RING}"], 16 * (PAIRS0 // RING + e // RING + 1))
                after(pe, "e_gelu", CHUNKS * (e - 1))
                for c in range(CHUNKS):
                    last = pe.matmul(ps[:, 2 * (e % 2) + c // 2, (c % 2) * SEQ:(c % 2 + 1) * SEQ],
                                     wbuf1[:, e % RING, c * P:(c + 1) * P], xe[:, :, e],
                                     start=True, stop=True)
                    if c % 2:
                        last.then_inc(sem["e_up"], 1)

            def down(e):
                pe.wait_ge(sem["e_gelu"], CHUNKS * (e + 1))
                after(pe, "e_out", e - 1)
                for c in range(CHUNKS):
                    last = pe.matmul(ps[:, 4 + e % 2, 0:SEQ], wbuf1[:, e % RING, HIDDEN + c * D:HIDDEN + (c + 1) * D],
                                     hT1[:, e % 2, c], start=(c == 0), stop=(c == CHUNKS - 1))
                last.then_inc(sem["e_down"], 1)

            pe.wait_ge(sem["slots_copied"], 4)
            pe.wait_ge(sem["d_turned"], 8)
            up(0)
            for e in range(1, EXPERTS):
                up(e)
                down(e - 1)
                for ev in FILL_AT[e]:
                    if ev[0] == "turn":
                        turn(ev[1], ev[2])
                    elif ev in PREP:
                        prepare(ev)
            down(EXPERTS - 1)
            pe.wait_ge(sem["e_out"], EXPERTS)
            for k in range(4):
                for n, (b, s) in enumerate(((2 * k, 0), (2 * k, 1), (2 * k + 1, 0), (2 * k + 1, 1))):
                    last = pe.transpose(ps[:, k, n * P:(n + 1) * P], xe[:, b, 4 * s:4 * s + 4].rearrange("p e c -> p (e c)"), ident[:])
                last.then_inc(sem["e_turn"], 1)
            for k in range(4):
                pe.wait_ge(sem["e_turned"], k + 1)
                after(pe, "e_added", k - 1)
                for t in range(4):
                    for s in range(2):
                        last = pe.matmul(ps[:, 4 + k % 2, t * D:(t + 1) * D], slotT[:, s, 4 * k + t], eo[:, 2 * k + t // 2, s],
                                         start=(s == 0), stop=(s == 1))
                last.then_inc(sem["e_comb"], 1)

            def scores(U):
                b, t = U // 6, U // 2
                kt, qt = BLOCKS[t % 3]
                l, r = b // SEQS, b % 2
                kvs = (2 * (U % 2), 2 * (U % 2) + 1)
                corner = l and kt != qt
                if t % 3 < 2:
                    pe.wait_ge(sem["turn_copied"], TURN["turn", b, 1 + t % 3] + 1)
                after(pe, "probs_ready", U - 1)
                near = slice(P - WINDOW, P)
                for kv in kvs:
                    if corner:
                        pe.matmul(ps[near, kv, 0:GROUP * WINDOW], ident16[:, near],
                                  masks[:, 2, 0:WINDOW].unsqueeze(1).broadcast_to([P, GROUP, WINDOW]), start=True, stop=False)
                    elif kt == qt:
                        pe.matmul(ps[:, kv], ident16[:], masks[:, l].unsqueeze(1).broadcast_to([P, GROUP, P]),
                                  start=True, stop=False)
                for kv in kvs:
                    g = slice(32 * kv, 32 * kv + 32)
                    if corner:
                        last = pe.matmul(ps[near, kv, 0:GROUP * WINDOW], kT[g, r, near], qT[g, r, :, P:P + WINDOW],
                                         start=False, stop=True)
                    else:
                        last = pe.matmul(ps[:, kv], kT[g, r, kt * P:(kt + 1) * P], qT[g, r, :, qt * P:(qt + 1) * P],
                                         start=(kt != qt), stop=True)
                last.then_inc(sem["scores_ready"], 1)

            def average(t):
                b = t // 3
                kt, qt = BLOCKS[t % 3]
                pe.wait_ge(sem["probs_ready"], 2 * t + 2)
                if t % 3 == 0:
                    pe.wait_ge(sem["v_ready"], b // 2 + 1)
                if t % 3 < 2:
                    after(pe, "av_copied", 2 * (b - 1) + qt + 1)
                near = slice(P - WINDOW, P)
                for kv in range(KV):
                    g = slice(32 * kv, 32 * kv + 32)
                    v = v_ring[:, b // 2 % 2, 2 * (b % 2) + kt, kv]
                    if b >= SEQS and kt != qt:
                        last = pe.matmul(ps[g, AV_BANK + 1].rearrange("p (j q) -> p j q", j=GROUP)[:, :, 0:WINDOW],
                                         v[near], probs[near, t % 3, kv, 0:GROUP * WINDOW], start=False, stop=True)
                    else:
                        last = pe.matmul(ps[g, AV_BANK + qt], v, probs[:, t % 3, kv], start=(t % 3 < 2), stop=(t % 3 != 1))
                last.then_inc(sem["av_done"], 1)

            def turn_back(n):
                pe.wait_ge(sem["av_copied"], n + 1)
                after(pe, "turn_copied", TURN["back", n])
                for j in range(GROUP):
                    last = pe.transpose(ps[:, BACK_BANK, j * P:(j + 1) * P], avT[:, n % 2, j * P:(j + 1) * P], ident[:])
                last.then_inc(sem["turn_q"], 1)

            for ev in AT_ORDER:
                if ev[0] == "unit":
                    scores(ev[1])
                elif ev[0] == "average":
                    average(ev[1])
                elif ev[0] == "turn":
                    turn(ev[1], ev[2])
                elif ev[0] == "back":
                    turn_back(ev[1])
                elif ev in PREP:
                    prepare(ev)


def layouts(v):
    import numpy as np

    def mamba(p):
        w = {k: np.asarray(v[f"L0_attn_{p}_{k}"]) for k in ("Win", "convw", "convb", "Wx", "Wdt", "bdt", "Alog", "D", "Wout")}
        per = np.concatenate([w["convw"][:, 0], w["convb"][:, None], w["bdt"][:, None], w["D"][:, None], w["Alog"]], 1)
        bc = w["Wx"][RANK:].T
        return {
            "par": per.reshape(HALVES, P, NPAR).transpose(1, 0, 2),
            "w_in": w["Win"].T,
            "w_x": np.concatenate([bc, bc, bc, w["Wx"][:RANK].T], 1).reshape(HALVES, P, XROWS).transpose(1, 0, 2),
            "w_dt": w["Wdt"].T,
            "w_out": w["Wout"].T.reshape(HALVES, P, D).transpose(1, 0, 2),
        }

    f, b = mamba("f"), mamba("b")
    a = {k: np.stack([f[k], b[k]], 1) for k in f}
    v = {k: np.asarray(x) for k, x in v.items()}
    a["x"] = v["L0_attn_x"].reshape(TOK, D)
    a["ident"] = np.eye(P, dtype=np.float32)
    a["cols"] = np.stack([v["L0_attn_norm_g"], v["L0_attn_norm_b"], v["L1_attn_norm1_w"], v["L1_attn_norm2_w"]], 1)
    a["w_r"] = v["L0_ffn_Wr"]
    a["br"] = v["L0_ffn_br"]
    a["b2"] = v["L0_ffn_b2"]
    a["iota8"] = np.arange(EXPERTS, dtype=np.float32)
    a["gamma"], a["beta"] = v["L0_ffn_gamma"], v["L0_ffn_beta"]
    down = lambda w: w.reshape(EXPERTS, CHUNKS, P, D).transpose(0, 2, 1, 3).reshape(EXPERTS, P, HIDDEN)
    b1 = v["L0_ffn_b1"].reshape(EXPERTS, CHUNKS, P).transpose(0, 2, 1)
    a["pack0"] = np.concatenate([v["L0_ffn_W1"], b1, down(v["L0_ffn_W2"])], 2)
    a["pack1"] = np.concatenate([v["L1_ffn_W1"], down(v["L1_ffn_W2"])], 2)
    a["w_g"] = v["L1_ffn_Wg"]
    a["w_q"] = np.stack([v["L1_attn_g_wq"], v["L1_attn_l_wq"]], 1).reshape(P, 2, KV, GROUP, HD).swapaxes(2, 3).reshape(P, 2, D)
    a["w_o"] = np.stack([v["L1_attn_g_wo"], v["L1_attn_l_wo"]], 1)
    a["w_kvd"] = v["L1_attn_g_kv_down"]
    a["w_kvu"] = np.concatenate([v["L1_attn_g_k_up"], v["L1_attn_g_v_up"]], 1)
    a["w_kv"] = np.concatenate([v["L1_attn_l_wk"], v["L1_attn_l_wv"]], 1)
    a.update(constants())
    return a


def constants():
    import numpy as np

    key, query = np.arange(P)[:, None], np.arange(P)[None, :]
    hide = lambda seen: np.where(seen, 0.0, MASKED)
    masks = [hide(query >= key), hide((query >= key) & (query - key < WINDOW)), hide(query + P - key < WINDOW)]
    ropes = []
    for base in (1000000.0, 10000.0):
        inv = (1.0 / np.float32(base) ** (np.arange(0, HD, 2, dtype=np.float32) / np.float32(HD))).astype(np.float32)
        angle = np.arange(SEQ, dtype=np.float32)[:, None] * inv[None, :]
        cos = np.repeat(np.cos(angle), 2, 1)
        sin = np.stack([-np.sin(angle), np.sin(angle)], 2).reshape(SEQ, HD)
        ropes.append([np.tile(t, (1, HEADS)).reshape(2, P, D).transpose(1, 0, 2).reshape(P, 2 * D) for t in (cos, sin)])
    rope = np.array(ropes).transpose(2, 0, 1, 3).astype(np.float32)
    k_part = rope.reshape(P, 2, 2, 2, D)[..., :KV * HD]
    tri = np.stack([key <= query, np.ones((P, P))], 1)
    return {
        "masks": np.stack(masks, 1).astype(np.float16),
        "ident16": np.eye(P, dtype=np.float16),
        "rope": rope,
        "rope_k": np.concatenate([k_part, k_part], 3).reshape(P, 2, 2, GT * KV * HD),
        "tri": tri.astype(np.float16),
        "iota32": np.arange(1, CAP + 1, dtype=np.float32),
        "iotar": np.arange(EXPERTS, 0, -1, dtype=np.float32),
    }


def kernel(**inputs):
    import numpy as _np
    import concourse.bacc as _bacc
    from concourse import mybir as _mybir
    from concourse.bass_utils import run_bass_kernel_spmd as _run

    nc = _bacc.Bacc("TRN2", target_bir_lowering=False, num_devices=1)
    arrays, args = {}, {}
    for name, a in layouts(inputs).items():
        a = _np.ascontiguousarray(a)
        arrays[f"in_{name}"] = a
        args[name] = nc.dram_tensor(f"in_{name}", a.shape, _mybir.dt.from_np(a.dtype), kind="ExternalInput").ap()
    out = nc.dram_tensor("out", (TOK, D), F32, kind="ExternalOutput").ap()
    build(nc, args, out)
    r = _run(nc, [arrays], core_ids=[0])
    return r.results[0]["out"].reshape(SEQS, SEQ, D)
```
